# Optimizing a Trainium2 kernel written in Bass

```python
import numpy as np
import jax
import jax.numpy as jnp

def _softmax(x, axis=-1):
    return jax.nn.softmax(x, axis=axis)

def _gelu(x):
    return jax.nn.gelu(x, approximate=True)

def _silu(x):
    return jax.nn.silu(x)

def _sigmoid(x):
    return jax.nn.sigmoid(x)

def _layernorm(x, axis=-1, eps=1e-05):
    m = jnp.mean(x, axis=axis, keepdims=True)
    v = jnp.var(x, axis=axis, keepdims=True)
    return (x - m) / jnp.sqrt(v + eps)

def _scatter_add(tgt, idx, src, axis=0):
    return tgt.at[idx].add(src)

def _segment_sum(src, seg, n):
    return jax.ops.segment_sum(src, seg, n)
kernel_name = 'mk_conv_attn_hybrid_d2_conv_nchw128_r2_0b04b8'

def setup_inputs(seed: int=0):
    np.random.seed(seed)
    _w = jnp.asarray

    def _rec_inputs():
        import jax
        import jax.numpy as jnp
        _gk = jax.random.key(seed)
        x = -0.0002928 + 1 * jax.random.normal(jax.random.fold_in(_gk, 1), (8, 64, 32, 32), jnp.float32)
        return x
    x = _rec_inputs()

    def _L0_conv_setup():
        import jax, jax.numpy as jnp
        import numpy as np
        D_MODEL = 64
        D_STATE = 16
        D_CONV = 2
        EXPAND = 2
        D_INNER = EXPAND * D_MODEL
        DT_RANK = (D_MODEL + 15) // 16
        GROUPS = 4
        EPS = 1e-05

        def _causal_conv_k2(x, w, b):
            xp = jnp.pad(x, ((0, 0), (1, 0), (0, 0)))
            return xp[:, :-1] * w[:, 0] + xp[:, 1:] * w[:, 1] + b

        def _selective_scan(xc, dt, Bmat, Cmat, A, D):

            def step(h, inp):
                dt_t, B_t, C_t, x_t = inp
                dA = jnp.exp(dt_t[..., None] * A)
                dBx = dt_t[..., None] * B_t[:, None, :] * x_t[..., None]
                h = dA * h + dBx
                y = jnp.einsum('bdn,bn->bd', h, C_t)
                return (h, y)
            B_, L, Din = xc.shape
            h0 = jnp.zeros((B_, Din, A.shape[1]), dtype=xc.dtype)
            xs = (jnp.swapaxes(dt, 0, 1), jnp.swapaxes(Bmat, 0, 1), jnp.swapaxes(Cmat, 0, 1), jnp.swapaxes(xc, 0, 1))
            _, ys = jax.lax.scan(step, h0, xs)
            return jnp.swapaxes(ys, 0, 1) + xc * D

        def _mamba(x, W_in, conv_w, conv_b, W_x, W_dt, b_dt, A_log, D, W_out):
            xz = x @ W_in
            xh, z = jnp.split(xz, 2, axis=-1)
            xh = jax.nn.silu(_causal_conv_k2(xh, conv_w, conv_b))
            x_dbl = xh @ W_x
            dt_low = x_dbl[..., :DT_RANK]
            Bmat = x_dbl[..., DT_RANK:DT_RANK + D_STATE]
            Cmat = x_dbl[..., DT_RANK + D_STATE:]
            dt = jax.nn.softplus(dt_low @ W_dt + b_dt)
            A = -jnp.exp(A_log)
            y = _selective_scan(xh, dt, Bmat, Cmat, A, D)
            y = y * jax.nn.silu(z)
            return y @ W_out

        def _group_norm(x, gamma, beta):
            B_, C, H, W = x.shape
            xr = x.reshape(B_, GROUPS, -1)
            mean = xr.mean(-1, keepdims=True)
            var = xr.var(-1, keepdims=True)
            xn = ((xr - mean) * jax.lax.rsqrt(var + EPS)).reshape(B_, C, H, W)
            return xn * gamma[:, None, None] + beta[:, None, None]
        key = jax.random.key(seed)
        ks = jax.random.split(key, 12)
        s = lambda k, shape, sc=0.02: jax.random.normal(k, shape, dtype=jnp.float32) * sc
        inp = {'x_hsi': jax.random.normal(ks[0], (8, D_MODEL, 32, 32), dtype=jnp.float32), 'W_in': s(ks[1], (D_MODEL, 2 * D_INNER)), 'conv_w': s(ks[2], (D_INNER, D_CONV), 0.5), 'conv_b': s(ks[3], (D_INNER,), 0.1), 'W_x': s(ks[4], (D_INNER, DT_RANK + 2 * D_STATE)), 'W_dt': s(ks[5], (DT_RANK, D_INNER), 0.1), 'b_dt': s(ks[6], (D_INNER,), 0.1), 'A_log': jnp.log(jnp.broadcast_to(jnp.arange(1, D_STATE + 1, dtype=jnp.float32), (D_INNER, D_STATE))), 'D': jnp.ones((D_INNER,), dtype=jnp.float32), 'W_out': s(ks[7], (D_INNER, D_MODEL)), 'gn_gamma': jnp.ones((D_MODEL,), dtype=jnp.float32), 'gn_beta': jnp.zeros((D_MODEL,), dtype=jnp.float32)}
        return inp
    _L0_conv_all = _L0_conv_setup()
    _L0_conv_in = {k: v for k, v in _L0_conv_all.items() if k in ('W_in', 'conv_w', 'conv_b', 'W_x', 'W_dt', 'b_dt', 'A_log', 'D', 'W_out', 'gn_gamma', 'gn_beta')}
    del _L0_conv_all

    def _L1_attn_setup():
        import jax, jax.numpy as jnp
        import numpy as np
        B, T, C = (2048, 32, 64)
        N_HEAD = 8
        D_HEAD = C // N_HEAD
        key = jax.random.key(seed)
        k1, k2, k3 = jax.random.split(key, 3)
        x = jax.random.normal(k1, (B, T, C), dtype=jnp.float32)
        w_attn = jax.random.normal(k2, (C, 3 * C), dtype=jnp.float32) * 0.02
        w_proj = jax.random.normal(k3, (C, C), dtype=jnp.float32) * 0.02
        return {'x': x, 'w_attn': w_attn, 'w_proj': w_proj}
    _L1_attn_all = _L1_attn_setup()
    _L1_attn_in = {k: v for k, v in _L1_attn_all.items() if k in ('w_attn', 'w_proj')}
    del _L1_attn_all

    def _L1_ffn_setup():
        import jax, jax.numpy as jnp
        import numpy as np
        B, N, D, C, E, K = (8, 4096, 64, 64, 8, 2)
        key = jax.random.key(seed)
        k0, k1, k2 = jax.random.split(key, 3)
        x = jax.random.normal(k0, (B, N, D), dtype=jnp.float32)
        router_w = jax.random.normal(k1, (D, E), dtype=jnp.float32) * 0.05
        router_b = jnp.zeros((E,), dtype=jnp.float32)
        expert_w = jax.random.normal(k2, (E, D, C), dtype=jnp.float32) * (1.0 / np.sqrt(D))
        expert_b = jnp.zeros((E, C), dtype=jnp.float32)
        return {'x': x, 'router_w': router_w, 'router_b': router_b, 'expert_w': expert_w, 'expert_b': expert_b}
    _L1_ffn_all = _L1_ffn_setup()
    _L1_ffn_in = {k: v for k, v in _L1_ffn_all.items() if k in ('router_w', 'router_b', 'expert_w', 'expert_b')}
    del _L1_ffn_all
    return {'x': x, 'L0_conv_W_in': _L0_conv_in['W_in'], 'L0_conv_conv_w': _L0_conv_in['conv_w'], 'L0_conv_conv_b': _L0_conv_in['conv_b'], 'L0_conv_W_x': _L0_conv_in['W_x'], 'L0_conv_W_dt': _L0_conv_in['W_dt'], 'L0_conv_b_dt': _L0_conv_in['b_dt'], 'L0_conv_A_log': _L0_conv_in['A_log'], 'L0_conv_D': _L0_conv_in['D'], 'L0_conv_W_out': _L0_conv_in['W_out'], 'L0_conv_gn_gamma': _L0_conv_in['gn_gamma'], 'L0_conv_gn_beta': _L0_conv_in['gn_beta'], 'L1_attn_w_attn': _L1_attn_in['w_attn'], 'L1_attn_w_proj': _L1_attn_in['w_proj'], 'L1_ffn_router_w': _L1_ffn_in['router_w'], 'L1_ffn_router_b': _L1_ffn_in['router_b'], 'L1_ffn_expert_w': _L1_ffn_in['expert_w'], 'L1_ffn_expert_b': _L1_ffn_in['expert_b']}

def reference(x, L0_conv_W_in, L0_conv_conv_w, L0_conv_conv_b, L0_conv_W_x, L0_conv_W_dt, L0_conv_b_dt, L0_conv_A_log, L0_conv_D, L0_conv_W_out, L0_conv_gn_gamma, L0_conv_gn_beta, L1_attn_w_attn, L1_attn_w_proj, L1_ffn_router_w, L1_ffn_router_b, L1_ffn_expert_w, L1_ffn_expert_b):
    import jax
    import jax.numpy as jnp

    def _L0_conv_ref(x_hsi, W_in, conv_w, conv_b, W_x, W_dt, b_dt, A_log, D, W_out, gn_gamma, gn_beta):
        import jax, jax.numpy as jnp
        import numpy as np
        D_MODEL = 64
        D_STATE = 16
        D_CONV = 2
        EXPAND = 2
        D_INNER = EXPAND * D_MODEL
        DT_RANK = (D_MODEL + 15) // 16
        GROUPS = 4
        EPS = 1e-05

        def _causal_conv_k2(x, w, b):
            xp = jnp.pad(x, ((0, 0), (1, 0), (0, 0)))
            return xp[:, :-1] * w[:, 0] + xp[:, 1:] * w[:, 1] + b

        def _selective_scan(xc, dt, Bmat, Cmat, A, D):

            def step(h, inp):
                dt_t, B_t, C_t, x_t = inp
                dA = jnp.exp(dt_t[..., None] * A)
                dBx = dt_t[..., None] * B_t[:, None, :] * x_t[..., None]
                h = dA * h + dBx
                y = jnp.einsum('bdn,bn->bd', h, C_t)
                return (h, y)
            B_, L, Din = xc.shape
            h0 = jnp.zeros((B_, Din, A.shape[1]), dtype=xc.dtype)
            xs = (jnp.swapaxes(dt, 0, 1), jnp.swapaxes(Bmat, 0, 1), jnp.swapaxes(Cmat, 0, 1), jnp.swapaxes(xc, 0, 1))
            _, ys = jax.lax.scan(step, h0, xs)
            return jnp.swapaxes(ys, 0, 1) + xc * D

        def _mamba(x, W_in, conv_w, conv_b, W_x, W_dt, b_dt, A_log, D, W_out):
            xz = x @ W_in
            xh, z = jnp.split(xz, 2, axis=-1)
            xh = jax.nn.silu(_causal_conv_k2(xh, conv_w, conv_b))
            x_dbl = xh @ W_x
            dt_low = x_dbl[..., :DT_RANK]
            Bmat = x_dbl[..., DT_RANK:DT_RANK + D_STATE]
            Cmat = x_dbl[..., DT_RANK + D_STATE:]
            dt = jax.nn.softplus(dt_low @ W_dt + b_dt)
            A = -jnp.exp(A_log)
            y = _selective_scan(xh, dt, Bmat, Cmat, A, D)
            y = y * jax.nn.silu(z)
            return y @ W_out

        def _group_norm(x, gamma, beta):
            B_, C, H, W = x.shape
            xr = x.reshape(B_, GROUPS, -1)
            mean = xr.mean(-1, keepdims=True)
            var = xr.var(-1, keepdims=True)
            xn = ((xr - mean) * jax.lax.rsqrt(var + EPS)).reshape(B_, C, H, W)
            return xn * gamma[:, None, None] + beta[:, None, None]
        B_, C, H, W = x_hsi.shape
        x = jnp.transpose(x_hsi, (0, 2, 3, 1)).reshape(B_, H * W, C)
        x = _mamba(x, W_in, conv_w, conv_b, W_x, W_dt, b_dt, A_log, D, W_out)
        x = jnp.transpose(x.reshape(B_, H, W, C), (0, 3, 1, 2))
        x = jax.nn.silu(_group_norm(x, gn_gamma, gn_beta))
        return x + x_hsi

    def _L1_attn_ref(x, w_attn, w_proj):
        import jax, jax.numpy as jnp
        import numpy as np
        B, T, C = (2048, 32, 64)
        N_HEAD = 8
        D_HEAD = C // N_HEAD
        Bt, Tt, Ct = x.shape
        qkv = x @ w_attn
        q, k, v = jnp.split(qkv, 3, axis=-1)
        q = q.reshape(Bt, Tt, N_HEAD, D_HEAD)
        k = k.reshape(Bt, Tt, N_HEAD, D_HEAD)
        v = v.reshape(Bt, Tt, N_HEAD, D_HEAD)
        scale = 1.0 / jnp.sqrt(jnp.float32(D_HEAD))
        att = jnp.einsum('bqhd,bkhd->bhqk', q, k) * scale
        causal = jnp.tril(jnp.ones((Tt, Tt), dtype=bool))
        att = jnp.where(causal[None, None, :, :], att, -jnp.inf)
        att = jax.nn.softmax(att, axis=-1)
        out = jnp.einsum('bhqk,bkhd->bqhd', att, v).reshape(Bt, Tt, Ct)
        return out @ w_proj

    def _L1_ffn_ref(x, router_w, router_b, expert_w, expert_b):
        import jax, jax.numpy as jnp
        import numpy as np
        B, N, D, C, E, K = (8, 4096, 64, 64, 8, 2)
        router_probs = jax.nn.softmax(x @ router_w + router_b, axis=-1)
        top_p, top_i = jax.lax.top_k(router_probs, K)
        top_p = top_p / jnp.sum(top_p, axis=-1, keepdims=True)
        expert_out = jnp.einsum('bnd,edc->bnec', x, expert_w) + expert_b
        gathered = jnp.take_along_axis(expert_out, top_i[..., None], axis=2)
        return jnp.einsum('bnk,bnkc->bnc', top_p, gathered)

    def _gn(v, G=32, eps=1e-05):
        B_, C_, H_, W_ = v.shape
        g = v.reshape(B_, G, C_ // G, H_, W_)
        m = jnp.mean(g, axis=(2, 3, 4), keepdims=True)
        s = jnp.var(g, axis=(2, 3, 4), keepdims=True)
        return ((g - m) / jnp.sqrt(s + eps)).reshape(v.shape)

    def _ln_c(v, eps=1e-06):
        m = jnp.mean(v, axis=1, keepdims=True)
        s = jnp.var(v, axis=1, keepdims=True)
        return (v - m) / jnp.sqrt(s + eps)

    def _ln_t(v, eps=1e-05):
        m = jnp.mean(v, axis=-1, keepdims=True)
        s = jnp.var(v, axis=-1, keepdims=True)
        return (v - m) / jnp.sqrt(s + eps)

    def _to_tokens(v):
        B_, C_, H_, W_ = v.shape
        return v.reshape(B_, C_, H_ * W_).transpose(0, 2, 1)

    def _from_tokens(t, like):
        B_, C_, H_, W_ = like.shape
        return t.transpose(0, 2, 1).reshape(B_, C_, H_, W_)
    x = _L0_conv_ref(x, L0_conv_W_in, L0_conv_conv_w, L0_conv_conv_b, L0_conv_W_x, L0_conv_W_dt, L0_conv_b_dt, L0_conv_A_log, L0_conv_D, L0_conv_W_out, L0_conv_gn_gamma, L0_conv_gn_beta)
    t = _to_tokens(x)
    t = t + _L1_attn_ref(_ln_t(t), L1_attn_w_attn, L1_attn_w_proj)
    t = t + _L1_ffn_ref(_ln_t(t), L1_ffn_router_w, L1_ffn_router_b, L1_ffn_expert_w, L1_ffn_expert_b)
    x = _from_tokens(t, x)
    return x

_drawn_inputs = setup_inputs


def setup_inputs(seed=0):
    import zlib

    import numpy as np

    out = dict(_drawn_inputs(seed))
    spreads = {'L0_conv_D': (1.0, 0.2),
     'L0_conv_gn_gamma': (1.0, 0.2),
     'L0_conv_gn_beta': (0.0, 0.1),
     'L1_ffn_router_b': (0.0, 0.1),
     'L1_ffn_expert_b': (0.0, 0.1)}
    factors = {'L0_conv_W_x': 7.726,
     'L0_conv_W_dt': 30.708,
     'L0_conv_b_dt': 8.0,
     'L0_conv_A_log': 27.829,
     'L1_attn_w_attn': 2.695}
    for name, (base, spread) in spreads.items():
        noise = np.random.default_rng([zlib.crc32(name.encode()), seed]).standard_normal(out[name].shape)
        drawn = base * np.exp(spread * noise) if base else spread * noise
        out[name] = jnp.asarray(drawn.astype(out[name].dtype))
    for name, factor in factors.items():
        out[name] = (out[name] * factor).astype(out[name].dtype)
    return out
```

```python
from contextlib import ExitStack

import concourse.bass as bass
from concourse import mybir

F32 = mybir.dt.float32
BF16 = mybir.dt.bfloat16
ALU = mybir.AluOpType
ACT = mybir.ActivationFunctionType
AX = mybir.AxisListType

P = 128
BANK = 512
MASKED = -1e30
GN_EPS = 1e-5
LN_EPS = 1e-5


class Signal:

    def __init__(self, ctx, nc, name, per, base=0):
        self.sem = ctx.enter_context(nc.semaphore(name))
        self.per = per
        self.base = base

    def at(self, batch, count):
        return batch * self.per + (self.base + count)


def mamba_attention_moe(nc, x, W_in, conv_w, conv_b, W_x, W_dt, b_dt, A_log, D, W_out, gn_gamma, gn_beta,
                        w_attn, w_proj, router_w, router_b, expert_w, expert_b, out):
    B, C, HH, WW = x.shape
    T = HH * WW
    DI = W_in.shape[1] // 2
    R = W_dt.shape[0]
    NS = (W_x.shape[1] - R) // 2
    E = router_w.shape[1]
    H = 8
    DH = C // H
    G = 4
    CG = C // G
    TB = T // P
    NH = T // BANK
    QB = BANK // P
    CH = P // NS
    NJ = DI // CH
    NG = 4
    JG = NJ // NG
    GW = P // NG
    SCALE = float(DH) ** -0.5
    K1 = C + 32
    KQ = 9 * DH + 3
    QUAD = 4
    assert DI == P and NS * CH == P and T == NH * BANK

    xr = x.rearrange("b c h w -> b c (h w)")
    outr = out.rearrange("b c h w -> b c (h w)")
    qk_parts_dram = nc.dram_tensor("qk_parts_dram", (3, P, T), BF16, kind="Internal").ap()
    max_parts_dram = nc.dram_tensor("max_parts_dram", (3 * H, T), BF16, kind="Internal").ap()

    with ExitStack() as ctx:
        def sb(name, shape, dt=F32):
            return ctx.enter_context(nc.sbuf_tensor(name, shape, dt))

        ps = ctx.enter_context(nc.psum_tensor("ps", [P, 8, BANK], F32))

        def banks(n, k=1):
            return ps[:, n:n + k, :].rearrange("p a b -> p (a b)")

        w_conv = sb("w_conv", [P, DI])
        w_z = sb("w_z", [P, DI])
        conv_rows = sb("conv_rows", [P, 2 * DI])
        conv_bias = sb("conv_bias", [P, 1])
        w_x = sb("w_x", [P, R + 2 * NS])
        w_x_dt_t = sb("w_x_dt_t", [R, P])
        w_dt = sb("w_dt", [R, DI])
        w_dt_full = sb("w_dt_full", [P, DI])
        dt_bias = sb("dt_bias", [P, 1])
        w_bc = sb("w_bc", [P, 2, NS, CH])
        a_scale = sb("a_scale", [P, NJ])
        d_skip = sb("d_skip", [P, 1])
        w_out = sb("w_out", [P, C])
        gn_gamma_half = sb("gn_gamma_half", [C, 1])
        gn_beta_half = sb("gn_beta_half", [C, 1])
        group_mean = sb("group_mean", [C, G, CG])
        w_qk = sb("w_qk", [K1, 2 * C])
        w_v = sb("w_v", [K1, C])
        w_o = sb("w_o", [C, C])
        w_router = sb("w_router", [K1, E])
        w_expert = sb("w_expert", [K1, E, C])
        ident = sb("ident", [P, P])
        ident_bf = sb("ident_bf", [P, P], BF16)
        mask_q = sb("mask_q", [P, P], BF16)
        mask_k = sb("mask_k", [P, P], BF16)
        pick = sb("pick", [96, JG, NS, CH], BF16)
        fold = sb("fold", [P, JG, GW])
        state_sum = sb("state_sum", [P, CH])
        minus_half = sb("minus_half", [P, TB])
        expert_start = sb("expert_start", [P, TB, E])

        xs = sb("xs", [P, T])
        xc = sb("xc", [P, T])
        z_gate = sb("z_gate", [P, T])
        b_rep = sb("b_rep", [P, T])
        c_rep = sb("c_rep", [P, T])
        dt = sb("dt", [P, T])
        u = sb("u", [P, T])
        part = [sb(f"part{i}", [P, T], BF16) for i in range(6)]
        dt_rows = sb("dt_rows", [96, NG, T], BF16)
        u_rows = sb("u_rows", [96, NG, T], BF16)
        decay = sb("decay", [P, 2, T])
        drive = sb("drive", [P, 3, T])
        state = sb("state", [P, 2, T])
        read = sb("read", [P, 2 * NG, T])
        rest = decay
        z_tanh = decay[:, 0, :]
        relu = drive[:, 0, :]
        silu_h, silu_t = drive[:, 1, :], drive[:, 2, :]
        gn_h, gn_t = drive[0:C, 1, :], drive[0:C, 2, :]
        softplus_a, softplus_b = state[:, 0, :], state[:, 1, :]
        y_skip, y = state[:, 0, :], state[:, 1, :]
        gn_stats = sb("gn_stats", [C, 2, 6])
        gn_mv = sb("gn_mv", [C, 2])
        gn_group = sb("gn_group", [C, 2])
        gn_v = sb("gn_v", [C, 5])
        x1 = sb("x1", [C, T])
        t1 = sb("t1", [P, TB, C])
        t2 = sb("t2", [P, TB, C])
        xcen = sb("xcen", [P, TB, C])
        xsq = sb("xsq", [P, TB, C])
        xn = sb("xn", [P, TB, C])
        ln_s = sb("ln_s", [P, 5, TB])
        xn_t = sb("xn_t", [K1, T])
        v_aug = sb("v_aug", [P, TB, H, GW])
        q_stack = sb("q_stack", [P, H, T], BF16)
        k_stack = sb("k_stack", [P, H, T], BF16)
        row_max = sb("row_max", [P, TB, H])
        max_rest = sb("max_rest", [P, 2, TB, H])
        max_parts = sb("max_parts", [P, TB, 3, H], BF16)
        max_t = sb("max_t", [3 * H, T], BF16)
        den = sb("den", [P, TB, H])
        attn = sb("attn", [P, TB, C])
        moe_out = sb("moe_out", [P, TB, C])
        gate_m = sb("gate_m", [P, 4, TB])
        gate_e = sb("gate_e", [P, 10, TB, E])
        probs = read[:, 0:4, :].rearrange("p a (b c) -> p a b c", b=2)
        acc_sb = read[:, 4, :].rearrange("p (a b) -> p a b", a=2)
        attn_t = read[0:C, 5, :]
        x_out = read[0:C, 6, :]
        moe = read[:, 7, :].rearrange("p (a e c) -> p a e c", a=2, e=E)

        weights_in = ctx.enter_context(nc.semaphore("weights_in"))
        masks_built = ctx.enter_context(nc.semaphore("masks_built"))
        dve_setup = ctx.enter_context(nc.semaphore("dve_setup"))
        pe_setup = ctx.enter_context(nc.semaphore("pe_setup"))
        act_setup = ctx.enter_context(nc.semaphore("act_setup"))
        pool_chain = ctx.enter_context(nc.semaphore("pool_chain"))
        LOADS = 20 + NS
        setup_dmas = [0]

        with nc.Block() as block:
            @block.sync
            def _(sp):
                sp.wait_ge(dve_setup, 5)
                def load(dst, src, strided=False):
                    sp.dma_start(dst, src, allow_slow_non_contiguous=strided).then_inc(weights_in, 16)
                    setup_dmas[0] += 1
                load(w_conv[0:C, :], W_in[:, 0:DI])
                load(w_conv[C:2 * C, :], W_in[:, 0:DI])
                load(w_z[0:C, :], W_in[:, DI:2 * DI])
                load(conv_rows[:, :], conv_w.rearrange("(a d) k -> a (d k)", a=1).to_broadcast([P, 2 * DI]))
                load(conv_bias[:, :], conv_b.rearrange("(d a) -> d a", a=1))
                load(w_x[:, :], W_x[:, :])
                load(w_x_dt_t[:, :], W_x[:, 0:R].rearrange("d r -> r d"), strided=True)
                load(w_dt[:, :], W_dt[:, :])
                load(dt_bias[:, :], b_dt.rearrange("(d a) -> d a", a=1))
                for n in range(NS):
                    load(a_scale[n * CH:(n + 1) * CH, :], A_log[:, n].rearrange("(j e) -> e j", e=CH), strided=True)
                load(d_skip[:, :], D.rearrange("(d a) -> d a", a=1))
                load(w_out[:, :], W_out[:, :])
                load(gn_gamma_half[:, :], gn_gamma.rearrange("(d a) -> d a", a=1))
                load(gn_beta_half[:, :], gn_beta.rearrange("(d a) -> d a", a=1))
                load(w_qk[0:C, :], w_attn[:, 0:2 * C])
                load(w_v[0:C, :], w_attn[:, 2 * C:3 * C])
                load(w_o[:, :], w_proj[:, :])
                load(w_router[0:C, :], router_w[:, :])
                load(w_router[C:C + 1, :], router_b.rearrange("(a e) -> a e", a=1))
                load(w_expert[0:C, :, :], expert_w.rearrange("e d c -> d e c"))
                load(w_expert[C:C + 1, :, :], expert_b.rearrange("(a e) c -> a e c", a=1))
                assert setup_dmas[0] == LOADS

            @block.vector
            def _(dve):
                dve.memset(w_z[C:P, :], 0.0).then_inc(dve_setup, 1)
                dve.memset(w_qk[C:K1, :], 0.0).then_inc(dve_setup, 1)
                dve.memset(w_v[C:K1, :], 0.0).then_inc(dve_setup, 1)
                dve.memset(w_router[C:K1, :], 0.0).then_inc(dve_setup, 1)
                dve.memset(w_expert[C:K1, :, :], 0.0).then_inc(dve_setup, 1)
                dve.memset(xn_t[C:K1, :], 1.0).then_inc(dve_setup, 1)
                dve.memset(xs[C:2 * C, 0:1], 0.0).then_inc(dve_setup, 1)
                dve.memset(v_aug[:, :, :, DH:GW], 1.0).then_inc(dve_setup, 1)
                dve.memset(k_stack[64:96, :, :], 1.0).then_inc(dve_setup, 1)
                dve.memset(minus_half[:, :], -0.5).then_inc(dve_setup, 1)
                dve.memset(expert_start[:, :, :], 1.0).then_inc(dve_setup, 1)
                dve.wait_ge(dve_setup, 11)
                dve.memset(expert_start[:, :, 0:1], 0.0).then_inc(dve_setup, 1)
                dve.wait_ge(weights_in, 16 * LOADS)
                conv_k = conv_rows[:, :].rearrange("p (d k) -> p k d", k=2)
                for rows, tap in ((slice(0, C), 1), (slice(C, 2 * C), 0)):
                    dve.scalar_tensor_tensor(w_conv[rows, :], w_conv[rows, :], 0.5, conv_k[rows, tap, :],
                                             ALU.mult, ALU.mult).then_inc(dve_setup, 1)
                for t in (w_z[0:C, :], conv_bias[:, :], gn_gamma_half[:, :], gn_beta_half[:, :]):
                    dve.tensor_scalar(t, t, 0.5, None, ALU.mult).then_inc(dve_setup, 1)
                for k in range(2):
                    cols = w_x[:, R + k * NS:R + (k + 1) * NS]
                    dve.tensor_copy(w_bc[:, k, :, :], cols.unsqueeze(2).to_broadcast([P, NS, CH]))\
                       .then_inc(dve_setup, 1)
                dve.wait_ge(pe_setup, 1)
                dve.tensor_copy(w_dt_full[:, :], ps[:, 0, 0:DI]).then_inc(dve_setup, 1)
                dve.wait_ge(act_setup, 1)
                dve.tensor_scalar(a_scale[:, :], a_scale[:, :], -1.0, None, ALU.mult).then_inc(dve_setup, 1)
                dve.wait_ge(masks_built, 1)
                for q in range(JG):
                    dve.tensor_copy(fold[:, q, q * CH:(q + 1) * CH], state_sum[:, :]).then_inc(dve_setup, 1)

            @block.scalar
            def _(act):
                act.wait_ge(weights_in, 16 * LOADS)
                act.activation(a_scale[:, :], a_scale[:, :], ACT.Exp).then_inc(act_setup, 1)

            @block.tensor
            def _(pe):
                pe.wait_ge(weights_in, 16 * LOADS)
                pe.matmul(ps[:, 0, 0:DI], w_x_dt_t[:, :], w_dt[:, :], start=True, stop=True).then_inc(pe_setup, 1)

            @block.gpsimd
            def _(pool):
                step = [0]

                def then(ins):
                    ins.then_inc(pool_chain, 1)
                    step[0] += 1
                    pool.wait_ge(pool_chain, step[0])

                def diagonal(tile, pattern, base, fill=1.0, op=ALU.not_equal, mult=1):
                    then(pool.affine_select(out=tile, in_=tile, pattern=pattern, compare_op=op, fill=fill,
                                            base=base, channel_multiplier=mult))
                then(pool.memset(state_sum[:, :], 0.0))
                then(pool.memset(fold[:, :, :], 0.0))
                for n in range(NS):
                    diagonal(state_sum[:, :], [[-1, CH]], -CH * n)
                pool.memset(ident[:, :], 0.0).then_inc(masks_built, 1)
                then(pool.memset(ident_bf[:, :], 0.0))
                pool.wait_ge(masks_built, 1)
                diagonal(ident[:, :], [[-1, P]], 0)
                diagonal(ident_bf[:, :], [[-1, P]], 0)
                then(pool.memset(pick[:, :, :, :], 0.0))
                for part_row in range(3):
                    diagonal(pick[:, :, :, :], [[-CH, JG], [0, NS], [-1, CH]], -32 * part_row)
                then(pool.memset(mask_q[:, :], 0.0))
                diagonal(mask_q[:, :], [[-1, P]], 0, MASKED, ALU.is_ge)
                then(pool.memset(mask_k[:, :], 0.0))
                diagonal(mask_k[:, :], [[1, P]], 0, MASKED, ALU.is_ge, -1)
                then(pool.memset(group_mean[:, :, :], 1.0 / CG))
                diagonal(group_mean[:, :, :], [[-CG, G], [0, CG]], 0, 0.0, ALU.is_ge)
                diagonal(group_mean[:, :, :], [[CG, G], [0, CG]], CG - 1, 0.0, ALU.is_ge, -1)

        def signal(name, per, base=0):
            return Signal(ctx, nc, name, per, base)

        x_in = signal("x_in", 32)
        dt_rows_in = signal("dt_rows_in", 16 * 3 * NG)
        u_rows_in = signal("u_rows_in", 16 * 3 * NG)
        qk_parts_out = signal("qk_parts_out", 16 * 3, base=1)
        stacks_in = signal("stacks_in", 16 * 18)
        max_t_out = signal("max_t_out", 16)
        max_in = signal("max_in", 16)
        out_stored = signal("out_stored", 16, base=1)

        conv_ps = signal("conv_ps", 1)
        z_ps = signal("z_ps", 1)
        dt_ps = signal("dt_ps", 1)
        bc_ps = signal("bc_ps", 2)
        dt_rep = signal("dt_rep", NJ)
        u_rep = signal("u_rep", NJ)
        folded = signal("folded", JG)
        out_ps = signal("out_ps", 1)
        gn_ps = signal("gn_ps", 1)
        t1_ps = signal("t1_ps", 1)
        xnt_ps = signal("xnt_ps", 2)
        qk_ps = signal("qk_ps", 1)
        v_ps = signal("v_ps", 1)
        SCORE_STEPS = [(i, h, 4 if i < QB else 2) for i in range(TB) for h in range(0, H, 4 if i < QB else 2)]
        scores_ps = signal("scores_ps", len(SCORE_STEPS))
        max_t_ps = signal("max_t_ps", 1)
        GROUPS = [(quad, half) for quad in range(H // QUAD) for half in range(NH)]
        KEY_STEPS = [(n, quad, half, j) for n, (quad, half) in enumerate(GROUPS) for j in range(QB * (half + 1))]
        LAST_STEP = [max(s for s, ks in enumerate(KEY_STEPS) if ks[0] == n) for n in range(len(GROUPS))]
        weights_ps = signal("weights_ps", 2 * len(KEY_STEPS))
        values_added = signal("values_added", len(KEY_STEPS))
        heads_t_ps = signal("heads_t_ps", len(GROUPS))
        attn_t_ps = signal("attn_t_ps", 1)
        proj_ps = signal("proj_ps", 1)
        router_ps = signal("router_ps", 1)
        expert_ps = signal("expert_ps", TB)
        x_out_ps = signal("x_out_ps", 1)

        silu_parts = signal("silu_parts", 2)
        z_tanh_done = signal("z_tanh_done", 1)
        softplus_steps = signal("softplus_steps", 3)
        b_copied = signal("b_copied", 1)
        c_copied = signal("c_copied", 1)
        high_parts = signal("high_parts", 3)
        mid_parts = signal("mid_parts", 3)
        decayed = signal("decayed", NJ)
        gn_parts = signal("gn_parts", 2)
        t1_copied = signal("t1_copied", 1)
        squared = signal("squared", 2)
        xnt_copied = signal("xnt_copied", 2)
        exped = signal("exped", 2 * len(KEY_STEPS))
        acc_copied = signal("acc_copied", len(GROUPS))
        attn_t_copied = signal("attn_t_copied", 1)
        gate_exped = signal("gate_exped", 1)
        x_out_copied = signal("x_out_copied", 1, base=1)

        xc_ready = signal("xc_ready", 1)
        z_ready = signal("z_ready", 1)
        relued = signal("relued", 1)
        dt_ready = signal("dt_ready", 1)
        u_ready = signal("u_ready", 1)
        rests = signal("rests", 3)
        low_parts = signal("low_parts", 3)
        driven = signal("driven", NJ)
        scanned = signal("scanned", NJ)
        skipped = signal("skipped", 1)
        y_ready = signal("y_ready", 1)
        gn_chain = signal("gn_chain", 9)
        gn_bias = signal("gn_bias", 1)
        gn_gated = signal("gn_gated", 1)
        x1_ready = signal("x1_ready", 1, base=1)
        ln_chain = signal("ln_chain", 6)
        centred = signal("centred", 2)
        ln_var = signal("ln_var", 2)
        xn_ready = signal("xn_ready", 2)
        v_copied = signal("v_copied", 1)
        row_maxed = signal("row_maxed", len(SCORE_STEPS))
        max_chain = signal("max_chain", 3)
        max_parts_ready = signal("max_parts_ready", 1)
        max_t_copied = signal("max_t_copied", 1)
        den_ready = signal("den_ready", len(GROUPS))
        attn_ready = signal("attn_ready", len(GROUPS))
        t2_ready = signal("t2_ready", 1)
        gate_chain = signal("gate_chain", 15)
        gate_centred = signal("gate_centred", 1)
        weighted = signal("weighted", TB)
        combined = signal("combined", TB)
        x2_ready = signal("x2_ready", 1)

        read_out = signal("read_out", NJ)
        gn_rstd = signal("gn_rstd", 1)
        ln_rstd = signal("ln_rstd", 2)

        def chunk(k):
            g, q = k % NG, k // NG
            return g, q, JG * g + q

        def halves(n):
            return slice(n * BANK, (n + 1) * BANK)

        def tokens(i):
            return slice(i * P, (i + 1) * P)

        def dt_bank(k):
            return 0 if k % 2 == 0 else 4

        held = {}
        for name in ("pe", "dve"):
            held[name] = ctx.enter_context(nc.semaphore(f"held_{name}"))

        def hold(engine, name):
            engine.sem_inc(held[name])

        with nc.Block() as block:
            @block.sync
            def _(sp):
                with sp.Fori(0, B) as b:
                    sp.wait_ge(x1_ready.sem, x1_ready.at(b, 0))
                    sp.dma_start(xs[0:C, :], xr[b, :, :]).then_inc(x_in.sem, 16)
                    sp.dma_start(xs[C:2 * C, 1:T], xr[b, :, 0:T - 1]).then_inc(x_in.sem, 16)
                    for rows, arrived, first, n in ((dt_rows, dt_rows_in, 0, 0), (u_rows, u_rows_in, 3, 1)):
                        for p, parts in enumerate((high_parts, mid_parts, low_parts)):
                            sp.wait_ge(parts.sem, parts.at(b, n + 1))
                            for g in range(NG):
                                sp.dma_start(rows[32 * p:32 * (p + 1), g, :], part[first + p][GW * g:GW * (g + 1), :])\
                                  .then_inc(arrived.sem, 16)
                    for p, parts in enumerate((high_parts, mid_parts, low_parts)):
                        sp.wait_ge(parts.sem, parts.at(b, 3))
                        sp.dma_start(qk_parts_dram[p, :, :], part[p][:, :]).then_inc(qk_parts_out.sem, 16)
                    sp.wait_ge(qk_parts_out.sem, qk_parts_out.at(b, 48))
                    for p in range(3):
                        for r in range(3):
                            rows = slice(DH * (3 * p + r), DH * (3 * p + r + 1))
                            sp.dma_start(q_stack[rows, :, :],
                                         qk_parts_dram[p, 0:C, :].rearrange("(h d) t -> d h t", d=DH))\
                              .then_inc(stacks_in.sem, 16)
                            sp.dma_start(k_stack[rows, :, :],
                                         qk_parts_dram[r, C:2 * C, :].rearrange("(h d) t -> d h t", d=DH))\
                              .then_inc(stacks_in.sem, 16)
                    sp.wait_ge(max_t_copied.sem, max_t_copied.at(b, 1))
                    sp.dma_start(max_parts_dram[:, :], max_t[:, :]).then_inc(max_t_out.sem, 16)
                    sp.wait_ge(max_t_out.sem, max_t_out.at(b, 16))
                    sp.dma_start(q_stack[KQ - 3:KQ, :, :],
                                 max_parts_dram.rearrange("(r h) t -> r h t", h=H)).then_inc(max_in.sem, 16)
                    sp.wait_ge(x_out_copied.sem, x_out_copied.at(b, 1))
                    sp.dma_start(outr[b, :, :], x_out).then_inc(out_stored.sem, 16)
                sp.wait_ge(out_stored.sem, out_stored.at(B, 0))

            @block.gpsimd
            def _(pool):
                for across_batches in (out_stored, x1_ready, x_out_copied, qk_parts_out):
                    pool.sem_inc(across_batches.sem, across_batches.base)
                with pool.Fori(0, B) as b:
                    pool.wait_ge(c_copied.sem, c_copied.at(b, 1))
                    for k in range(NJ):
                        pool.wait_ge(scanned.sem, scanned.at(b, k + 1))
                        if k >= 2 * NG:
                            pool.wait_ge(folded.sem, folded.at(b, k // NG - 1))
                        pool.tensor_tensor(read[:, k % (2 * NG), :], state[:, k % 2, :], c_rep[:, :], ALU.mult)\
                            .then_inc(read_out.sem, 1)
                    pool.wait_ge(gn_chain.sem, gn_chain.at(b, 7))
                    pool.tensor_tensor(gn_v[:, 1:2], gn_v[:, 0:1], minus_half[0:C, 0:1], ALU.pow)\
                        .then_inc(gn_rstd.sem, 1)
                    for n in range(2):
                        pool.wait_ge(ln_var.sem, ln_var.at(b, n + 1))
                        pool.tensor_tensor(ln_s[:, 4, :], ln_s[:, 3, :], minus_half[:, :], ALU.pow)\
                            .then_inc(ln_rstd.sem, 1)

            @block.scalar
            def _(act):
                with act.Fori(0, B) as b:
                    act.wait_ge(conv_ps.sem, conv_ps.at(b, 1))
                    act.activation(silu_h, banks(0, 2), ACT.Identity, bias=conv_bias[:, :]).then_inc(silu_parts.sem, 1)
                    act.activation(silu_t, banks(0, 2), ACT.Tanh, bias=conv_bias[:, :]).then_inc(silu_parts.sem, 1)
                    act.wait_ge(z_ps.sem, z_ps.at(b, 1))
                    act.activation(z_tanh, banks(2, 2), ACT.Tanh).then_inc(z_tanh_done.sem, 1)
                    act.wait_ge(dt_ps.sem, dt_ps.at(b, 1))
                    act.activation(softplus_a, banks(4, 2), ACT.Abs, bias=dt_bias[:, :])\
                       .then_inc(softplus_steps.sem, 1)
                    act.wait_ge(softplus_steps.sem, softplus_steps.at(b, 1))
                    act.activation(softplus_b, softplus_a, ACT.Exp, scale=-1.0).then_inc(softplus_steps.sem, 1)
                    act.wait_ge(softplus_steps.sem, softplus_steps.at(b, 2))
                    act.activation(softplus_a, softplus_b, ACT.Ln, bias=1.0).then_inc(softplus_steps.sem, 1)
                    act.wait_ge(bc_ps.sem, bc_ps.at(b, 1))
                    act.copy(b_rep[:, :], banks(0, 2)).then_inc(b_copied.sem, 1)
                    act.wait_ge(bc_ps.sem, bc_ps.at(b, 2))
                    act.copy(c_rep[:, :], banks(2, 2)).then_inc(c_copied.sem, 1)
                    act.wait_ge(qk_parts_out.sem, qk_parts_out.at(b, 0))
                    for n, (src, ready) in enumerate(((dt, dt_ready), (u, u_ready))):
                        act.wait_ge(ready.sem, ready.at(b, 1))
                        act.copy(part[3 * n][:, :], src[:, :]).then_inc(high_parts.sem, 1)
                    for n in range(2):
                        act.wait_ge(rests.sem, rests.at(b, n + 1))
                        act.copy(part[3 * n + 1][:, :], rest[:, n, :]).then_inc(mid_parts.sem, 1)
                    for k in range(NJ):
                        j = chunk(k)[2]
                        act.wait_ge(dt_rep.sem, dt_rep.at(b, k + 1))
                        if k >= 2:
                            act.wait_ge(scanned.sem, scanned.at(b, k - 1))
                        else:
                            act.wait_ge(low_parts.sem, low_parts.at(b, 2))
                        act.activation(decay[:, k % 2, :], banks(dt_bank(k), 2), ACT.Exp, scale=a_scale[:, j:j + 1])\
                           .then_inc(decayed.sem, 1)
                    act.wait_ge(gn_bias.sem, gn_bias.at(b, 1))
                    act.activation(gn_h, banks(0, 2)[0:C, :], ACT.Identity, bias=gn_v[:, 4:5], scale=gn_v[:, 2:3])\
                       .then_inc(gn_parts.sem, 1)
                    act.activation(gn_t, banks(0, 2)[0:C, :], ACT.Tanh, bias=gn_v[:, 4:5], scale=gn_v[:, 2:3])\
                       .then_inc(gn_parts.sem, 1)
                    def norm(n):
                        act.wait_ge(centred.sem, centred.at(b, n + 1))
                        act.activation(xsq[:, :, :], xcen[:, :, :], ACT.Square).then_inc(squared.sem, 1)
                        if n == 0:
                            act.copy(t1[:, :, :], banks(3).rearrange("p (i c) -> p i c", c=C))\
                               .then_inc(t1_copied.sem, 1)
                        act.wait_ge(xnt_ps.sem, xnt_ps.at(b, n + 1))
                        act.copy(xn_t[0:C, :], banks(4 - n, 2)[0:C, :]).then_inc(xnt_copied.sem, 1)
                    norm(0)
                    act.wait_ge(qk_ps.sem, qk_ps.at(b, 1))
                    act.wait_ge(dt_rows_in.sem, dt_rows_in.at(b, 16 * 3 * NG))
                    act.copy(part[0][:, :], banks(0, 2)).then_inc(high_parts.sem, 1)
                    act.wait_ge(rests.sem, rests.at(b, 3))
                    act.copy(part[1][:, :], rest[:, 0, :]).then_inc(mid_parts.sem, 1)

                    def copy_sums(n):
                        act.wait_ge(values_added.sem, values_added.at(b, LAST_STEP[n] + 1))
                        if n >= 2:
                            act.wait_ge(heads_t_ps.sem, heads_t_ps.at(b, n - 1))
                        act.copy(acc_sb[:, n % 2, :], banks(6 + n % 2)).then_inc(acc_copied.sem, 1)

                    for s, (n, quad, half, j) in enumerate(KEY_STEPS):
                        w = BANK - max(0, j * P - half * BANK)
                        for pair in range(2):
                            m = 2 * s + pair
                            act.wait_ge(weights_ps.sem, weights_ps.at(b, m + 1))
                            if s >= 2:
                                act.wait_ge(values_added.sem, values_added.at(b, s - 1))
                            act.activation(probs[:, m % 4, :, 0:w], ps[:, 2 * (m % 2):2 * (m % 2) + 2, 0:w],
                                           ACT.Exp, scale=SCALE).then_inc(exped.sem, 1)
                        if n > 0 and s == LAST_STEP[n - 1] + 2:
                            copy_sums(n - 1)
                    copy_sums(len(GROUPS) - 1)
                    act.wait_ge(attn_t_ps.sem, attn_t_ps.at(b, 1))
                    act.copy(attn_t, banks(0, 2)[0:C, :]).then_inc(attn_t_copied.sem, 1)
                    norm(1)
                    act.wait_ge(gate_centred.sem, gate_centred.at(b, 1))
                    act.activation(gate_e[:, 1, :, :], gate_e[:, 0, :, :], ACT.Exp).then_inc(gate_exped.sem, 1)
                    act.wait_ge(x_out_ps.sem, x_out_ps.at(b, 1))
                    act.wait_ge(out_stored.sem, out_stored.at(b, 0))
                    act.copy(x_out, banks(0, 2)[0:C, :]).then_inc(x_out_copied.sem, 1)

            @block.vector
            def _(dve):
                with dve.Fori(0, B) as b:
                    dve.wait_ge(silu_parts.sem, silu_parts.at(b, 2))
                    dve.scalar_tensor_tensor(xc[:, :], silu_t, 1.0, silu_h, ALU.add, ALU.mult)\
                       .then_inc(xc_ready.sem, 1)
                    dve.wait_ge(z_tanh_done.sem, z_tanh_done.at(b, 1))
                    dve.scalar_tensor_tensor(z_gate[:, :], z_tanh, 1.0, banks(2, 2), ALU.add, ALU.mult)\
                       .then_inc(z_ready.sem, 1)
                    dve.wait_ge(softplus_steps.sem, softplus_steps.at(b, 1))
                    dve.tensor_scalar(relu, banks(4, 2), dt_bias[:, :], 0.0, ALU.add, ALU.max).then_inc(relued.sem, 1)
                    dve.wait_ge(softplus_steps.sem, softplus_steps.at(b, 3))
                    dve.wait_ge(relued.sem, relued.at(b, 1))
                    dve.tensor_tensor(dt[:, :], relu, softplus_a, ALU.add).then_inc(dt_ready.sem, 1)
                    dve.wait_ge(dt_ready.sem, dt_ready.at(b, 1))
                    dve.tensor_tensor(u[:, :], dt[:, :], xc[:, :], ALU.mult).then_inc(u_ready.sem, 1)
                    for n, src in enumerate((dt, u)):
                        dve.wait_ge(high_parts.sem, high_parts.at(b, n + 1))
                        dve.tensor_tensor(rest[:, n, :], src[:, :], part[3 * n][:, :], ALU.subtract)\
                           .then_inc(rests.sem, 1)
                    for n in range(2):
                        dve.wait_ge(mid_parts.sem, mid_parts.at(b, n + 1))
                        dve.tensor_tensor(part[3 * n + 2][:, :], rest[:, n, :], part[3 * n + 1][:, :], ALU.subtract)\
                           .then_inc(low_parts.sem, 1)

                    def make_drive(k):
                        dve.wait_ge(u_rep.sem, u_rep.at(b, k + 1))
                        if k >= 3:
                            dve.wait_ge(scanned.sem, scanned.at(b, k - 2))
                        dve.tensor_tensor(drive[:, k % 3, :], banks(2, 2), b_rep[:, :], ALU.mult)\
                           .then_inc(driven.sem, 1)
                    dve.wait_ge(b_copied.sem, b_copied.at(b, 1))
                    make_drive(0)
                    for k in range(NJ):
                        if k + 1 < NJ:
                            make_drive(k + 1)
                        dve.wait_ge(decayed.sem, decayed.at(b, k + 1))
                        dve.wait_ge(driven.sem, driven.at(b, k + 1))
                        if k >= 2:
                            dve.wait_ge(read_out.sem, read_out.at(b, k - 1))
                        dve.tensor_tensor_scan(state[:, k % 2, :], decay[:, k % 2, :], drive[:, k % 3, :], 0.0,
                                               ALU.mult, ALU.add).then_inc(scanned.sem, 1)
                    dve.wait_ge(folded.sem, folded.at(b, JG))
                    dve.scalar_tensor_tensor(y_skip, xc[:, :], d_skip[:, :], banks(6, 2), ALU.mult, ALU.add)\
                       .then_inc(skipped.sem, 1)
                    dve.wait_ge(skipped.sem, skipped.at(b, 1))
                    dve.tensor_tensor(y, y_skip, z_gate[:, :], ALU.mult).then_inc(y_ready.sem, 1)

                    dve.wait_ge(out_ps.sem, out_ps.at(b, 1))
                    for h in range(NH):
                        dve.bn_stats(gn_stats[:, h, :], ps[0:C, h, :]).then_inc(gn_chain.sem, 1)
                    dve.wait_ge(gn_chain.sem, gn_chain.at(b, 2))
                    hold(dve, "dve")
                    dve.bn_aggr(gn_mv[:, :], gn_stats[:, :, :]).then_inc(gn_chain.sem, 1)
                    dve.wait_ge(gn_chain.sem, gn_chain.at(b, 3))
                    dve.scalar_tensor_tensor(gn_mv[:, 1:2], gn_mv[:, 0:1], gn_mv[:, 0:1], gn_mv[:, 1:2],
                                             ALU.mult, ALU.add).then_inc(gn_chain.sem, 1)
                    dve.wait_ge(gn_ps.sem, gn_ps.at(b, 1))
                    dve.tensor_copy(gn_group[:, :], ps[0:C, 2, 0:2]).then_inc(gn_chain.sem, 1)
                    dve.wait_ge(gn_chain.sem, gn_chain.at(b, 5))
                    mean, mean_sq = gn_group[:, 0:1], gn_group[:, 1:2]
                    dve.scalar_tensor_tensor(gn_v[:, 3:4], mean, mean, mean_sq, ALU.mult, ALU.subtract)\
                       .then_inc(gn_chain.sem, 1)
                    dve.wait_ge(gn_chain.sem, gn_chain.at(b, 6))
                    dve.tensor_scalar(gn_v[:, 0:1], gn_v[:, 3:4], -1.0, GN_EPS, ALU.mult, ALU.add)\
                       .then_inc(gn_chain.sem, 1)
                    dve.wait_ge(gn_rstd.sem, gn_rstd.at(b, 1))
                    dve.tensor_tensor(gn_v[:, 2:3], gn_v[:, 1:2], gn_gamma_half[:, :], ALU.mult)\
                       .then_inc(gn_chain.sem, 1)
                    dve.wait_ge(gn_chain.sem, gn_chain.at(b, 8))
                    dve.scalar_tensor_tensor(gn_v[:, 3:4], mean, gn_v[:, 2:3], gn_beta_half[:, :],
                                             ALU.mult, ALU.subtract).then_inc(gn_chain.sem, 1)
                    dve.wait_ge(gn_chain.sem, gn_chain.at(b, 9))
                    dve.tensor_scalar(gn_v[:, 4:5], gn_v[:, 3:4], -1.0, None, ALU.mult).then_inc(gn_bias.sem, 1)
                    dve.wait_ge(gn_parts.sem, gn_parts.at(b, 2))
                    dve.scalar_tensor_tensor(x1[:, :], gn_t, 1.0, gn_h, ALU.add, ALU.mult).then_inc(gn_gated.sem, 1)
                    dve.wait_ge(gn_gated.sem, gn_gated.at(b, 1))
                    dve.tensor_tensor(x1[:, :], x1[:, :], xs[0:C, :], ALU.add).then_inc(x1_ready.sem, 1)

                    def norm(n, src):
                        dve.tensor_reduce(ln_s[:, 0, :], src, AX.X, ALU.add).then_inc(ln_chain.sem, 1)
                        dve.wait_ge(ln_chain.sem, ln_chain.at(b, 3 * n + 1))
                        dve.tensor_scalar(ln_s[:, 1, :], ln_s[:, 0, :], 1.0 / C, None, ALU.mult)\
                           .then_inc(ln_chain.sem, 1)
                        dve.wait_ge(ln_chain.sem, ln_chain.at(b, 3 * n + 2))
                        dve.tensor_tensor(xcen[:, :, :], src, ln_s[:, 1, :].unsqueeze(2).to_broadcast([P, TB, C]),
                                          ALU.subtract).then_inc(centred.sem, 1)
                        dve.wait_ge(squared.sem, squared.at(b, n + 1))
                        dve.tensor_reduce(ln_s[:, 2, :], xsq[:, :, :], AX.X, ALU.add).then_inc(ln_chain.sem, 1)
                        dve.wait_ge(ln_chain.sem, ln_chain.at(b, 3 * n + 3))
                        dve.tensor_scalar(ln_s[:, 3, :], ln_s[:, 2, :], 1.0 / C, LN_EPS, ALU.mult, ALU.add)\
                           .then_inc(ln_var.sem, 1)
                        dve.wait_ge(ln_rstd.sem, ln_rstd.at(b, n + 1))
                        dve.tensor_tensor(xn[:, :, :], xcen[:, :, :],
                                          ln_s[:, 4, :].unsqueeze(2).to_broadcast([P, TB, C]), ALU.mult)\
                           .then_inc(xn_ready.sem, 1)
                    dve.wait_ge(t1_ps.sem, t1_ps.at(b, 1))
                    norm(0, banks(3).rearrange("p (i c) -> p i c", c=C))

                    dve.wait_ge(high_parts.sem, high_parts.at(b, 3))
                    dve.tensor_tensor(rest[:, 0, :], banks(0, 2), part[0][:, :], ALU.subtract).then_inc(rests.sem, 1)
                    dve.wait_ge(v_ps.sem, v_ps.at(b, 1))
                    dve.tensor_copy(v_aug[:, :, :, 0:DH], banks(2).rearrange("p (i h d) -> p i h d", h=H, d=DH))\
                       .then_inc(v_copied.sem, 1)
                    dve.wait_ge(mid_parts.sem, mid_parts.at(b, 3))
                    dve.tensor_tensor(part[2][:, :], rest[:, 0, :], part[1][:, :], ALU.subtract)\
                       .then_inc(low_parts.sem, 1)

                    for s, (i, h0, nh) in enumerate(SCORE_STEPS):
                        dve.wait_ge(scores_ps.sem, scores_ps.at(b, s + 1))
                        stride = BANK if nh == 4 else 2 * BANK
                        scores = banks(4 * (s % 2), 4).rearrange("p (h k) -> p h k", k=stride)[:, :, 0:P * (i + 1)]
                        dve.tensor_reduce(row_max[:, i, h0:h0 + nh], scores, AX.X, ALU.max, negate=True)\
                           .then_inc(row_maxed.sem, 1)
                    dve.wait_ge(row_maxed.sem, row_maxed.at(b, len(SCORE_STEPS)))
                    dve.tensor_copy(max_parts[:, :, 0, :], row_max[:, :, :]).then_inc(max_chain.sem, 1)
                    dve.wait_ge(max_chain.sem, max_chain.at(b, 1))
                    dve.tensor_tensor(max_rest[:, 0, :, :], row_max[:, :, :], max_parts[:, :, 0, :], ALU.subtract)\
                       .then_inc(max_chain.sem, 1)
                    dve.wait_ge(max_chain.sem, max_chain.at(b, 2))
                    dve.tensor_copy(max_parts[:, :, 1, :], max_rest[:, 0, :, :]).then_inc(max_chain.sem, 1)
                    dve.wait_ge(max_chain.sem, max_chain.at(b, 3))
                    dve.tensor_tensor(max_parts[:, :, 2, :], max_rest[:, 0, :, :], max_parts[:, :, 1, :],
                                      ALU.subtract).then_inc(max_parts_ready.sem, 1)
                    dve.wait_ge(max_t_ps.sem, max_t_ps.at(b, 1))
                    dve.tensor_copy(max_t[:, :], banks(0).bitcast(BF16)[0:3 * H, :]).then_inc(max_t_copied.sem, 1)

                    for n, (quad, half) in enumerate(GROUPS):
                        dve.wait_ge(heads_t_ps.sem, heads_t_ps.at(b, n + 1))
                        heads = banks(4 + n % 2).rearrange("p (i h d) -> p i h d", i=QB, d=GW)
                        blocks, hs = slice(half * QB, (half + 1) * QB), slice(quad * QUAD, (quad + 1) * QUAD)
                        dve.reciprocal(den[:, blocks, hs], heads[:, :, :, DH]).then_inc(den_ready.sem, 1)
                        dve.wait_ge(den_ready.sem, den_ready.at(b, n + 1))
                        out_heads = attn[:, blocks, :].rearrange("p i (h d) -> p i h d", d=DH)[:, :, hs, :]
                        dve.tensor_tensor(out_heads, heads[:, :, :, 0:DH],
                                          den[:, blocks, hs].unsqueeze(3).to_broadcast([P, QB, QUAD, DH]),
                                          ALU.mult).then_inc(attn_ready.sem, 1)
                    dve.wait_ge(proj_ps.sem, proj_ps.at(b, 1))
                    dve.wait_ge(t1_copied.sem, t1_copied.at(b, 1))
                    dve.tensor_tensor(t2[:, :, :], t1[:, :, :], banks(2).rearrange("p (i c) -> p i c", c=C), ALU.add)\
                       .then_inc(t2_ready.sem, 1)
                    dve.wait_ge(t2_ready.sem, t2_ready.at(b, 1))
                    norm(1, t2[:, :, :])

                    (centre, ex, is_1, count_1, first, left, is_2, count_2, both, gate) = (
                        gate_e[:, k, :, :] for k in range(10))
                    top, top_1, top_2, inverse = (gate_m[:, k, :] for k in range(4))
                    step = [0]

                    def then(ins):
                        step[0] += 1
                        ins.then_inc(gate_chain.sem, 1)
                        dve.wait_ge(gate_chain.sem, gate_chain.at(b, step[0]))

                    def flat(t):
                        return t.rearrange("p i e -> p (i e)")

                    def per_expert(t):
                        return t.unsqueeze(2).to_broadcast([P, TB, E])
                    dve.wait_ge(router_ps.sem, router_ps.at(b, 1))
                    logits = banks(5)[:, 0:TB * E].rearrange("p (i e) -> p i e", e=E)
                    then(dve.tensor_reduce(top, logits, AX.X, ALU.max))
                    dve.tensor_tensor(centre, logits, per_expert(top), ALU.subtract).then_inc(gate_centred.sem, 1)
                    dve.wait_ge(gate_exped.sem, gate_exped.at(b, 1))
                    then(dve.tensor_reduce(top_1, ex, AX.X, ALU.max))
                    then(dve.tensor_tensor(is_1, ex, per_expert(top_1), ALU.is_ge))
                    then(dve.tensor_tensor_scan(flat(count_1), flat(expert_start[:, :, :]), flat(is_1), 0.0,
                                                ALU.mult, ALU.add))
                    then(dve.scalar_tensor_tensor(first, count_1, 1.0, is_1, ALU.is_equal, ALU.mult))
                    then(dve.scalar_tensor_tensor(left, first, -2.0, ex, ALU.mult, ALU.add))
                    then(dve.tensor_reduce(top_2, left, AX.X, ALU.max))
                    then(dve.tensor_tensor(is_2, left, per_expert(top_2), ALU.is_ge))
                    then(dve.tensor_tensor_scan(flat(count_2), flat(expert_start[:, :, :]), flat(is_2), 0.0,
                                                ALU.mult, ALU.add))
                    then(dve.scalar_tensor_tensor(both, count_2, 1.0, is_2, ALU.is_equal, ALU.mult))
                    then(dve.tensor_tensor(both, both, first, ALU.add))
                    then(dve.tensor_tensor(top, top_1, top_2, ALU.add))
                    then(dve.reciprocal(inverse, top))
                    then(dve.tensor_tensor(both, both, ex, ALU.mult))
                    then(dve.tensor_tensor(gate, both, per_expert(inverse), ALU.mult))

                    for i in range(TB):
                        dve.wait_ge(expert_ps.sem, expert_ps.at(b, i + 1))
                        if i >= 2:
                            dve.wait_ge(combined.sem, combined.at(b, i - 1))
                        dve.tensor_tensor(moe[:, i % 2, :, :], banks(6 + i % 2).rearrange("p (e c) -> p e c", c=C),
                                          gate[:, i, :].unsqueeze(2).to_broadcast([P, E, C]), ALU.mult)\
                           .then_inc(weighted.sem, 1)
                        dve.wait_ge(weighted.sem, weighted.at(b, i + 1))
                        dve.tensor_reduce(moe_out[:, i, :], moe[:, i % 2, :, :].rearrange("p e c -> p c e"), AX.X,
                                          ALU.add).then_inc(combined.sem, 1)
                    dve.wait_ge(combined.sem, combined.at(b, TB))
                    dve.tensor_tensor(moe_out[:, :, :], moe_out[:, :, :], t2[:, :, :], ALU.add)\
                       .then_inc(x2_ready.sem, 1)

            @block.tensor
            def _(pe):
                with pe.Fori(0, B) as b:
                    pe.wait_ge(x_in.sem, x_in.at(b, 32))
                    pe.wait_ge(x_out_copied.sem, x_out_copied.at(b, 0))
                    for h in range(NH):
                        last = pe.matmul(ps[:, h, :], w_conv[:, :], xs[:, halves(h)], start=True, stop=True)
                    last.then_inc(conv_ps.sem, 1)
                    for h in range(NH):
                        last = pe.matmul(ps[:, 2 + h, :], w_z[:, :], xs[:, halves(h)], start=True, stop=True)
                    last.then_inc(z_ps.sem, 1)
                    pe.wait_ge(xc_ready.sem, xc_ready.at(b, 1))
                    for h in range(NH):
                        last = pe.matmul(ps[:, 4 + h, :], w_dt_full[:, :], xc[:, halves(h)], start=True, stop=True)
                    last.then_inc(dt_ps.sem, 1)
                    for k in range(2):
                        if k == 1:
                            pe.wait_ge(z_ready.sem, z_ready.at(b, 1))
                        for h in range(NH):
                            last = pe.matmul(ps[:, 2 * k + h, :], w_bc[:, k, :, :].rearrange("p n e -> p (n e)"),
                                             xc[:, halves(h)], start=True, stop=True)
                        last.then_inc(bc_ps.sem, 1)

                    def replicate(k, bank, rows):
                        g, q, _ = chunk(k)
                        for h in range(NH):
                            last = pe.matmul(ps[:, bank + h, :], pick[:, q, :, :].rearrange("p n e -> p (n e)"),
                                             rows[:, g, halves(h)], start=True, stop=True)
                        return last

                    def fold_round(q):
                        pe.wait_ge(read_out.sem, read_out.at(b, NG * (q + 1)))
                        for h in range(NH):
                            for g in range(NG):
                                k = NG * q + g
                                last = pe.matmul(ps[GW * g:GW * (g + 1), 6 + h, :], fold[:, q, :],
                                                 read[:, k % (2 * NG), halves(h)], start=(q == 0), stop=(q == JG - 1))
                        last.then_inc(folded.sem, 1)

                    pe.wait_ge(dt_rows_in.sem, dt_rows_in.at(b, 16 * 3 * NG))
                    for k in range(NJ):
                        if k == 0:
                            pe.wait_ge(b_copied.sem, b_copied.at(b, 1))
                        elif k == 1:
                            pe.wait_ge(relued.sem, relued.at(b, 1))
                        else:
                            pe.wait_ge(decayed.sem, decayed.at(b, k - 1))
                        replicate(k, dt_bank(k), dt_rows).then_inc(dt_rep.sem, 1)
                        if k == 0:
                            pe.wait_ge(u_rows_in.sem, u_rows_in.at(b, 16 * 3 * NG))
                            pe.wait_ge(c_copied.sem, c_copied.at(b, 1))
                        else:
                            pe.wait_ge(driven.sem, driven.at(b, k))
                        replicate(k, 2, u_rows).then_inc(u_rep.sem, 1)
                        if k >= NG + 1 and k % NG == 1:
                            fold_round(k // NG - 1)
                    fold_round(JG - 1)

                    pe.wait_ge(y_ready.sem, y_ready.at(b, 1))
                    for h in range(NH):
                        last = pe.matmul(ps[0:C, h, :], w_out[:, :], y[:, halves(h)], start=True, stop=True)
                    last.then_inc(out_ps.sem, 1)
                    pe.wait_ge(gn_chain.sem, gn_chain.at(b, 4))
                    hold(pe, "pe")
                    pe.matmul(ps[0:C, 2, 0:2], group_mean[:, :, :].rearrange("p g c -> p (g c)"), gn_mv[:, :],
                              start=True, stop=True).then_inc(gn_ps.sem, 1)

                    def to_tokens(src, dst):
                        for i in range(TB):
                            last = pe.transpose(dst[:, i * C:(i + 1) * C], src[:, tokens(i)], ident[0:C, 0:C])
                        return last

                    def to_channels(src, dst):
                        for i in range(TB):
                            last = pe.transpose(dst[0:C, tokens(i)], src[:, i, :], ident[:, :])
                        return last
                    pe.wait_ge(x1_ready.sem, x1_ready.at(b, 1))
                    hold(pe, "pe")
                    to_tokens(x1, banks(3)).then_inc(t1_ps.sem, 1)
                    pe.wait_ge(xn_ready.sem, xn_ready.at(b, 1))
                    hold(pe, "pe")
                    to_channels(xn, banks(4, 2)).then_inc(xnt_ps.sem, 1)

                    pe.wait_ge(xnt_copied.sem, xnt_copied.at(b, 1))
                    for h in range(NH):
                        last = pe.matmul(ps[:, h, :], w_qk[:, :], xn_t[:, halves(h)], start=True, stop=True)
                    last.then_inc(qk_ps.sem, 1)
                    for i in range(TB):
                        last = pe.matmul(ps[:, 2, i * C:(i + 1) * C], xn_t[:, tokens(i)], w_v[:, :],
                                         start=True, stop=True)
                    last.then_inc(v_ps.sem, 1)

                    pe.wait_ge(stacks_in.sem, stacks_in.at(b, 16 * 18))
                    pe.wait_ge(v_copied.sem, v_copied.at(b, 1))
                    for s, (i, h0, nh) in enumerate(SCORE_STEPS):
                        if s >= 2:
                            pe.wait_ge(row_maxed.sem, row_maxed.at(b, s - 1))
                        per_head = BANK // BANK if nh == 4 else 2
                        for hh in range(nh):
                            bank = 4 * (s % 2) + hh * per_head
                            for h in range(i // QB + 1):
                                diagonal = h == i // QB
                                w = P * (i % QB + 1) if diagonal else BANK
                                last = pe.matmul(ps[:, bank + h, 0:w], q_stack[0:9 * DH, h0 + hh, tokens(i)],
                                                 k_stack[0:9 * DH, h0 + hh, h * BANK:h * BANK + w],
                                                 start=True, stop=not diagonal)
                                if diagonal:
                                    last = pe.matmul(ps[:, bank + h, w - P:w], ident_bf[:, :], mask_q[:, :],
                                                     start=False, stop=True)
                        last.then_inc(scores_ps.sem, 1)
                    pe.wait_ge(max_parts_ready.sem, max_parts_ready.at(b, 1))
                    for i in range(TB):
                        last = pe.transpose(banks(0).bitcast(BF16)[0:3 * H, tokens(i)],
                                            max_parts[:, i, :, :].rearrange("p r h -> p (r h)"), ident_bf[:, :])
                    last.then_inc(max_t_ps.sem, 1)

                    def add_values(s):
                        n, quad, half, j = KEY_STEPS[s]
                        lo = max(0, j * P - half * BANK)
                        pe.wait_ge(exped.sem, exped.at(b, 2 * s + 2))
                        if n >= 2 and j == 0:
                            pe.wait_ge(acc_copied.sem, acc_copied.at(b, n - 1))
                        for hq in range(QUAD):
                            last = pe.matmul(ps[GW * hq:GW * (hq + 1), 6 + n % 2, lo:BANK],
                                             v_aug[:, j, quad * QUAD + hq, :],
                                             probs[:, (2 * s + hq // 2) % 4, hq % 2, 0:BANK - lo],
                                             start=(j == 0), stop=(j == QB * (half + 1) - 1))
                        last.then_inc(values_added.sem, 1)

                    def heads_to_tokens(n):
                        pe.wait_ge(acc_copied.sem, acc_copied.at(b, n + 1))
                        if n >= 2:
                            pe.wait_ge(attn_ready.sem, attn_ready.at(b, n - 1))
                        for i in range(QB):
                            last = pe.transpose(ps[:, 4 + n % 2, tokens(i)], acc_sb[:, n % 2, tokens(i)], ident[:, :])
                        last.then_inc(heads_t_ps.sem, 1)

                    pe.wait_ge(max_in.sem, max_in.at(b, 16))
                    for s, (n, quad, half, j) in enumerate(KEY_STEPS):
                        lo = max(half * BANK, j * P)
                        w = (half + 1) * BANK - lo
                        for pair in range(2):
                            m = 2 * s + pair
                            if m >= 2:
                                pe.wait_ge(exped.sem, exped.at(b, m - 1))
                            for hh in range(2):
                                head = quad * QUAD + 2 * pair + hh
                                bank = 2 * (m % 2) + hh
                                diagonal = lo == j * P
                                last = pe.matmul(ps[:, bank, 0:w], k_stack[0:KQ, head, tokens(j)],
                                                 q_stack[0:KQ, head, lo:lo + w], start=True, stop=not diagonal)
                                if diagonal:
                                    last = pe.matmul(ps[:, bank, 0:P], ident_bf[:, :], mask_k[:, :],
                                                     start=False, stop=True)
                            last.then_inc(weights_ps.sem, 1)
                        if s > 0:
                            add_values(s - 1)
                        if n > 0 and s == LAST_STEP[n - 1] + 3:
                            heads_to_tokens(n - 1)
                    add_values(len(KEY_STEPS) - 1)
                    heads_to_tokens(len(GROUPS) - 1)

                    pe.wait_ge(attn_ready.sem, attn_ready.at(b, len(GROUPS)))
                    hold(pe, "pe")
                    to_channels(attn, banks(0, 2)).then_inc(attn_t_ps.sem, 1)
                    pe.wait_ge(attn_t_copied.sem, attn_t_copied.at(b, 1))
                    for i in range(TB):
                        last = pe.matmul(ps[:, 2, i * C:(i + 1) * C], attn_t[:, tokens(i)], w_o[:, :],
                                         start=True, stop=True)
                    last.then_inc(proj_ps.sem, 1)
                    pe.wait_ge(xn_ready.sem, xn_ready.at(b, 2))
                    hold(pe, "pe")
                    to_channels(xn, banks(3, 2)).then_inc(xnt_ps.sem, 1)

                    pe.wait_ge(xnt_copied.sem, xnt_copied.at(b, 2))
                    for i in range(TB):
                        last = pe.matmul(ps[:, 5, i * E:(i + 1) * E], xn_t[:, tokens(i)], w_router[:, :],
                                         start=True, stop=True)
                    last.then_inc(router_ps.sem, 1)
                    for i in range(TB):
                        if i >= 2:
                            pe.wait_ge(weighted.sem, weighted.at(b, i - 1))
                        pe.matmul(ps[:, 6 + i % 2, :], xn_t[:, tokens(i)], w_expert[:, :, :].rearrange("p e c -> p (e c)"),
                                  start=True, stop=True).then_inc(expert_ps.sem, 1)
                    pe.wait_ge(x2_ready.sem, x2_ready.at(b, 1))
                    hold(pe, "pe")
                    to_channels(moe_out, banks(0, 2)).then_inc(x_out_ps.sem, 1)


_INS = ["x", "L0_conv_W_in", "L0_conv_conv_w", "L0_conv_conv_b", "L0_conv_W_x", "L0_conv_W_dt", "L0_conv_b_dt",
        "L0_conv_A_log", "L0_conv_D", "L0_conv_W_out", "L0_conv_gn_gamma", "L0_conv_gn_beta", "L1_attn_w_attn",
        "L1_attn_w_proj", "L1_ffn_router_w", "L1_ffn_router_b", "L1_ffn_expert_w", "L1_ffn_expert_b"]


def kernel(**inputs):
    import numpy as np
    import concourse.bacc as bacc
    from concourse.bass_utils import run_bass_kernel_spmd

    nc = bacc.Bacc("TRN2", target_bir_lowering=False, num_devices=1)
    arrays, args = {}, []
    for name in _INS:
        a = np.ascontiguousarray(inputs[name])
        arrays[f"in_{name}"] = a
        args.append(nc.dram_tensor(f"in_{name}", a.shape, mybir.dt.from_np(a.dtype), kind="ExternalInput").ap())
    out = nc.dram_tensor("out", inputs["x"].shape, F32, kind="ExternalOutput").ap()
    mamba_attention_moe(nc, *args, out)
    r = run_bass_kernel_spmd(nc, [arrays], core_ids=[0])
    return r.results[0]["out"]
```

```python
from contextlib import ExitStack

import concourse.bass as bass
from concourse import mybir

F32 = mybir.dt.float32
BF16 = mybir.dt.bfloat16
ALU = mybir.AluOpType
ACT = mybir.ActivationFunctionType
AX = mybir.AxisListType

P = 128
BANK = 512
MASKED = -1e30
GN_EPS = 1e-5
LN_EPS = 1e-5


class Batch:

    def __init__(self, register, offset):
        self.register = register
        self.offset = offset
        self.number = offset if register is None else register + offset if offset else register
        self.is_first = register is None and offset == 0


class Signal:

    def __init__(self, ctx, nc, name, per, base=0):
        self.sem = ctx.enter_context(nc.semaphore(name))
        self.per = per
        self.base = base

    def at(self, batch, count):
        constant = self.base + batch.offset * self.per + count
        return constant if batch.register is None else batch.register * self.per + constant


def mamba_attention_moe(nc, x, W_in, conv_w, conv_b, W_x, W_dt, b_dt, A_log, D, W_out, gn_gamma, gn_beta,
                        w_attn, w_proj, router_w, router_b, expert_w, expert_b, out):
    B, C, HH, WW = x.shape
    T = HH * WW
    DI = W_in.shape[1] // 2
    R = W_dt.shape[0]
    NS = (W_x.shape[1] - R) // 2
    E = router_w.shape[1]
    H = 8
    DH = C // H
    G = 4
    CG = C // G
    TB = T // P
    NH = T // BANK
    QB = BANK // P
    CH = P // NS
    NJ = DI // CH
    NG = 4
    JG = NJ // NG
    GW = P // NG
    SCALE = float(DH) ** -0.5
    K1 = C + 32
    KQ = 9 * DH + 3
    QUAD = 4
    assert DI == P and NS * CH == P and T == NH * BANK

    xr = x.rearrange("b c h w -> b c (h w)")
    outr = out.rearrange("b c h w -> b c (h w)")
    qk_parts_dram = nc.dram_tensor("qk_parts_dram", (3, P, T), BF16, kind="Internal").ap()
    max_parts_dram = nc.dram_tensor("max_parts_dram", (3 * H, T), BF16, kind="Internal").ap()

    with ExitStack() as ctx:
        def sb(name, shape, dt=F32):
            return ctx.enter_context(nc.sbuf_tensor(name, shape, dt))

        ps = ctx.enter_context(nc.psum_tensor("ps", [P, 8, BANK], F32))

        def banks(n, k=1):
            return ps[:, n:n + k, :].rearrange("p a b -> p (a b)")

        w_conv = sb("w_conv", [P, DI])
        w_z = sb("w_z", [P, DI])
        conv_rows = sb("conv_rows", [P, 2 * DI])
        conv_bias = sb("conv_bias", [P, 1])
        w_x = sb("w_x", [P, R + 2 * NS])
        w_x_dt_t = sb("w_x_dt_t", [R, P])
        w_dt = sb("w_dt", [R, DI])
        w_dt_full = sb("w_dt_full", [P, DI])
        dt_bias = sb("dt_bias", [P, 1])
        w_bc = sb("w_bc", [P, 2, NS, CH])
        a_scale = sb("a_scale", [P, NJ])
        d_skip = sb("d_skip", [P, 1])
        w_out = sb("w_out", [P, C])
        gn_gamma_half = sb("gn_gamma_half", [C, 1])
        gn_beta_half = sb("gn_beta_half", [C, 1])
        group_mean = sb("group_mean", [C, G, CG])
        w_qk = sb("w_qk", [K1, 2 * C])
        w_v = sb("w_v", [K1, C])
        w_o = sb("w_o", [C, C])
        w_router = sb("w_router", [K1, E])
        w_expert = sb("w_expert", [K1, E, C])
        ident = sb("ident", [P, P])
        ident_bf = sb("ident_bf", [P, P], BF16)
        mask_q = sb("mask_q", [P, P], BF16)
        mask_k = sb("mask_k", [P, P], BF16)
        pick = sb("pick", [96, JG, NS, CH], BF16)
        fold = sb("fold", [P, JG, GW])
        state_sum = sb("state_sum", [P, CH])
        minus_half = sb("minus_half", [P, TB])
        expert_start = sb("expert_start", [P, TB, E])

        xs = sb("xs", [P, T])
        xc = sb("xc", [P, T])
        z_gate = sb("z_gate", [P, T])
        b_rep = sb("b_rep", [P, T])
        c_rep = sb("c_rep", [P, T])
        dt_rows = sb("dt_rows", [96, NG, T], BF16)
        u_rows = sb("u_rows", [96, NG, T], BF16)
        decay = sb("decay", [P, 2, T])
        drive = sb("drive", [P, 3, T])
        state = sb("state", [P, 2, T])
        read = sb("read", [P, 2 * NG, T])
        rest = decay
        z_tanh = decay[:, 0, :]
        relu = drive[:, 0, :]
        silu_h, silu_t = drive[:, 1, :], drive[:, 2, :]
        gn_h, gn_t = drive[0:C, 1, :], drive[0:C, 2, :]
        softplus_a, softplus_b = state[:, 0, :], state[:, 1, :]
        y_skip, y = state[:, 0, :], state[:, 1, :]
        dt, u = read[:, 0, :], read[:, 1, :]
        x1 = read[0:C, 2, :]
        part = [read[:, 4 + i // 2, (i % 2) * (T // 2):(i % 2 + 1) * (T // 2)].bitcast(BF16) for i in range(6)]
        gn_stats = sb("gn_stats", [C, 2, 6])
        gn_mv = sb("gn_mv", [C, 2])
        gn_group = sb("gn_group", [C, 2])
        gn_v = sb("gn_v", [C, 5])
        t1 = sb("t1", [P, 2, TB, C])
        t2 = sb("t2", [P, TB, C])
        xcen = sb("xcen", [P, 2, TB, C])
        xsq = sb("xsq", [P, 2, TB, C])
        xn = sb("xn", [P, 2, TB, C])
        ln_s = sb("ln_s", [P, 2, 5, TB])
        xn_t = sb("xn_t", [K1, 2, T])
        v_aug = sb("v_aug", [P, TB, H, GW])
        q_stack = sb("q_stack", [P, H, T], BF16)
        k_stack = sb("k_stack", [P, H, T], BF16)
        row_max = sb("row_max", [P, TB, H])
        max_rest = sb("max_rest", [P, TB, H])
        max_parts = sb("max_parts", [P, TB, 3, H], BF16)
        max_t = sb("max_t", [3 * H, T], BF16)
        probs = sb("probs", [P, 2 * QUAD, BANK])
        acc_sb = sb("acc_sb", [P, 2, BANK])
        den = sb("den", [P, TB, H])
        attn = sb("attn", [P, TB, C])
        attn_t = xn_t[0:C, 1, :]
        moe_out = sb("moe_out", [P, TB, C])
        gate_m = sb("gate_m", [P, 4, TB])
        gate_e = sb("gate_e", [P, 10, TB, E])
        moe = sb("moe", [P, 2, E, C])
        x_out = moe[0:C, :, :, :].rearrange("p a e c -> p (a e c)")

        weights_in = ctx.enter_context(nc.semaphore("weights_in"))
        masks_built = ctx.enter_context(nc.semaphore("masks_built"))
        dve_setup = ctx.enter_context(nc.semaphore("dve_setup"))
        pe_setup = ctx.enter_context(nc.semaphore("pe_setup"))
        act_setup = ctx.enter_context(nc.semaphore("act_setup"))
        pool_chain = ctx.enter_context(nc.semaphore("pool_chain"))
        LOADS = 20 + NS
        setup_dmas = [0]

        with nc.Block() as block:
            @block.sync
            def _(sp):
                sp.wait_ge(dve_setup, 5)
                def load(dst, src, strided=False):
                    sp.dma_start(dst, src, allow_slow_non_contiguous=strided).then_inc(weights_in, 16)
                    setup_dmas[0] += 1
                load(w_conv[0:C, :], W_in[:, 0:DI])
                load(w_conv[C:2 * C, :], W_in[:, 0:DI])
                load(w_z[0:C, :], W_in[:, DI:2 * DI])
                load(conv_rows[:, :], conv_w.rearrange("(a d) k -> a (d k)", a=1).to_broadcast([P, 2 * DI]))
                load(conv_bias[:, :], conv_b.rearrange("(d a) -> d a", a=1))
                load(w_x[:, :], W_x[:, :])
                load(w_x_dt_t[:, :], W_x[:, 0:R].rearrange("d r -> r d"), strided=True)
                load(w_dt[:, :], W_dt[:, :])
                load(dt_bias[:, :], b_dt.rearrange("(d a) -> d a", a=1))
                for n in range(NS):
                    load(a_scale[n * CH:(n + 1) * CH, :], A_log[:, n].rearrange("(j e) -> e j", e=CH), strided=True)
                load(d_skip[:, :], D.rearrange("(d a) -> d a", a=1))
                load(w_out[:, :], W_out[:, :])
                load(gn_gamma_half[:, :], gn_gamma.rearrange("(d a) -> d a", a=1))
                load(gn_beta_half[:, :], gn_beta.rearrange("(d a) -> d a", a=1))
                load(w_qk[0:C, :], w_attn[:, 0:2 * C])
                load(w_v[0:C, :], w_attn[:, 2 * C:3 * C])
                load(w_o[:, :], w_proj[:, :])
                load(w_router[0:C, :], router_w[:, :])
                load(w_router[C:C + 1, :], router_b.rearrange("(a e) -> a e", a=1))
                load(w_expert[0:C, :, :], expert_w.rearrange("e d c -> d e c"))
                load(w_expert[C:C + 1, :, :], expert_b.rearrange("(a e) c -> a e c", a=1))
                assert setup_dmas[0] == LOADS

            @block.vector
            def _(dve):
                dve.memset(w_z[C:P, :], 0.0).then_inc(dve_setup, 1)
                dve.memset(w_qk[C:K1, :], 0.0).then_inc(dve_setup, 1)
                dve.memset(w_v[C:K1, :], 0.0).then_inc(dve_setup, 1)
                dve.memset(w_router[C:K1, :], 0.0).then_inc(dve_setup, 1)
                dve.memset(w_expert[C:K1, :, :], 0.0).then_inc(dve_setup, 1)
                dve.memset(xn_t[C:K1, :, :], 1.0).then_inc(dve_setup, 1)
                dve.memset(xs[C:2 * C, 0:1], 0.0).then_inc(dve_setup, 1)
                dve.memset(v_aug[:, :, :, DH:GW], 1.0).then_inc(dve_setup, 1)
                dve.memset(k_stack[64:96, :, :], 1.0).then_inc(dve_setup, 1)
                dve.memset(minus_half[:, :], -0.5).then_inc(dve_setup, 1)
                dve.memset(expert_start[:, :, :], 1.0).then_inc(dve_setup, 1)
                dve.wait_ge(dve_setup, 11)
                dve.memset(expert_start[:, :, 0:1], 0.0).then_inc(dve_setup, 1)
                dve.wait_ge(weights_in, 16 * LOADS)
                conv_k = conv_rows[:, :].rearrange("p (d k) -> p k d", k=2)
                for rows, tap in ((slice(0, C), 1), (slice(C, 2 * C), 0)):
                    dve.scalar_tensor_tensor(w_conv[rows, :], w_conv[rows, :], 0.5, conv_k[rows, tap, :],
                                             ALU.mult, ALU.mult).then_inc(dve_setup, 1)
                for t in (w_z[0:C, :], conv_bias[:, :], gn_gamma_half[:, :], gn_beta_half[:, :]):
                    dve.tensor_scalar(t, t, 0.5, None, ALU.mult).then_inc(dve_setup, 1)
                for k in range(2):
                    cols = w_x[:, R + k * NS:R + (k + 1) * NS]
                    dve.tensor_copy(w_bc[:, k, :, :], cols.unsqueeze(2).to_broadcast([P, NS, CH]))\
                       .then_inc(dve_setup, 1)
                dve.wait_ge(pe_setup, 1)
                dve.tensor_copy(w_dt_full[:, :], ps[:, 0, 0:DI]).then_inc(dve_setup, 1)
                dve.wait_ge(act_setup, 1)
                dve.tensor_scalar(a_scale[:, :], a_scale[:, :], -1.0, None, ALU.mult).then_inc(dve_setup, 1)
                dve.wait_ge(masks_built, 1)
                for q in range(JG):
                    dve.tensor_copy(fold[:, q, q * CH:(q + 1) * CH], state_sum[:, :]).then_inc(dve_setup, 1)

            @block.scalar
            def _(act):
                act.wait_ge(weights_in, 16 * LOADS)
                act.activation(a_scale[:, :], a_scale[:, :], ACT.Exp).then_inc(act_setup, 1)

            @block.tensor
            def _(pe):
                pe.wait_ge(weights_in, 16 * LOADS)
                pe.matmul(ps[:, 0, 0:DI], w_x_dt_t[:, :], w_dt[:, :], start=True, stop=True).then_inc(pe_setup, 1)

            @block.gpsimd
            def _(pool):
                step = [0]

                def then(ins):
                    ins.then_inc(pool_chain, 1)
                    step[0] += 1
                    pool.wait_ge(pool_chain, step[0])

                def diagonal(tile, pattern, base, fill=1.0, op=ALU.not_equal, mult=1):
                    then(pool.affine_select(out=tile, in_=tile, pattern=pattern, compare_op=op, fill=fill,
                                            base=base, channel_multiplier=mult))
                then(pool.memset(state_sum[:, :], 0.0))
                then(pool.memset(fold[:, :, :], 0.0))
                for n in range(NS):
                    diagonal(state_sum[:, :], [[-1, CH]], -CH * n)
                pool.memset(ident[:, :], 0.0).then_inc(masks_built, 1)
                then(pool.memset(ident_bf[:, :], 0.0))
                pool.wait_ge(masks_built, 1)
                diagonal(ident[:, :], [[-1, P]], 0)
                diagonal(ident_bf[:, :], [[-1, P]], 0)
                then(pool.memset(pick[:, :, :, :], 0.0))
                for part_row in range(3):
                    diagonal(pick[:, :, :, :], [[-CH, JG], [0, NS], [-1, CH]], -32 * part_row)
                then(pool.memset(mask_q[:, :], 0.0))
                diagonal(mask_q[:, :], [[-1, P]], 0, MASKED, ALU.is_ge)
                then(pool.memset(mask_k[:, :], 0.0))
                diagonal(mask_k[:, :], [[1, P]], 0, MASKED, ALU.is_ge, -1)
                then(pool.memset(group_mean[:, :, :], 1.0 / CG))
                diagonal(group_mean[:, :, :], [[-CG, G], [0, CG]], 0, 0.0, ALU.is_ge)
                diagonal(group_mean[:, :, :], [[CG, G], [0, CG]], CG - 1, 0.0, ALU.is_ge, -1)

        def signal(name, per, base=0):
            return Signal(ctx, nc, name, per, base)

        SCORE_STEPS = [(i, h, 2 if i < QB else 1) for i in range(TB) for h in range(0, H, 2 if i < QB else 1)]
        NSCORE = len(SCORE_STEPS)
        GROUPS = [(quad, half) for quad in range(H // QUAD) for half in range(NH)]
        KEY_STEPS = [(n, quad, half, j) for n, (quad, half) in enumerate(GROUPS) for j in range(QB * (half + 1))]
        NKEY = len(KEY_STEPS)
        LAST_STEP = [max(s for s, ks in enumerate(KEY_STEPS) if ks[0] == n) for n in range(len(GROUPS))]
        LAG = 2
        UNITS = 2 * NJ
        AHEAD = UNITS - NKEY
        ACC = 4
        RING = (5, 6, 7)

        ring_items = []
        for s in range(NKEY):
            ring_items += [("scores", QUAD * s + hq) for hq in range(QUAD)]
            ring_items += [("heads", n) for n, last in enumerate(LAST_STEP[:-1]) if s == last + LAG]
        ring_items.append(("heads", len(GROUPS) - 1))
        ring_place = {item: r for r, item in enumerate(ring_items)}

        def ring_bank(item):
            return RING[ring_place[item] % len(RING)]

        x_in = signal("x_in", 32)
        dt_rows_in = signal("dt_rows_in", 16 * 3 * NG)
        u_rows_in = signal("u_rows_in", 16 * 3 * NG)
        qk_parts_out = signal("qk_parts_out", 16 * 3)
        stacks_in = signal("stacks_in", 16 * 18)
        max_t_out = signal("max_t_out", 16)
        max_in = signal("max_in", 16)
        out_stored = signal("out_stored", 16, base=1)
        conv_ps = signal("conv_ps", 1)
        z_ps = signal("z_ps", 1)
        dt_ps = signal("dt_ps", 1)
        bc_ps = signal("bc_ps", 2)
        dt_rep = signal("dt_rep", UNITS)
        u_rep = signal("u_rep", UNITS)
        folded = signal("folded", JG)
        out_ps = signal("out_ps", 1)
        gn_ps = signal("gn_ps", 1)
        t1_ps = signal("t1_ps", 1)
        xnt_ps = [signal("xnt_ps_1", 1), signal("xnt_ps_2", 1)]
        qk_ps = signal("qk_ps", 1)
        v_ps = signal("v_ps", 1)
        scores_ps = signal("scores_ps", NSCORE)
        max_t_ps = signal("max_t_ps", 1)
        weights_ps = signal("weights_ps", QUAD * NKEY)
        values_added = signal("values_added", NKEY)
        heads_t_ps = signal("heads_t_ps", len(GROUPS))
        attn_t_ps = signal("attn_t_ps", 1)
        proj_ps = signal("proj_ps", 1)
        router_ps = signal("router_ps", 1)
        expert_ps = signal("expert_ps", TB)
        x_out_ps = signal("x_out_ps", 1)
        silu_parts = signal("silu_parts", 2)
        z_tanh_done = signal("z_tanh_done", 1)
        softplus_steps = signal("softplus_steps", 3)
        b_copied = signal("b_copied", 1)
        c_copied = signal("c_copied", 1)
        high_parts = signal("high_parts", 3)
        mid_parts = signal("mid_parts", 3)
        decayed = signal("decayed", UNITS)
        gn_parts = signal("gn_parts", 2)
        t1_copied = signal("t1_copied", 1)
        t1_taken = signal("t1_taken", 1)
        squared = [signal("squared_1", 1), signal("squared_2", 1)]
        xnt_copied = [signal("xnt_copied_1", 1), signal("xnt_copied_2", 1)]
        exped = signal("exped", QUAD * NKEY)
        acc_copied = signal("acc_copied", len(GROUPS))
        attn_t_copied = signal("attn_t_copied", 1)
        gate_exped = signal("gate_exped", 1)
        x_out_copied = signal("x_out_copied", 1, base=1)
        xc_ready = signal("xc_ready", 1)
        z_ready = signal("z_ready", 1)
        relued = signal("relued", 1)
        dt_ready = signal("dt_ready", 1)
        driven = signal("driven", UNITS)
        scanned = signal("scanned", NJ)
        skipped = signal("skipped", 1)
        y_ready = signal("y_ready", 1)
        gn_chain = signal("gn_chain", 9)
        gn_bias = signal("gn_bias", 1)
        gn_gated = signal("gn_gated", 1)
        x1_ready = signal("x1_ready", 1)
        ln_chain = [signal("ln_chain_1", 3), signal("ln_chain_2", 3)]
        centred = [signal("centred_1", 1), signal("centred_2", 1)]
        ln_var = [signal("ln_var_1", 1), signal("ln_var_2", 1)]
        xn_ready = [signal("xn_ready_1", 1), signal("xn_ready_2", 1)]
        qk_rest = signal("qk_rest", 1)
        qk_low = signal("qk_low", 1)
        v_copied = signal("v_copied", 1)
        row_maxed = signal("row_maxed", NSCORE)
        max_chain = signal("max_chain", 3)
        max_parts_ready = signal("max_parts_ready", 1)
        max_t_copied = signal("max_t_copied", 1)
        den_ready = signal("den_ready", len(GROUPS))
        attn_ready = signal("attn_ready", len(GROUPS))
        t2_ready = signal("t2_ready", 1)
        gate_chain = signal("gate_chain", 15)
        gate_centred = signal("gate_centred", 1)
        weighted = signal("weighted", TB)
        combined = signal("combined", TB)
        x2_ready = signal("x2_ready", 1)
        u_ready = signal("u_ready", 1)
        rests = signal("rests", 2)
        low_parts = signal("low_parts", 2)
        read_out = signal("read_out", NJ)
        gn_rstd = signal("gn_rstd", 1)
        ln_rstd = [signal("ln_rstd_1", 1), signal("ln_rstd_2", 1)]

        held = {name: ctx.enter_context(nc.semaphore(f"held_{name}")) for name in ("pe", "dve")}

        def hold(engine, name):
            engine.sem_inc(held[name])

        def chunk(k):
            g, q = k % NG, k // NG
            return g, q, JG * g + q

        def halves(n):
            return slice(n * BANK, (n + 1) * BANK)

        def tokens(i):
            return slice(i * P, (i + 1) * P)

        def tokens_by_channels(bank):
            return banks(bank).rearrange("p (i c) -> p i c", c=C)

        def both_streams(engine, program):
            program(Batch(None, 0), None)
            with engine.Fori(0, B - 1) as i:
                program(Batch(i, 1), Batch(i, 0))
            program(None, Batch(None, B - 1))

        with nc.Block() as block:
            @block.sync
            def _(sp):
                def program(a, b):
                    if a:
                        if not a.is_first:
                            sp.wait_ge(x1_ready.sem, x1_ready.at(a, 0))
                        sp.dma_start(xs[0:C, :], xr[a.number, :, :]).then_inc(x_in.sem, 16)
                        sp.dma_start(xs[C:2 * C, 1:T], xr[a.number, :, 0:T - 1]).then_inc(x_in.sem, 16)
                        for rows, arrived, first, n in ((dt_rows, dt_rows_in, 0, 0), (u_rows, u_rows_in, 3, 1)):
                            for p, parts in enumerate((high_parts, mid_parts, low_parts)):
                                sp.wait_ge(parts.sem, parts.at(a, n + 1))
                                for g in range(NG):
                                    sp.dma_start(rows[32 * p:32 * (p + 1), g, :],
                                                 part[first + p][GW * g:GW * (g + 1), :]).then_inc(arrived.sem, 16)
                    if b:
                        sp.wait_ge(max_t_copied.sem, max_t_copied.at(b, 1))
                        sp.dma_start(max_parts_dram[:, :], max_t[:, :]).then_inc(max_t_out.sem, 16)
                        sp.wait_ge(max_t_out.sem, max_t_out.at(b, 16))
                        sp.dma_start(q_stack[KQ - 3:KQ, :, :],
                                     max_parts_dram.rearrange("(r h) t -> r h t", h=H)).then_inc(max_in.sem, 16)
                    if a:
                        for p, (parts, count) in enumerate(((high_parts, 3), (mid_parts, 3), (qk_low, 1))):
                            sp.wait_ge(parts.sem, parts.at(a, count))
                            sp.dma_start(qk_parts_dram[p, :, :], part[p]).then_inc(qk_parts_out.sem, 16)
                        sp.wait_ge(qk_parts_out.sem, qk_parts_out.at(a, 48))
                        if b:
                            sp.wait_ge(weights_ps.sem, weights_ps.at(b, QUAD * NKEY))
                        for p in range(3):
                            for r in range(3):
                                rows = slice(DH * (3 * p + r), DH * (3 * p + r + 1))
                                sp.dma_start(q_stack[rows, :, :],
                                             qk_parts_dram[p, 0:C, :].rearrange("(h d) t -> d h t", d=DH))\
                                  .then_inc(stacks_in.sem, 16)
                                sp.dma_start(k_stack[rows, :, :],
                                             qk_parts_dram[r, C:2 * C, :].rearrange("(h d) t -> d h t", d=DH))\
                                  .then_inc(stacks_in.sem, 16)
                    if b:
                        sp.wait_ge(x_out_copied.sem, x_out_copied.at(b, 1))
                        sp.dma_start(outr[b.number, :, :], x_out).then_inc(out_stored.sem, 16)
                both_streams(sp, program)
                sp.wait_ge(out_stored.sem, out_stored.at(Batch(None, B), 0))

            @block.gpsimd
            def _(pool):
                for across_batches in (out_stored, x_out_copied):
                    pool.sem_inc(across_batches.sem, across_batches.base)

                def program(a, b):
                    if a:
                        pool.wait_ge(dt_ready.sem, dt_ready.at(a, 1))
                        pool.tensor_tensor(u, dt, xc[:, :], ALU.mult).then_inc(u_ready.sem, 1)
                        for n, src in enumerate((dt, u)):
                            pool.wait_ge(high_parts.sem, high_parts.at(a, n + 1))
                            pool.tensor_tensor(rest[:, n, :], src, part[3 * n], ALU.subtract).then_inc(rests.sem, 1)
                        for n in range(2):
                            pool.wait_ge(mid_parts.sem, mid_parts.at(a, n + 1))
                            pool.tensor_tensor(part[3 * n + 2], rest[:, n, :], part[3 * n + 1], ALU.subtract)\
                                .then_inc(low_parts.sem, 1)
                        pool.wait_ge(c_copied.sem, c_copied.at(a, 1))
                        for k in range(NJ):
                            pool.wait_ge(scanned.sem, scanned.at(a, k + 1))
                            if k >= 2 * NG:
                                pool.wait_ge(folded.sem, folded.at(a, k // NG - 1))
                            pool.tensor_tensor(read[:, k % (2 * NG), :], state[:, k % 2, :], c_rep[:, :], ALU.mult)\
                                .then_inc(read_out.sem, 1)
                        pool.wait_ge(gn_chain.sem, gn_chain.at(a, 7))
                        pool.tensor_tensor(gn_v[:, 1:2], gn_v[:, 0:1], minus_half[0:C, 0:1], ALU.pow)\
                            .then_inc(gn_rstd.sem, 1)
                    for n, batch in ((1, b), (0, a)):
                        if batch:
                            pool.wait_ge(ln_var[n].sem, ln_var[n].at(batch, 1))
                            pool.tensor_tensor(ln_s[:, n, 4, :], ln_s[:, n, 3, :], minus_half[:, :], ALU.pow)\
                                .then_inc(ln_rstd[n].sem, 1)
                both_streams(pool, program)

            @block.scalar
            def _(act):
                def program(a, b):
                    if b:
                        act.wait_ge(t1_copied.sem, t1_copied.at(b, 1))
                        act.copy(t1[:, 1, :, :], t1[:, 0, :, :]).then_inc(t1_taken.sem, 1)
                    if a:
                        act.wait_ge(conv_ps.sem, conv_ps.at(a, 1))
                        act.activation(silu_h, banks(0, 2), ACT.Identity, bias=conv_bias[:, :])\
                           .then_inc(silu_parts.sem, 1)
                        act.activation(silu_t, banks(0, 2), ACT.Tanh, bias=conv_bias[:, :])\
                           .then_inc(silu_parts.sem, 1)
                        act.wait_ge(z_ps.sem, z_ps.at(a, 1))
                        act.activation(z_tanh, banks(2, 2), ACT.Tanh).then_inc(z_tanh_done.sem, 1)
                        act.wait_ge(dt_ps.sem, dt_ps.at(a, 1))
                        act.activation(softplus_a, banks(0, 2), ACT.Abs, bias=dt_bias[:, :])\
                           .then_inc(softplus_steps.sem, 1)
                        act.wait_ge(softplus_steps.sem, softplus_steps.at(a, 1))
                        act.activation(softplus_b, softplus_a, ACT.Exp, scale=-1.0).then_inc(softplus_steps.sem, 1)
                        act.wait_ge(softplus_steps.sem, softplus_steps.at(a, 2))
                        act.activation(softplus_a, softplus_b, ACT.Ln, bias=1.0).then_inc(softplus_steps.sem, 1)
                        act.wait_ge(bc_ps.sem, bc_ps.at(a, 1))
                        act.copy(b_rep[:, :], banks(2, 2)).then_inc(b_copied.sem, 1)
                        act.wait_ge(bc_ps.sem, bc_ps.at(a, 2))
                        act.copy(c_rep[:, :], banks(0, 2)).then_inc(c_copied.sem, 1)
                        for n, (src, ready) in enumerate(((dt, dt_ready), (u, u_ready))):
                            act.wait_ge(ready.sem, ready.at(a, 1))
                            act.copy(part[3 * n], src).then_inc(high_parts.sem, 1)
                        for n in range(2):
                            act.wait_ge(rests.sem, rests.at(a, n + 1))
                            act.copy(part[3 * n + 1], rest[:, n, :]).then_inc(mid_parts.sem, 1)

                    def decay_unit(c):
                        k, h = c // 2, c % 2
                        act.wait_ge(dt_rep.sem, dt_rep.at(a, c + 1))
                        if k >= 2:
                            act.wait_ge(scanned.sem, scanned.at(a, k - 1))
                        j = chunk(k)[2]
                        act.activation(decay[:, k % 2, halves(h)], banks(0), ACT.Exp, scale=a_scale[:, j:j + 1])\
                           .then_inc(decayed.sem, 1)

                    def copy_sums(n):
                        act.wait_ge(values_added.sem, values_added.at(b, LAST_STEP[n] + 1))
                        if n >= 2:
                            act.wait_ge(heads_t_ps.sem, heads_t_ps.at(b, n - 1))
                        act.copy(acc_sb[:, n % 2, :], banks(ACC)).then_inc(acc_copied.sem, 1)

                    def softmax_step(s):
                        n, quad, half, j = KEY_STEPS[s]
                        w = BANK - max(0, j * P - half * BANK)
                        for hq in range(QUAD):
                            e = QUAD * s + hq
                            act.wait_ge(weights_ps.sem, weights_ps.at(b, e + 1))
                            if hq == 0 and s >= 2:
                                act.wait_ge(values_added.sem, values_added.at(b, s - 1))
                            act.activation(probs[:, e % (2 * QUAD), 0:w], banks(ring_bank(("scores", e)))[:, 0:w],
                                           ACT.Exp, scale=SCALE).then_inc(exped.sem, 1)
                        if n > 0 and s == LAST_STEP[n - 1] + 1:
                            copy_sums(n - 1)

                    if a:
                        act.wait_ge(low_parts.sem, low_parts.at(a, 2))
                        for c in range(AHEAD):
                            decay_unit(c)
                    for s in range(NKEY):
                        if b:
                            softmax_step(s)
                        if a:
                            decay_unit(AHEAD + s)
                    if b:
                        copy_sums(len(GROUPS) - 1)

                    def square(n, batch):
                        act.wait_ge(centred[n].sem, centred[n].at(batch, 1))
                        act.activation(xsq[:, n, :, :], xcen[:, n, :, :], ACT.Square).then_inc(squared[n].sem, 1)

                    def copy_xn_t(n, batch, bank):
                        act.wait_ge(xnt_ps[n].sem, xnt_ps[n].at(batch, 1))
                        act.copy(xn_t[0:C, n, :], banks(bank, 2)[0:C, :]).then_inc(xnt_copied[n].sem, 1)
                    if b:
                        act.wait_ge(attn_t_ps.sem, attn_t_ps.at(b, 1))
                        act.copy(attn_t, banks(5, 2)[0:C, :]).then_inc(attn_t_copied.sem, 1)
                        square(1, b)
                    if a:
                        act.wait_ge(gn_bias.sem, gn_bias.at(a, 1))
                        act.activation(gn_h, banks(0, 2)[0:C, :], ACT.Identity, bias=gn_v[:, 4:5],
                                       scale=gn_v[:, 2:3]).then_inc(gn_parts.sem, 1)
                        act.activation(gn_t, banks(0, 2)[0:C, :], ACT.Tanh, bias=gn_v[:, 4:5],
                                       scale=gn_v[:, 2:3]).then_inc(gn_parts.sem, 1)
                    if b:
                        copy_xn_t(1, b, 5)
                        act.wait_ge(gate_centred.sem, gate_centred.at(b, 1))
                        act.activation(gate_e[:, 1, :, :], gate_e[:, 0, :, :], ACT.Exp).then_inc(gate_exped.sem, 1)
                    if a:
                        square(0, a)
                        act.copy(t1[:, 0, :, :], tokens_by_channels(3)).then_inc(t1_copied.sem, 1)
                        copy_xn_t(0, a, 0)
                        act.wait_ge(qk_ps.sem, qk_ps.at(a, 1))
                        act.copy(part[0], banks(2, 2)).then_inc(high_parts.sem, 1)
                        act.wait_ge(qk_rest.sem, qk_rest.at(a, 1))
                        act.copy(part[1], rest[:, 0, :]).then_inc(mid_parts.sem, 1)
                    if b:
                        act.wait_ge(x_out_ps.sem, x_out_ps.at(b, 1))
                        act.copy(x_out, banks(4, 2)[0:C, :]).then_inc(x_out_copied.sem, 1)
                both_streams(act, program)

            @block.vector
            def _(dve):
                def program(a, b):
                    def convolved():
                        dve.wait_ge(silu_parts.sem, silu_parts.at(a, 2))
                        dve.scalar_tensor_tensor(xc[:, :], silu_t, 1.0, silu_h, ALU.add, ALU.mult)\
                           .then_inc(xc_ready.sem, 1)

                    def gated():
                        dve.wait_ge(z_tanh_done.sem, z_tanh_done.at(a, 1))
                        dve.scalar_tensor_tensor(z_gate[:, :], z_tanh, 1.0, banks(2, 2), ALU.add, ALU.mult)\
                           .then_inc(z_ready.sem, 1)

                    def rectified():
                        dve.wait_ge(softplus_steps.sem, softplus_steps.at(a, 1))
                        dve.tensor_scalar(relu, banks(0, 2), dt_bias[:, :], 0.0, ALU.add, ALU.max)\
                           .then_inc(relued.sem, 1)

                    def dt_made():
                        dve.wait_ge(softplus_steps.sem, softplus_steps.at(a, 3))
                        dve.wait_ge(relued.sem, relued.at(a, 1))
                        dve.tensor_tensor(dt, relu, softplus_a, ALU.add).then_inc(dt_ready.sem, 1)

                    before_score = {6: convolved, 9: gated, 14: rectified, 20: dt_made}
                    for s, (i, h0, nh) in enumerate(SCORE_STEPS):
                        if a and s in before_score:
                            before_score[s]()
                        if b:
                            dve.wait_ge(scores_ps.sem, scores_ps.at(b, s + 1))
                            scores = banks(4 + 2 * (s % 2), 2).rearrange("p (h k) -> p h k", h=nh)
                            dve.tensor_reduce(row_max[:, i, h0:h0 + nh], scores[:, :, 0:P * (i + 1)], AX.X, ALU.max,
                                              negate=True).then_inc(row_maxed.sem, 1)
                    if b:
                        dve.wait_ge(row_maxed.sem, row_maxed.at(b, NSCORE))
                        dve.tensor_copy(max_parts[:, :, 0, :], row_max[:, :, :]).then_inc(max_chain.sem, 1)
                        dve.wait_ge(max_chain.sem, max_chain.at(b, 1))
                        dve.tensor_tensor(max_rest[:, :, :], row_max[:, :, :], max_parts[:, :, 0, :], ALU.subtract)\
                           .then_inc(max_chain.sem, 1)
                        dve.wait_ge(max_chain.sem, max_chain.at(b, 2))
                        dve.tensor_copy(max_parts[:, :, 1, :], max_rest[:, :, :]).then_inc(max_chain.sem, 1)
                        dve.wait_ge(max_chain.sem, max_chain.at(b, 3))
                        dve.tensor_tensor(max_parts[:, :, 2, :], max_rest[:, :, :], max_parts[:, :, 1, :],
                                          ALU.subtract).then_inc(max_parts_ready.sem, 1)
                        dve.wait_ge(max_t_ps.sem, max_t_ps.at(b, 1))
                        dve.tensor_copy(max_t[:, :], banks(ACC).bitcast(BF16)[0:3 * H, :])\
                           .then_inc(max_t_copied.sem, 1)

                    def scan(k):
                        dve.wait_ge(decayed.sem, decayed.at(a, 2 * k + 2))
                        dve.wait_ge(driven.sem, driven.at(a, 2 * k + 2))
                        if k >= 2:
                            dve.wait_ge(read_out.sem, read_out.at(a, k - 1))
                        dve.tensor_tensor_scan(state[:, k % 2, :], decay[:, k % 2, :], drive[:, k % 3, :], 0.0,
                                               ALU.mult, ALU.add).then_inc(scanned.sem, 1)

                    def drive_unit(c):
                        k, h = c // 2, c % 2
                        dve.wait_ge(u_rep.sem, u_rep.at(a, c + 1))
                        if k >= 3:
                            dve.wait_ge(scanned.sem, scanned.at(a, k - 2))
                        dve.tensor_tensor(drive[:, k % 3, halves(h)], banks(1), b_rep[:, halves(h)], ALU.mult)\
                           .then_inc(driven.sem, 1)
                        if h == 0 and k > 0:
                            scan(k - 1)

                    def divide_heads(n):
                        quad, half = GROUPS[n]
                        dve.wait_ge(heads_t_ps.sem, heads_t_ps.at(b, n + 1))
                        heads = banks(ring_bank(("heads", n))).rearrange("p (i h d) -> p i h d", i=QB, d=GW)
                        blocks, hs = slice(half * QB, (half + 1) * QB), slice(quad * QUAD, (quad + 1) * QUAD)
                        dve.reciprocal(den[:, blocks, hs], heads[:, :, :, DH]).then_inc(den_ready.sem, 1)
                        dve.wait_ge(den_ready.sem, den_ready.at(b, n + 1))
                        out_heads = attn[:, blocks, :].rearrange("p i (h d) -> p i h d", d=DH)[:, :, hs, :]
                        dve.tensor_tensor(out_heads, heads[:, :, :, 0:DH],
                                          den[:, blocks, hs].unsqueeze(3).to_broadcast([P, QB, QUAD, DH]),
                                          ALU.mult).then_inc(attn_ready.sem, 1)
                    if a:
                        dve.wait_ge(b_copied.sem, b_copied.at(a, 1))
                        for c in range(AHEAD):
                            drive_unit(c)
                    for s in range(NKEY):
                        if a:
                            drive_unit(AHEAD + s)
                        n = KEY_STEPS[s][0]
                        if b and n > 0 and s == LAST_STEP[n - 1] + LAG:
                            divide_heads(n - 1)
                    if a:
                        scan(NJ - 1)
                        dve.wait_ge(folded.sem, folded.at(a, JG))
                        dve.scalar_tensor_tensor(y_skip, xc[:, :], d_skip[:, :], banks(2, 2), ALU.mult, ALU.add)\
                           .then_inc(skipped.sem, 1)
                        dve.wait_ge(skipped.sem, skipped.at(a, 1))
                        dve.tensor_tensor(y, y_skip, z_gate[:, :], ALU.mult).then_inc(y_ready.sem, 1)
                    if b:
                        divide_heads(len(GROUPS) - 1)

                    def centre(n, batch, src):
                        dve.tensor_reduce(ln_s[:, n, 0, :], src, AX.X, ALU.add).then_inc(ln_chain[n].sem, 1)
                        dve.wait_ge(ln_chain[n].sem, ln_chain[n].at(batch, 1))
                        dve.tensor_scalar(ln_s[:, n, 1, :], ln_s[:, n, 0, :], 1.0 / C, None, ALU.mult)\
                           .then_inc(ln_chain[n].sem, 1)
                        dve.wait_ge(ln_chain[n].sem, ln_chain[n].at(batch, 2))
                        dve.tensor_tensor(xcen[:, n, :, :], src,
                                          ln_s[:, n, 1, :].unsqueeze(2).to_broadcast([P, TB, C]), ALU.subtract)\
                           .then_inc(centred[n].sem, 1)

                    def variance(n, batch):
                        dve.wait_ge(squared[n].sem, squared[n].at(batch, 1))
                        dve.tensor_reduce(ln_s[:, n, 2, :], xsq[:, n, :, :], AX.X, ALU.add)\
                           .then_inc(ln_chain[n].sem, 1)
                        dve.wait_ge(ln_chain[n].sem, ln_chain[n].at(batch, 3))
                        dve.tensor_scalar(ln_s[:, n, 3, :], ln_s[:, n, 2, :], 1.0 / C, LN_EPS, ALU.mult, ALU.add)\
                           .then_inc(ln_var[n].sem, 1)

                    def scale(n, batch):
                        dve.wait_ge(ln_rstd[n].sem, ln_rstd[n].at(batch, 1))
                        dve.tensor_tensor(xn[:, n, :, :], xcen[:, n, :, :],
                                          ln_s[:, n, 4, :].unsqueeze(2).to_broadcast([P, TB, C]), ALU.mult)\
                           .then_inc(xn_ready[n].sem, 1)

                    if a:
                        dve.wait_ge(out_ps.sem, out_ps.at(a, 1))
                        for h in range(NH):
                            dve.bn_stats(gn_stats[:, h, :], ps[0:C, h, :]).then_inc(gn_chain.sem, 1)
                        dve.wait_ge(gn_chain.sem, gn_chain.at(a, 2))
                        hold(dve, "dve")
                        dve.bn_aggr(gn_mv[:, :], gn_stats[:, :, :]).then_inc(gn_chain.sem, 1)
                        dve.wait_ge(gn_chain.sem, gn_chain.at(a, 3))
                        dve.scalar_tensor_tensor(gn_mv[:, 1:2], gn_mv[:, 0:1], gn_mv[:, 0:1], gn_mv[:, 1:2],
                                                 ALU.mult, ALU.add).then_inc(gn_chain.sem, 1)
                    if b:
                        dve.wait_ge(proj_ps.sem, proj_ps.at(b, 1))
                        dve.wait_ge(t1_taken.sem, t1_taken.at(b, 1))
                        dve.tensor_tensor(t2[:, :, :], t1[:, 1, :, :], tokens_by_channels(7), ALU.add)\
                           .then_inc(t2_ready.sem, 1)
                        dve.wait_ge(t2_ready.sem, t2_ready.at(b, 1))
                        centre(1, b, t2[:, :, :])
                    if a:
                        dve.wait_ge(gn_ps.sem, gn_ps.at(a, 1))
                        dve.tensor_copy(gn_group[:, :], ps[0:C, 2, 0:2]).then_inc(gn_chain.sem, 1)
                        dve.wait_ge(gn_chain.sem, gn_chain.at(a, 5))
                        mean, mean_sq = gn_group[:, 0:1], gn_group[:, 1:2]
                        dve.scalar_tensor_tensor(gn_v[:, 3:4], mean, mean, mean_sq, ALU.mult, ALU.subtract)\
                           .then_inc(gn_chain.sem, 1)
                        dve.wait_ge(gn_chain.sem, gn_chain.at(a, 6))
                        dve.tensor_scalar(gn_v[:, 0:1], gn_v[:, 3:4], -1.0, GN_EPS, ALU.mult, ALU.add)\
                           .then_inc(gn_chain.sem, 1)
                        dve.wait_ge(gn_rstd.sem, gn_rstd.at(a, 1))
                        dve.tensor_tensor(gn_v[:, 2:3], gn_v[:, 1:2], gn_gamma_half[:, :], ALU.mult)\
                           .then_inc(gn_chain.sem, 1)
                        dve.wait_ge(gn_chain.sem, gn_chain.at(a, 8))
                        dve.scalar_tensor_tensor(gn_v[:, 3:4], mean, gn_v[:, 2:3], gn_beta_half[:, :],
                                                 ALU.mult, ALU.subtract).then_inc(gn_chain.sem, 1)
                        dve.wait_ge(gn_chain.sem, gn_chain.at(a, 9))
                        dve.tensor_scalar(gn_v[:, 4:5], gn_v[:, 3:4], -1.0, None, ALU.mult)\
                           .then_inc(gn_bias.sem, 1)
                    if b:
                        variance(1, b)
                        scale(1, b)
                    if a:
                        dve.wait_ge(gn_parts.sem, gn_parts.at(a, 2))
                        dve.scalar_tensor_tensor(x1, gn_t, 1.0, gn_h, ALU.add, ALU.mult).then_inc(gn_gated.sem, 1)
                        dve.wait_ge(gn_gated.sem, gn_gated.at(a, 1))
                        dve.tensor_tensor(x1, x1, xs[0:C, :], ALU.add).then_inc(x1_ready.sem, 1)

                    (shifted, ex, is_1, count_1, first, left, is_2, count_2, both, gate) = (
                        gate_e[:, k, :, :] for k in range(10))
                    top, top_1, top_2, inverse = (gate_m[:, k, :] for k in range(4))
                    step = [0]

                    def then(ins):
                        step[0] += 1
                        ins.then_inc(gate_chain.sem, 1)
                        dve.wait_ge(gate_chain.sem, gate_chain.at(b, step[0]))

                    def flat(t):
                        return t.rearrange("p i e -> p (i e)")

                    def per_expert(t):
                        return t.unsqueeze(2).to_broadcast([P, TB, E])

                    def combine(blocks):
                        for i in blocks:
                            dve.wait_ge(expert_ps.sem, expert_ps.at(b, i + 1))
                            if i >= 2:
                                dve.wait_ge(combined.sem, combined.at(b, i - 1))
                            else:
                                dve.wait_ge(out_stored.sem, out_stored.at(b, 0))
                            dve.tensor_tensor(moe[:, i % 2, :, :],
                                              banks(6 + i % 2).rearrange("p (e c) -> p e c", c=C),
                                              gate[:, i, :].unsqueeze(2).to_broadcast([P, E, C]), ALU.mult)\
                               .then_inc(weighted.sem, 1)
                            dve.wait_ge(weighted.sem, weighted.at(b, i + 1))
                            dve.tensor_reduce(moe_out[:, i, :], moe[:, i % 2, :, :].rearrange("p e c -> p c e"),
                                              AX.X, ALU.add).then_inc(combined.sem, 1)

                    if b:
                        dve.wait_ge(router_ps.sem, router_ps.at(b, 1))
                        logits = banks(4)[:, 0:TB * E].rearrange("p (i e) -> p i e", e=E)
                        then(dve.tensor_reduce(top, logits, AX.X, ALU.max))
                        dve.tensor_tensor(shifted, logits, per_expert(top), ALU.subtract)\
                           .then_inc(gate_centred.sem, 1)
                    if a:
                        dve.wait_ge(t1_ps.sem, t1_ps.at(a, 1))
                        centre(0, a, tokens_by_channels(3))
                    if b:
                        dve.wait_ge(gate_exped.sem, gate_exped.at(b, 1))
                        then(dve.tensor_reduce(top_1, ex, AX.X, ALU.max))
                        then(dve.tensor_tensor(is_1, ex, per_expert(top_1), ALU.is_ge))
                        then(dve.tensor_tensor_scan(flat(count_1), flat(expert_start[:, :, :]), flat(is_1), 0.0,
                                                    ALU.mult, ALU.add))
                        then(dve.scalar_tensor_tensor(first, count_1, 1.0, is_1, ALU.is_equal, ALU.mult))
                        then(dve.scalar_tensor_tensor(left, first, -2.0, ex, ALU.mult, ALU.add))
                        then(dve.tensor_reduce(top_2, left, AX.X, ALU.max))
                        then(dve.tensor_tensor(is_2, left, per_expert(top_2), ALU.is_ge))
                        then(dve.tensor_tensor_scan(flat(count_2), flat(expert_start[:, :, :]), flat(is_2), 0.0,
                                                    ALU.mult, ALU.add))
                        then(dve.scalar_tensor_tensor(both, count_2, 1.0, is_2, ALU.is_equal, ALU.mult))
                        then(dve.tensor_tensor(both, both, first, ALU.add))
                        then(dve.tensor_tensor(top, top_1, top_2, ALU.add))
                        then(dve.reciprocal(inverse, top))
                        then(dve.tensor_tensor(both, both, ex, ALU.mult))
                        then(dve.tensor_tensor(gate, both, per_expert(inverse), ALU.mult))
                    if a:
                        variance(0, a)
                        scale(0, a)
                    if b:
                        combine(range(0, 4))
                    if a:
                        dve.wait_ge(high_parts.sem, high_parts.at(a, 3))
                        dve.tensor_tensor(rest[:, 0, :], banks(2, 2), part[0], ALU.subtract).then_inc(qk_rest.sem, 1)
                        dve.wait_ge(v_ps.sem, v_ps.at(a, 1))
                        if b:
                            dve.wait_ge(values_added.sem, values_added.at(b, NKEY))
                        dve.tensor_copy(v_aug[:, :, :, 0:DH], banks(0).rearrange("p (i h d) -> p i h d", h=H, d=DH))\
                           .then_inc(v_copied.sem, 1)
                        dve.wait_ge(mid_parts.sem, mid_parts.at(a, 3))
                        dve.tensor_tensor(part[2], rest[:, 0, :], part[1], ALU.subtract).then_inc(qk_low.sem, 1)
                    if b:
                        combine(range(4, TB))
                        dve.wait_ge(combined.sem, combined.at(b, TB))
                        dve.tensor_tensor(moe_out[:, :, :], moe_out[:, :, :], t2[:, :, :], ALU.add)\
                           .then_inc(x2_ready.sem, 1)
                both_streams(dve, program)

            @block.tensor
            def _(pe):
                def program(a, b):
                    def project(weights, src, bank, rows=P):
                        for h in range(NH):
                            last = pe.matmul(ps[0:rows, bank + h, :], weights, src[:, halves(h)],
                                             start=True, stop=True)
                        return last

                    def convolution():
                        pe.wait_ge(x_in.sem, x_in.at(a, 32))
                        if not a.is_first:
                            pe.wait_ge(v_copied.sem, v_copied.at(a, 0))
                            pe.wait_ge(qk_rest.sem, qk_rest.at(a, 0))
                        project(w_conv[:, :], xs, 0).then_inc(conv_ps.sem, 1)
                        project(w_z[:, :], xs, 2).then_inc(z_ps.sem, 1)

                    def dt_before_bias():
                        pe.wait_ge(xc_ready.sem, xc_ready.at(a, 1))
                        project(w_dt_full[:, :], xc, 0).then_inc(dt_ps.sem, 1)

                    def b_and_c():
                        for k, bank, free in ((0, 2, z_ready), (1, 0, relued)):
                            pe.wait_ge(free.sem, free.at(a, 1))
                            project(w_bc[:, k, :, :].rearrange("p n e -> p (n e)"), xc, bank).then_inc(bc_ps.sem, 1)

                    def score_step(s):
                        i, h0, nh = SCORE_STEPS[s]
                        if s >= 2:
                            pe.wait_ge(row_maxed.sem, row_maxed.at(b, s - 1))
                        for hh in range(nh):
                            for h in range(i // QB + 1):
                                bank = 4 + 2 * (s % 2) + hh + h
                                diagonal = h == i // QB
                                w = P * (i % QB + 1) if diagonal else BANK
                                last = pe.matmul(ps[:, bank, 0:w], q_stack[0:9 * DH, h0 + hh, tokens(i)],
                                                 k_stack[0:9 * DH, h0 + hh, h * BANK:h * BANK + w],
                                                 start=True, stop=not diagonal)
                                if diagonal:
                                    last = pe.matmul(ps[:, bank, w - P:w], ident_bf[:, :], mask_q[:, :],
                                                     start=False, stop=True)
                        last.then_inc(scores_ps.sem, 1)

                    if b:
                        pe.wait_ge(stacks_in.sem, stacks_in.at(b, 16 * 18))
                        pe.wait_ge(x_out_copied.sem, x_out_copied.at(b, 0))
                    before_score = {3: convolution, 12: dt_before_bias, 20: b_and_c}
                    for s in range(NSCORE):
                        if a and s in before_score:
                            before_score[s]()
                        if b:
                            score_step(s)
                    if b:
                        pe.wait_ge(max_parts_ready.sem, max_parts_ready.at(b, 1))
                        for i in range(TB):
                            last = pe.transpose(banks(ACC).bitcast(BF16)[0:3 * H, tokens(i)],
                                                max_parts[:, i, :, :].rearrange("p r h -> p (r h)"), ident_bf[:, :])
                        last.then_inc(max_t_ps.sem, 1)

                    def replicate(c, bank, rows):
                        g, q, _ = chunk(c // 2)
                        return pe.matmul(banks(bank), pick[:, q, :, :].rearrange("p n e -> p (n e)"),
                                         rows[:, g, halves(c % 2)], start=True, stop=True)

                    def fold_round(q):
                        pe.wait_ge(read_out.sem, read_out.at(a, NG * (q + 1)))
                        for h in range(NH):
                            for g in range(NG):
                                k = NG * q + g
                                last = pe.matmul(ps[GW * g:GW * (g + 1), 2 + h, :], fold[:, q, :],
                                                 read[:, k % (2 * NG), halves(h)], start=(q == 0),
                                                 stop=(q == JG - 1))
                        last.then_inc(folded.sem, 1)

                    def unit(c):
                        if c == 0:
                            pe.wait_ge(dt_rows_in.sem, dt_rows_in.at(a, 16 * 3 * NG))
                            pe.wait_ge(c_copied.sem, c_copied.at(a, 1))
                        else:
                            pe.wait_ge(decayed.sem, decayed.at(a, c))
                        replicate(c, 0, dt_rows).then_inc(dt_rep.sem, 1)
                        if c == 0:
                            pe.wait_ge(u_rows_in.sem, u_rows_in.at(a, 16 * 3 * NG))
                        else:
                            pe.wait_ge(driven.sem, driven.at(a, c))
                        replicate(c, 1, u_rows).then_inc(u_rep.sem, 1)
                        k = c // 2
                        if c % 2 == 1 and k > NG and k % NG == 2:
                            fold_round(k // NG - 1)

                    def ring_wait(item):
                        r = ring_place[item] - len(RING)
                        if r >= 0:
                            kind, index = ring_items[r]
                            read_by = exped if kind == "scores" else attn_ready
                            pe.wait_ge(read_by.sem, read_by.at(b, index + 1))

                    def weigh(s):
                        n, quad, half, j = KEY_STEPS[s]
                        lo = max(half * BANK, j * P)
                        w = (half + 1) * BANK - lo
                        diagonal = lo == j * P
                        for hq in range(QUAD):
                            head, item = quad * QUAD + hq, ("scores", QUAD * s + hq)
                            ring_wait(item)
                            last = pe.matmul(ps[:, ring_bank(item), 0:w], k_stack[0:KQ, head, tokens(j)],
                                             q_stack[0:KQ, head, lo:lo + w], start=True, stop=not diagonal)
                            if diagonal:
                                last = pe.matmul(ps[:, ring_bank(item), 0:P], ident_bf[:, :], mask_k[:, :],
                                                 start=False, stop=True)
                            last.then_inc(weights_ps.sem, 1)

                    def add_values(s):
                        n, quad, half, j = KEY_STEPS[s]
                        lo = max(0, j * P - half * BANK)
                        pe.wait_ge(exped.sem, exped.at(b, QUAD * (s + 1)))
                        if n > 0 and j == 0:
                            pe.wait_ge(acc_copied.sem, acc_copied.at(b, n))
                        for hq in range(QUAD):
                            last = pe.matmul(ps[GW * hq:GW * (hq + 1), ACC, lo:BANK],
                                             v_aug[:, j, quad * QUAD + hq, :],
                                             probs[:, (QUAD * s + hq) % (2 * QUAD), 0:BANK - lo],
                                             start=(j == 0), stop=(j == QB * (half + 1) - 1))
                        last.then_inc(values_added.sem, 1)

                    def heads_to_tokens(n):
                        item = ("heads", n)
                        pe.wait_ge(acc_copied.sem, acc_copied.at(b, n + 1))
                        ring_wait(item)
                        for i in range(QB):
                            last = pe.transpose(ps[:, ring_bank(item), tokens(i)], acc_sb[:, n % 2, tokens(i)],
                                                ident[:, :])
                        last.then_inc(heads_t_ps.sem, 1)

                    if a:
                        for c in range(AHEAD):
                            unit(c)
                    if b:
                        pe.wait_ge(v_copied.sem, v_copied.at(b, 1))
                        pe.wait_ge(max_in.sem, max_in.at(b, 16))
                    for s in range(NKEY):
                        if b:
                            weigh(s)
                        if a:
                            unit(AHEAD + s)
                        if b:
                            if s > 0:
                                add_values(s - 1)
                            n = KEY_STEPS[s][0]
                            if n > 0 and s == LAST_STEP[n - 1] + LAG:
                                heads_to_tokens(n - 1)
                    if b:
                        add_values(NKEY - 1)
                    if a:
                        fold_round(JG - 1)
                    if a:
                        pe.wait_ge(y_ready.sem, y_ready.at(a, 1))
                        project(w_out[:, :], y, 0, C).then_inc(out_ps.sem, 1)
                    if b:
                        heads_to_tokens(len(GROUPS) - 1)

                    def to_tokens(src, dst):
                        for i in range(TB):
                            last = pe.transpose(dst[:, i * C:(i + 1) * C], src[:, tokens(i)], ident[0:C, 0:C])
                        return last

                    def to_channels(src, dst):
                        for i in range(TB):
                            last = pe.transpose(dst[0:C, tokens(i)], src[:, i, :], ident[:, :])
                        return last

                    def by_tokens(src, weights, dst, width):
                        for i in range(TB):
                            last = pe.matmul(dst[:, i * width:(i + 1) * width], src[:, tokens(i)], weights,
                                             start=True, stop=True)
                        return last

                    def experts(blocks):
                        for i in blocks:
                            if i >= 2:
                                pe.wait_ge(weighted.sem, weighted.at(b, i - 1))
                            pe.matmul(banks(6 + i % 2), xn_t[:, 1, tokens(i)],
                                      w_expert[:, :, :].rearrange("p e c -> p (e c)"), start=True, stop=True)\
                              .then_inc(expert_ps.sem, 1)

                    if a:
                        pe.wait_ge(gn_chain.sem, gn_chain.at(a, 4))
                        hold(pe, "pe")
                        pe.matmul(ps[0:C, 2, 0:2], group_mean[:, :, :].rearrange("p g c -> p (g c)"), gn_mv[:, :],
                                  start=True, stop=True).then_inc(gn_ps.sem, 1)
                    if b:
                        pe.wait_ge(attn_ready.sem, attn_ready.at(b, len(GROUPS)))
                        hold(pe, "pe")
                        to_channels(attn, banks(5, 2)).then_inc(attn_t_ps.sem, 1)
                        pe.wait_ge(attn_t_copied.sem, attn_t_copied.at(b, 1))
                        by_tokens(attn_t, w_o[:, :], banks(7), C).then_inc(proj_ps.sem, 1)
                        pe.wait_ge(xn_ready[1].sem, xn_ready[1].at(b, 1))
                        hold(pe, "pe")
                        to_channels(xn[:, 1, :, :], banks(5, 2)).then_inc(xnt_ps[1].sem, 1)
                    if a:
                        pe.wait_ge(x1_ready.sem, x1_ready.at(a, 1))
                        hold(pe, "pe")
                        to_tokens(x1, banks(3)).then_inc(t1_ps.sem, 1)
                    if b:
                        pe.wait_ge(xnt_copied[1].sem, xnt_copied[1].at(b, 1))
                        by_tokens(xn_t[:, 1, :], w_router[:, :], banks(4), E).then_inc(router_ps.sem, 1)
                        experts(range(0, 2))
                    if a:
                        pe.wait_ge(xn_ready[0].sem, xn_ready[0].at(a, 1))
                        hold(pe, "pe")
                        to_channels(xn[:, 0, :, :], banks(0, 2)).then_inc(xnt_ps[0].sem, 1)
                    if b:
                        experts(range(2, 4))
                    if a:
                        pe.wait_ge(xnt_copied[0].sem, xnt_copied[0].at(a, 1))
                        pe.wait_ge(t1_copied.sem, t1_copied.at(a, 1))
                        project(w_qk[:, :], xn_t[:, 0, :], 2).then_inc(qk_ps.sem, 1)
                        by_tokens(xn_t[:, 0, :], w_v[:, :], banks(0), C).then_inc(v_ps.sem, 1)
                    if b:
                        experts(range(4, TB))
                        pe.wait_ge(x2_ready.sem, x2_ready.at(b, 1))
                        hold(pe, "pe")
                        to_channels(moe_out, banks(4, 2)).then_inc(x_out_ps.sem, 1)
                both_streams(pe, program)


_INS = ["x", "L0_conv_W_in", "L0_conv_conv_w", "L0_conv_conv_b", "L0_conv_W_x", "L0_conv_W_dt", "L0_conv_b_dt",
        "L0_conv_A_log", "L0_conv_D", "L0_conv_W_out", "L0_conv_gn_gamma", "L0_conv_gn_beta", "L1_attn_w_attn",
        "L1_attn_w_proj", "L1_ffn_router_w", "L1_ffn_router_b", "L1_ffn_expert_w", "L1_ffn_expert_b"]


def kernel(**inputs):
    import numpy as np
    import concourse.bacc as bacc
    from concourse.bass_utils import run_bass_kernel_spmd

    nc = bacc.Bacc("TRN2", target_bir_lowering=False, num_devices=1)
    arrays, args = {}, []
    for name in _INS:
        a = np.ascontiguousarray(inputs[name])
        arrays[f"in_{name}"] = a
        args.append(nc.dram_tensor(f"in_{name}", a.shape, mybir.dt.from_np(a.dtype), kind="ExternalInput").ap())
    out = nc.dram_tensor("out", inputs["x"].shape, F32, kind="ExternalOutput").ap()
    mamba_attention_moe(nc, *args, out)
    r = run_bass_kernel_spmd(nc, [arrays], core_ids=[0])
    return r.results[0]["out"]
```

```python
from contextlib import ExitStack

import concourse.bass as bass
from concourse import mybir

F32 = mybir.dt.float32
BF16 = mybir.dt.bfloat16
ALU = mybir.AluOpType
ACT = mybir.ActivationFunctionType
AX = mybir.AxisListType

P = 128
BANK = 512
MASKED = -1e30
GN_EPS = 1e-5
LN_EPS = 1e-5


class Batch:

    def __init__(self, register, offset):
        self.register = register
        self.offset = offset
        self.number = offset if register is None else register + offset if offset else register
        self.is_first = register is None and offset == 0


class Signal:

    def __init__(self, ctx, nc, name, per, base=0):
        self.sem = ctx.enter_context(nc.semaphore(name))
        self.per = per
        self.base = base

    def at(self, batch, count):
        constant = self.base + batch.offset * self.per + count
        return constant if batch.register is None else batch.register * self.per + constant


def mamba_attention_moe(nc, x, W_in, conv_w, conv_b, W_x, W_dt, b_dt, A_log, D, W_out, gn_gamma, gn_beta,
                        w_attn, w_proj, router_w, router_b, expert_w, expert_b, out):
    B, C, HH, WW = x.shape
    T = HH * WW
    DI = W_in.shape[1] // 2
    R = W_dt.shape[0]
    NS = (W_x.shape[1] - R) // 2
    E = router_w.shape[1]
    H = 8
    DH = C // H
    G = 4
    CG = C // G
    TB = T // P
    NH = T // BANK
    QB = BANK // P
    CH = P // NS
    NJ = DI // CH
    NG = 4
    JG = NJ // NG
    GW = P // NG
    SCALE = float(DH) ** -0.5
    K1 = C + 32
    KQ = 9 * DH + 3
    QUAD = 4
    assert DI == P and NS * CH == P and T == NH * BANK

    xr = x.rearrange("b c h w -> b c (h w)")
    outr = out.rearrange("b c h w -> b c (h w)")
    q_parts_dram = nc.dram_tensor("q_parts_dram", (3, C, T), BF16, kind="Internal").ap()
    k_parts_dram = nc.dram_tensor("k_parts_dram", (5, C, T), BF16, kind="Internal").ap()
    t1_dram = nc.dram_tensor("t1_dram", (B, P, TB * C), F32, kind="Internal").ap()
    max_parts_dram = nc.dram_tensor("max_parts_dram", (3 * H, T), BF16, kind="Internal").ap()

    with ExitStack() as ctx:
        def sb(name, shape, dt=F32):
            return ctx.enter_context(nc.sbuf_tensor(name, shape, dt))

        ps = ctx.enter_context(nc.psum_tensor("ps", [P, 8, BANK], F32))

        def banks(n, k=1):
            return ps[:, n:n + k, :].rearrange("p a b -> p (a b)")

        w_conv = sb("w_conv", [P, DI])
        w_z = sb("w_z", [P, DI])
        conv_rows = sb("conv_rows", [P, 2 * DI])
        conv_bias = sb("conv_bias", [P, 1])
        w_x = sb("w_x", [P, R + 2 * NS])
        w_x_dt_t = sb("w_x_dt_t", [R, P])
        w_dt = sb("w_dt", [R, DI])
        w_dt_full = sb("w_dt_full", [P, DI])
        dt_bias = sb("dt_bias", [P, 1])
        w_bc = sb("w_bc", [P, 2, NS, CH])
        a_scale = sb("a_scale", [P, NJ])
        d_skip = sb("d_skip", [P, 1])
        w_out = sb("w_out", [P, C])
        gn_gamma_half = sb("gn_gamma_half", [C, 1])
        gn_beta_half = sb("gn_beta_half", [C, 1])
        group_mean = sb("group_mean", [C, G, CG])
        w_qk = sb("w_qk", [K1, 2 * C])
        w_v = sb("w_v", [K1, C])
        w_o = sb("w_o", [C, C])
        w_router = sb("w_router", [K1, E])
        w_expert = sb("w_expert", [K1, E, C])
        ident = sb("ident", [P, P])
        ident_bf = sb("ident_bf", [P, P], BF16)
        mask_q = sb("mask_q", [P, P], BF16)
        mask_k = sb("mask_k", [P, P], BF16)
        pick = sb("pick", [96, JG, NS, CH], BF16)
        fold = sb("fold", [P, JG, GW])
        state_sum = sb("state_sum", [P, CH])
        minus_half = sb("minus_half", [P, TB])
        expert_start = sb("expert_start", [P, TB, E])

        xs = sb("xs", [P, T])
        xc = sb("xc", [P, T])
        z_gate = sb("z_gate", [P, T])
        b_rep = sb("b_rep", [P, T])
        c_rep = sb("c_rep", [P, T])
        dt_rows = sb("dt_rows", [96, NG, T], BF16)
        u_rows = sb("u_rows", [96, NG, T], BF16)
        decay = sb("decay", [P, 2, T])
        drive = sb("drive", [P, 3, T])
        state = sb("state", [P, 2, T])
        read = sb("read", [P, 2 * NG, T])
        rest = decay
        z_tanh = decay[:, 0, :]
        relu = drive[:, 0, :]
        silu_h, silu_t = drive[:, 1, :], drive[:, 2, :]
        softplus_a, softplus_b = state[:, 0, :], state[:, 1, :]
        y_skip, y = state[:, 0, :], state[:, 1, :]
        dt, u = read[:, 0, :], read[:, 1, :]
        x1, rest_qk = read[0:C, 2, :], read[:, 2, :]
        gn_h, gn_t = read[0:C, 3, :], read[0:C, 7, :]
        qk_part = [read[:, *place].bitcast(BF16) for place in ((3, slice(0, T // 2)), (3, slice(T // 2, T)),
                                                               (7, slice(0, T // 2)))]
        part = [read[:, 4 + i // 2, (i % 2) * (T // 2):(i % 2 + 1) * (T // 2)].bitcast(BF16) for i in range(6)]
        gn_stats = sb("gn_stats", [C, 2, 6])
        gn_mv = sb("gn_mv", [C, 2])
        gn_group = sb("gn_group", [C, 2])
        gn_v = sb("gn_v", [C, 5])
        residual = sb("residual", [C, T])
        t1 = sb("t1", [P, TB, C])
        t1_back = sb("t1_back", [P, TB, C])
        t2 = sb("t2", [P, TB, C])
        xcen = sb("xcen", [P, 2, TB, C])
        xn = sb("xn", [P, 2, TB, C])
        ln_s = sb("ln_s", [P, 2, 5, TB])
        xn_t = sb("xn_t", [K1, 2, T])
        v_aug = sb("v_aug", [P, TB, H, GW])
        q_stack = sb("q_stack", [P, H, T], BF16)
        k_stack = sb("k_stack", [P, H, T], BF16)
        row_max = sb("row_max", [P, TB, H])
        max_rest = sb("max_rest", [P, TB, H])
        max_parts = sb("max_parts", [P, TB, 3, H], BF16)
        max_t = sb("max_t", [3 * H, T], BF16)
        probs = sb("probs", [P, 2 * QUAD, BANK])
        acc_sb = sb("acc_sb", [P, 2, BANK])
        den = sb("den", [P, TB, H])
        attn = sb("attn", [P, TB, C])
        attn_t = xn_t[0:C, 1, :]
        moe_out = sb("moe_out", [P, TB, C])
        gate_m = sb("gate_m", [P, 4, TB])
        gate_e = sb("gate_e", [P, 10, TB, E])
        moe = sb("moe", [P, 2, E, C])
        x_out = moe[0:C, :, :, :].rearrange("p a e c -> p (a e c)")

        w_qk_by_head = z_gate[0:C, 0:2 * C]
        a_log, a_exp = z_gate[:, 2 * C:2 * C + NS], z_gate[:, 3 * C:3 * C + NS]
        chunk_of = z_gate[:, 4 * C:4 * C + NJ]
        a_spread = z_gate[:, T // 2:T // 2 + P].rearrange("p (n e) -> p n e", e=CH)

        weights_in = ctx.enter_context(nc.semaphore("weights_in"))
        masks_built = ctx.enter_context(nc.semaphore("masks_built"))
        dve_setup = ctx.enter_context(nc.semaphore("dve_setup"))
        pe_setup = ctx.enter_context(nc.semaphore("pe_setup"))
        act_setup = ctx.enter_context(nc.semaphore("act_setup"))
        pool_chain = ctx.enter_context(nc.semaphore("pool_chain"))
        LOADS = 21
        a_spread_ready = ctx.enter_context(nc.semaphore("a_spread_ready"))
        setup_dmas = [0]

        with nc.Block() as block:
            @block.sync
            def _(sp):
                sp.wait_ge(dve_setup, 5)
                def load(dst, src, strided=False):
                    sp.dma_start(dst, src, allow_slow_non_contiguous=strided).then_inc(weights_in, 16)
                    setup_dmas[0] += 1
                load(w_conv[0:C, :], W_in[:, 0:DI])
                load(w_conv[C:2 * C, :], W_in[:, 0:DI])
                load(w_z[0:C, :], W_in[:, DI:2 * DI])
                load(conv_rows[:, :], conv_w.rearrange("(a d) k -> a (d k)", a=1).to_broadcast([P, 2 * DI]))
                load(conv_bias[:, :], conv_b.rearrange("(d a) -> d a", a=1))
                load(w_x[:, :], W_x[:, :])
                load(w_x_dt_t[:, :], W_x[:, 0:R].rearrange("d r -> r d"), strided=True)
                load(w_dt[:, :], W_dt[:, :])
                load(dt_bias[:, :], b_dt.rearrange("(d a) -> d a", a=1))
                load(a_log, A_log[:, :])
                load(d_skip[:, :], D.rearrange("(d a) -> d a", a=1))
                load(w_out[:, :], W_out[:, :])
                load(gn_gamma_half[:, :], gn_gamma.rearrange("(d a) -> d a", a=1))
                load(gn_beta_half[:, :], gn_beta.rearrange("(d a) -> d a", a=1))
                load(w_qk_by_head, w_attn[:, 0:2 * C])
                load(w_v[0:C, :], w_attn[:, 2 * C:3 * C])
                load(w_o[:, :], w_proj[:, :])
                load(w_router[0:C, :], router_w[:, :])
                load(w_router[C:C + 1, :], router_b.rearrange("(a e) -> a e", a=1))
                load(w_expert[0:C, :, :], expert_w.rearrange("e d c -> d e c"))
                load(w_expert[C:C + 1, :, :], expert_b.rearrange("(a e) c -> a e c", a=1))
                assert setup_dmas[0] == LOADS

            @block.vector
            def _(dve):
                dve.memset(w_z[C:P, :], 0.0).then_inc(dve_setup, 1)
                dve.memset(w_qk[C:K1, :], 0.0).then_inc(dve_setup, 1)
                dve.memset(w_v[C:K1, :], 0.0).then_inc(dve_setup, 1)
                dve.memset(w_router[C:K1, :], 0.0).then_inc(dve_setup, 1)
                dve.memset(w_expert[C:K1, :, :], 0.0).then_inc(dve_setup, 1)
                dve.memset(xn_t[C:K1, :, :], 1.0).then_inc(dve_setup, 1)
                dve.memset(xs[C:2 * C, 0:1], 0.0).then_inc(dve_setup, 1)
                dve.memset(v_aug[:, :, :, DH:GW], 1.0).then_inc(dve_setup, 1)
                dve.memset(k_stack[64:96, :, :], 1.0).then_inc(dve_setup, 1)
                dve.memset(minus_half[:, :], -0.5).then_inc(dve_setup, 1)
                dve.memset(expert_start[:, :, :], 1.0).then_inc(dve_setup, 1)
                dve.wait_ge(dve_setup, 11)
                dve.memset(expert_start[:, :, 0:1], 0.0).then_inc(dve_setup, 1)
                dve.wait_ge(weights_in, 16 * LOADS)
                conv_k = conv_rows[:, :].rearrange("p (d k) -> p k d", k=2)
                for rows, tap in ((slice(0, C), 1), (slice(C, 2 * C), 0)):
                    dve.scalar_tensor_tensor(w_conv[rows, :], w_conv[rows, :], 0.5, conv_k[rows, tap, :],
                                             ALU.mult, ALU.mult).then_inc(dve_setup, 1)
                for t in (w_z[0:C, :], conv_bias[:, :], gn_gamma_half[:, :], gn_beta_half[:, :]):
                    dve.tensor_scalar(t, t, 0.5, None, ALU.mult).then_inc(dve_setup, 1)
                dve.tensor_copy(w_qk[0:C, :].rearrange("p (s d h) -> p s d h", s=2, d=DH),
                                w_qk_by_head.rearrange("p (s h d) -> p s d h", s=2, d=DH)).then_inc(dve_setup, 1)
                for k in range(2):
                    cols = w_x[:, R + k * NS:R + (k + 1) * NS]
                    dve.tensor_copy(w_bc[:, k, :, :], cols.unsqueeze(2).to_broadcast([P, NS, CH]))\
                       .then_inc(dve_setup, 1)
                dve.wait_ge(pe_setup, 1)
                dve.tensor_copy(w_dt_full[:, :], ps[:, 0, 0:DI]).then_inc(dve_setup, 1)
                dve.wait_ge(masks_built, 1)
                dve.wait_ge(act_setup, 1)
                dve.tensor_tensor(a_spread, a_exp.unsqueeze(2).to_broadcast([P, NS, CH]),
                                  state_sum[:, :].unsqueeze(1).to_broadcast([P, NS, CH]), ALU.mult)\
                   .then_inc(a_spread_ready, 1)
                dve.wait_ge(pe_setup, 2)
                dve.tensor_scalar(a_scale[:, :], ps[:, 1, 0:NJ], -1.0, None, ALU.mult).then_inc(dve_setup, 1)
                for q in range(JG):
                    dve.tensor_copy(fold[:, q, q * CH:(q + 1) * CH], state_sum[:, :]).then_inc(dve_setup, 1)

            @block.scalar
            def _(act):
                act.wait_ge(weights_in, 16 * LOADS)
                act.activation(a_exp, a_log, ACT.Exp).then_inc(act_setup, 1)

            @block.tensor
            def _(pe):
                pe.wait_ge(weights_in, 16 * LOADS)
                pe.matmul(ps[:, 0, 0:DI], w_x_dt_t[:, :], w_dt[:, :], start=True, stop=True).then_inc(pe_setup, 1)
                pe.wait_ge(a_spread_ready, 1)
                pe.matmul(ps[:, 1, 0:NJ], a_spread.rearrange("p n e -> p (n e)"), chunk_of, start=True, stop=True)\
                  .then_inc(pe_setup, 1)

            @block.gpsimd
            def _(pool):
                step = [0]

                def then(ins):
                    ins.then_inc(pool_chain, 1)
                    step[0] += 1
                    pool.wait_ge(pool_chain, step[0])

                def diagonal(tile, pattern, base, fill=1.0, op=ALU.not_equal, mult=1):
                    then(pool.affine_select(out=tile, in_=tile, pattern=pattern, compare_op=op, fill=fill,
                                            base=base, channel_multiplier=mult))
                then(pool.memset(state_sum[:, :], 0.0))
                then(pool.memset(fold[:, :, :], 0.0))
                for n in range(NS):
                    diagonal(state_sum[:, :], [[-1, CH]], -CH * n)
                then(pool.memset(chunk_of, 1.0))
                diagonal(chunk_of, [[-CH, NJ]], 0, 0.0, ALU.is_ge)
                diagonal(chunk_of, [[CH, NJ]], CH - 1, 0.0, ALU.is_ge, -1)
                pool.sem_inc(masks_built, 1)
                then(pool.memset(ident[:, :], 0.0))
                then(pool.memset(ident_bf[:, :], 0.0))
                diagonal(ident[:, :], [[-1, P]], 0)
                diagonal(ident_bf[:, :], [[-1, P]], 0)
                then(pool.memset(pick[:, :, :, :], 0.0))
                for part_row in range(3):
                    diagonal(pick[:, :, :, :], [[-CH, JG], [0, NS], [-1, CH]], -32 * part_row)
                then(pool.memset(mask_q[:, :], 0.0))
                diagonal(mask_q[:, :], [[-1, P]], 0, MASKED, ALU.is_ge)
                then(pool.memset(mask_k[:, :], 0.0))
                diagonal(mask_k[:, :], [[1, P]], 0, MASKED, ALU.is_ge, -1)
                then(pool.memset(group_mean[:, :, :], 1.0 / CG))
                diagonal(group_mean[:, :, :], [[-CG, G], [0, CG]], 0, 0.0, ALU.is_ge)
                diagonal(group_mean[:, :, :], [[CG, G], [0, CG]], CG - 1, 0.0, ALU.is_ge, -1)

        def signal(name, per, base=0):
            return Signal(ctx, nc, name, per, base)

        SCORE_STEPS = [(i, h, 2 if i < QB else 1) for quad in range(H // QUAD) for i in range(TB)
                       for h in range(quad * QUAD, (quad + 1) * QUAD, 2 if i < QB else 1)]
        NSCORE = len(SCORE_STEPS)
        GROUPS = [(quad, half) for quad in range(H // QUAD) for half in range(NH)]
        KEY_STEPS = [(n, quad, half, j) for n, (quad, half) in enumerate(GROUPS) for j in range(QB * (half + 1))]
        NKEY = len(KEY_STEPS)
        LAST_STEP = [max(s for s, ks in enumerate(KEY_STEPS) if ks[0] == n) for n in range(len(GROUPS))]
        LAG = 2
        UNITS = 2 * NJ
        UNITS_IN = (2, 2, 2, 1, 0, 2, 2, 0, 2, 1, 2, 1, 1, 1, 2, 1, 0, 0, 1, 1, 2, 1, 1, 2, 0, 1, 0, 1)
        FOLDS = ((0, 0, 13), (0, 1, 13), (1, 0, 18), (1, 1, 19))
        TURNS = ((1, "attn_t", 0), (1, "attn_t", 1), (2, "proj", 0), (8, "xn_t", 0), (9, "xn_t", 1),
                 (11, "router", 0), (13, "expert", 0), (15, "expert", 1), (16, "expert", 2), (16, "expert", 3),
                 (19, "expert", 4), (20, "expert", 5), (22, "expert", 6), (22, "expert", 7), (26, "out_t", 0),
                 (27, "out_t", 1))
        VARIANCE_AT, SCALE_AT, GATES_AT = 3, 6, 12
        BEFORE = len(UNITS_IN) - NKEY
        assert sum(UNITS_IN) == UNITS
        ROUNDS = [(n - BEFORE if n >= BEFORE else None, list(range(sum(UNITS_IN[:n]), sum(UNITS_IN[:n + 1]))),
                   [(kind, index) for at, kind, index in TURNS if at == n]) for n in range(len(UNITS_IN))]
        ACC = 4
        RING = (0, 1, 5, 6, 7)

        x_in = signal("x_in", 32)
        residual_in = signal("residual_in", 16)
        t1_stored = signal("t1_stored", 16)
        t1_back_in = signal("t1_back_in", 16)
        dt_rows_in = signal("dt_rows_in", 16 * 3 * NG)
        u_rows_in = signal("u_rows_in", 16 * 3 * NG)
        qk_parts_out = signal("qk_parts_out", 16 * 8)
        stacks_in = [signal(f"stacks_in_{quad}", 16 * 6) for quad in range(2)]
        max_t_out = signal("max_t_out", 16)
        max_in = signal("max_in", 16)
        out_stored = signal("out_stored", 16, base=1)
        conv_ps = signal("conv_ps", NH)
        z_ps = signal("z_ps", NH)
        dt_ps = signal("dt_ps", NH)
        bc_ps = signal("bc_ps", 2 * NH)
        dt_rep = signal("dt_rep", UNITS)
        u_rep = signal("u_rep", UNITS)
        folded = signal("folded", NH * JG)
        out_ps = signal("out_ps", NH)
        gn_ps = signal("gn_ps", 1)
        t1_ps = signal("t1_ps", 1)
        xnt_ps = [signal("xnt_ps_1", NH), signal("xnt_ps_2", NH)]
        qk_ps = signal("qk_ps", NH)
        v_ps = signal("v_ps", 1)
        scores_ps = signal("scores_ps", NSCORE)
        max_t_ps = signal("max_t_ps", 1)
        weights_ps = signal("weights_ps", QUAD * NKEY)
        values_added = signal("values_added", NKEY)
        heads_t_ps = signal("heads_t_ps", len(GROUPS))
        attn_t_ps = signal("attn_t_ps", NH)
        proj_ps = signal("proj_ps", 1)
        router_ps = signal("router_ps", 1)
        expert_ps = signal("expert_ps", TB)
        x_out_ps = signal("x_out_ps", NH)
        silu_parts = signal("silu_parts", 2)
        z_tanh_done = signal("z_tanh_done", 1)
        relued = signal("relued", 1)
        softplus_steps = signal("softplus_steps", 3)
        b_copied = signal("b_copied", 1)
        c_copied = signal("c_copied", 1)
        high_parts = signal("high_parts", 2)
        mid_parts = signal("mid_parts", 2)
        qk_high = signal("qk_high", 1)
        qk_mid = signal("qk_mid", 1)
        decayed = signal("decayed", UNITS)
        gn_parts = signal("gn_parts", 2)
        t1_copied = signal("t1_copied", 1)
        squared = [signal("squared_1", 1), signal("squared_2", 1)]
        xnt_copied = [signal("xnt_copied_1", 1), signal("xnt_copied_2", NH)]
        exped = signal("exped", QUAD * NKEY)
        acc_copied = signal("acc_copied", len(GROUPS))
        attn_t_copied = signal("attn_t_copied", NH)
        gate_exped = signal("gate_exped", 1)
        x_out_copied = signal("x_out_copied", NH)
        xc_ready = signal("xc_ready", 1)
        z_ready = signal("z_ready", 1)
        driven = signal("driven", UNITS)
        scanned = signal("scanned", NJ)
        skipped = signal("skipped", 1)
        gn_chain = signal("gn_chain", 9)
        gn_bias = signal("gn_bias", 1)
        gn_gated = signal("gn_gated", 1)
        ln_chain = [signal("ln_chain_1", 3), signal("ln_chain_2", 3)]
        centred = [signal("centred_1", 1), signal("centred_2", 1)]
        ln_var = [signal("ln_var_1", 1), signal("ln_var_2", 1)]
        xn_ready = [signal("xn_ready_1", 1), signal("xn_ready_2", 1)]
        qk_rest = signal("qk_rest", 1)
        v_copied = signal("v_copied", 1)
        row_maxed = signal("row_maxed", NSCORE)
        max_chain = signal("max_chain", 3)
        max_parts_ready = signal("max_parts_ready", 1)
        max_t_copied = signal("max_t_copied", 1)
        den_ready = signal("den_ready", len(GROUPS))
        attn_ready = signal("attn_ready", len(GROUPS))
        t2_ready = signal("t2_ready", 1)
        gate_chain = signal("gate_chain", 15)
        gate_centred = signal("gate_centred", 1)
        weighted = signal("weighted", TB)
        combined = signal("combined", TB)
        x2_ready = signal("x2_ready", 1)
        qk_low = signal("qk_low", 1)
        x1_ready = signal("x1_ready", 1)
        y_ready = signal("y_ready", 1)
        dt_ready = signal("dt_ready", 1)
        u_ready = signal("u_ready", 1)
        rests = signal("rests", 2)
        low_parts = signal("low_parts", 2)
        read_out = signal("read_out", NJ)
        gn_rstd = signal("gn_rstd", 1)
        ln_rstd = [signal("ln_rstd_1", 1), signal("ln_rstd_2", 1)]

        held = {name: ctx.enter_context(nc.semaphore(f"held_{name}")) for name in ("pe", "dve", "sp")}

        def hold(engine, name):
            engine.sem_inc(held[name])

        def chunk(k):
            g, q = k % NG, k // NG
            return g, q, JG * g + q

        def halves(n):
            return slice(n * BANK, (n + 1) * BANK)

        def tokens(i):
            return slice(i * P, (i + 1) * P)

        def tokens_by_channels(bank):
            return banks(bank).rearrange("p (i c) -> p i c", c=C)

        def pipeline(engine, program):
            depth = 4
            for t in range(depth):
                program(*(Batch(None, t - k) if t >= k else None for k in range(depth + 1)))
            with engine.Fori(0, B - depth) as i:
                program(*(Batch(i, depth - k) for k in range(depth + 1)))
            for t in range(B, B + depth):
                program(*(Batch(None, t - k) if t - k < B else None for k in range(depth + 1)))

        def ring_users(c, b, f):
            users = []
            for s, units, turns in ROUNDS:
                at_step = b and s is not None
                if at_step:
                    users += [("scores", QUAD * s + hq) for hq in range(QUAD - 1)]
                if c:
                    users += [(kind, k2) for k2 in units[:1] for kind in ("dt", "u")]
                if at_step:
                    users.append(("scores", QUAD * s + QUAD - 1))
                    if s - LAG in LAST_STEP:
                        users.append(("heads", LAST_STEP.index(s - LAG)))
                if c:
                    users += [(kind, k2) for k2 in units[1:] for kind in ("dt", "u")]
                if f:
                    users += turns
            if b:
                users.append(("heads", len(GROUPS) - 1))
            return users

        def ring_places(c, b, f):
            return {user: n for n, user in enumerate(ring_users(c, b, f))}

        def bank_read(user, c, b, f):
            kind, n = user
            return {"dt": (decayed, c), "u": (driven, c), "scores": (exped, b), "heads": (attn_ready, b),
                    "attn_t": (attn_t_copied, f), "proj": (t2_ready, f), "xn_t": (xnt_copied[1], f),
                    "router": (gate_centred, f), "expert": (weighted, f), "out_t": (x_out_copied, f)}[kind] + (n + 1,)

        def scale(engine, n, batch):
            engine.tensor_tensor(xn[:, n, :, :], xcen[:, n, :, :],
                                 ln_s[:, n, 4, :].unsqueeze(2).to_broadcast([P, TB, C]), ALU.mult)\
                  .then_inc(xn_ready[n].sem, 1)

        with nc.Block() as block:
            @block.sync
            def _(sp):
                def program(a, c, p, b, f):
                    if p:
                        if not p.is_first:
                            sp.wait_ge(x1_ready.sem, x1_ready.at(p, 0))
                            hold(sp, "sp")
                        sp.dma_start(residual[:, :], xr[p.number, :, :]).then_inc(residual_in.sem, 16)
                    if a:
                        if c:
                            sp.wait_ge(z_ps.sem, z_ps.at(c, NH))
                            hold(sp, "sp")
                        sp.dma_start(xs[0:C, :], xr[a.number, :, :]).then_inc(x_in.sem, 16)
                        sp.dma_start(xs[C:2 * C, 1:T], xr[a.number, :, 0:T - 1]).then_inc(x_in.sem, 16)
                    if f:
                        sp.wait_ge(t1_stored.sem, t1_stored.at(f, 16))
                        hold(sp, "sp")
                        sp.dma_start(t1_back[:, :, :].rearrange("p i c -> p (i c)"), t1_dram[f.number, :, :])\
                          .then_inc(t1_back_in.sem, 16)
                    if c:
                        for r, parts in enumerate((high_parts, mid_parts, low_parts)):
                            for n, (rows, arrived) in enumerate(((dt_rows, dt_rows_in), (u_rows, u_rows_in))):
                                sp.wait_ge(parts.sem, parts.at(c, n + 1))
                                hold(sp, "sp")
                                for g in range(NG):
                                    sp.dma_start(rows[32 * r:32 * (r + 1), g, :],
                                                 part[3 * n + r][GW * g:GW * (g + 1), :]).then_inc(arrived.sem, 16)
                    if p:
                        sp.wait_ge(t1_copied.sem, t1_copied.at(p, 1))
                        hold(sp, "sp")
                        sp.dma_start(t1_dram[p.number, :, :], t1[:, :, :].rearrange("p i c -> p (i c)"))\
                          .then_inc(t1_stored.sem, 16)
                        if not p.is_first:
                            for quad in range(2):
                                sp.wait_ge(stacks_in[quad].sem, stacks_in[quad].at(p, 0))
                                hold(sp, "sp")
                        for r, parts in enumerate((qk_high, qk_mid, qk_low)):
                            sp.wait_ge(parts.sem, parts.at(p, 1))
                            hold(sp, "sp")
                            sp.dma_start(q_parts_dram[r, :, :], qk_part[r][0:C, :]).then_inc(qk_parts_out.sem, 16)
                            for copy in range(r, 5, 3):
                                sp.dma_start(k_parts_dram[copy, :, :], qk_part[r][C:2 * C, :])\
                                  .then_inc(qk_parts_out.sem, 16)
                    if b:
                        sp.wait_ge(max_t_copied.sem, max_t_copied.at(b, 1))
                        hold(sp, "sp")
                        sp.dma_start(max_parts_dram[:, :], max_t[:, :]).then_inc(max_t_out.sem, 16)
                        sp.wait_ge(max_t_out.sem, max_t_out.at(b, 16))
                        hold(sp, "sp")
                        sp.dma_start(q_stack[KQ - 3:KQ, :, :],
                                     max_parts_dram.rearrange("(r h) t -> r h t", h=H)).then_inc(max_in.sem, 16)
                    if p:
                        sp.wait_ge(qk_parts_out.sem, qk_parts_out.at(p, 16 * 8))
                        hold(sp, "sp")
                        for quad in range(2):
                            if b:
                                last_step = LAST_STEP[NH * quad + NH - 1]
                                sp.wait_ge(weights_ps.sem, weights_ps.at(b, QUAD * (last_step + 1)))
                                hold(sp, "sp")
                            heads = slice(quad * QUAD, (quad + 1) * QUAD)
                            for shift in range(3):
                                rows = slice(3 * DH * shift, 3 * DH * (shift + 1))
                                for stack, src in ((q_stack, q_parts_dram[0:3, :, :]),
                                                   (k_stack, k_parts_dram[shift:shift + 3, :, :])):
                                    sp.dma_start(stack[rows, heads, :],
                                                 src.rearrange("a (d h) t -> (a d) h t", h=H)[:, heads, :])\
                                      .then_inc(stacks_in[quad].sem, 16)
                    if f:
                        sp.wait_ge(x_out_copied.sem, x_out_copied.at(f, NH))
                        hold(sp, "sp")
                        sp.dma_start(outr[f.number, :, :], x_out).then_inc(out_stored.sem, 16)
                pipeline(sp, program)
                sp.wait_ge(out_stored.sem, out_stored.at(Batch(None, B), 0))

            @block.gpsimd
            def _(pool):
                pool.sem_inc(out_stored.sem, out_stored.base)

                def inverse_root(n, batch):
                    pool.wait_ge(ln_var[n].sem, ln_var[n].at(batch, 1))
                    pool.tensor_tensor(ln_s[:, n, 4, :], ln_s[:, n, 3, :], minus_half[:, :], ALU.pow)\
                        .then_inc(ln_rstd[n].sem, 1)

                def program(_, c, p, b, f):
                    def gate_y():
                        pool.wait_ge(skipped.sem, skipped.at(p, 1))
                        pool.tensor_tensor(y, y_skip, z_gate[:, :], ALU.mult).then_inc(y_ready.sem, 1)

                    def group_inverse_root():
                        pool.wait_ge(gn_chain.sem, gn_chain.at(p, 7))
                        pool.tensor_tensor(gn_v[:, 1:2], gn_v[:, 0:1], minus_half[0:C, 0:1], ALU.pow)\
                            .then_inc(gn_rstd.sem, 1)

                    def add_residual():
                        pool.wait_ge(gn_gated.sem, gn_gated.at(p, 1))
                        pool.wait_ge(residual_in.sem, residual_in.at(p, 16))
                        pool.tensor_tensor(x1, x1, residual[:, :], ALU.add).then_inc(x1_ready.sem, 1)

                    def add_softplus():
                        pool.wait_ge(softplus_steps.sem, softplus_steps.at(c, 3))
                        pool.wait_ge(relued.sem, relued.at(c, 1))
                        pool.tensor_tensor(dt, relu, softplus_a, ALU.add).then_inc(dt_ready.sem, 1)

                    def make_u():
                        pool.wait_ge(dt_ready.sem, dt_ready.at(c, 1))
                        pool.tensor_tensor(u, dt, xc[:, :], ALU.mult).then_inc(u_ready.sem, 1)

                    def less_high(n):
                        pool.wait_ge(high_parts.sem, high_parts.at(c, n + 1))
                        pool.tensor_tensor(rest[:, n, :], (dt, u)[n], part[3 * n], ALU.subtract)\
                            .then_inc(rests.sem, 1)

                    def less_mid(n):
                        pool.wait_ge(mid_parts.sem, mid_parts.at(c, n + 1))
                        pool.tensor_tensor(part[3 * n + 2], rest[:, n, :], part[3 * n + 1], ALU.subtract)\
                            .then_inc(low_parts.sem, 1)

                    def normalise_first():
                        inverse_root(0, p)
                        pool.wait_ge(ln_rstd[0].sem, ln_rstd[0].at(p, 1))
                        scale(pool, 0, p)

                    def qk_less_mid():
                        pool.wait_ge(qk_mid.sem, qk_mid.at(p, 1))
                        pool.tensor_tensor(qk_part[2], rest_qk, qk_part[1], ALU.subtract).then_inc(qk_low.sem, 1)

                    for batch, work in ((p, gate_y), (p, group_inverse_root), (c, add_softplus), (c, make_u),
                                        (p, add_residual), (c, lambda: less_high(0)), (p, normalise_first),
                                        (c, lambda: less_high(1)), (c, lambda: less_mid(0)),
                                        (c, lambda: less_mid(1)), (p, qk_less_mid)):
                        if batch:
                            work()
                    if c:
                        pool.wait_ge(c_copied.sem, c_copied.at(c, 1))
                        if p:
                            pool.wait_ge(qk_parts_out.sem, qk_parts_out.at(p, 16 * 8))
                    for k in range(NJ):
                        if c:
                            pool.wait_ge(scanned.sem, scanned.at(c, k + 1))
                            if k >= 2 * NG:
                                pool.wait_ge(folded.sem, folded.at(c, NH * (k // NG - 1)))
                            pool.tensor_tensor(read[:, k % (2 * NG), :], state[:, k % 2, :], c_rep[:, :], ALU.mult)\
                                .then_inc(read_out.sem, 1)
                        if f and k == 1:
                            inverse_root(1, f)
                pipeline(pool, program)

            @block.scalar
            def _(act):
                def program(_, c, p, b, f):
                    def silu_argument():
                        act.wait_ge(conv_ps.sem, conv_ps.at(c, NH))
                        act.activation(silu_h, banks(0, 2), ACT.Identity, bias=conv_bias[:, :])\
                           .then_inc(silu_parts.sem, 1)
                        act.activation(silu_t, banks(0, 2), ACT.Tanh, bias=conv_bias[:, :])\
                           .then_inc(silu_parts.sem, 1)

                    def gate_tanh():
                        act.wait_ge(z_ps.sem, z_ps.at(c, NH))
                        act.activation(z_tanh, banks(0, 2), ACT.Tanh).then_inc(z_tanh_done.sem, 1)

                    def group_norm():
                        act.wait_ge(gn_bias.sem, gn_bias.at(p, 1))
                        act.activation(gn_h, banks(2, 2)[0:C, :], ACT.Identity, bias=gn_v[:, 4:5],
                                       scale=gn_v[:, 2:3]).then_inc(gn_parts.sem, 1)
                        act.activation(gn_t, banks(2, 2)[0:C, :], ACT.Tanh, bias=gn_v[:, 4:5],
                                       scale=gn_v[:, 2:3]).then_inc(gn_parts.sem, 1)

                    def softplus_start():
                        act.wait_ge(dt_ps.sem, dt_ps.at(c, NH))
                        act.activation(softplus_a, banks(0, 2), ACT.Abs, bias=dt_bias[:, :])\
                           .then_inc(softplus_steps.sem, 1)
                        act.activation(relu, banks(0, 2), ACT.Relu, bias=dt_bias[:, :]).then_inc(relued.sem, 1)
                        act.wait_ge(softplus_steps.sem, softplus_steps.at(c, 1))
                        act.activation(softplus_b, softplus_a, ACT.Exp, scale=-1.0).then_inc(softplus_steps.sem, 1)

                    def softplus_end():
                        act.wait_ge(softplus_steps.sem, softplus_steps.at(c, 2))
                        act.activation(softplus_a, softplus_b, ACT.Ln, bias=1.0).then_inc(softplus_steps.sem, 1)

                    def square(n, batch):
                        act.wait_ge(centred[n].sem, centred[n].at(batch, 1))
                        act.activation(xn[:, n, :, :], xcen[:, n, :, :], ACT.Square).then_inc(squared[n].sem, 1)

                    def take_t1():
                        square(0, p)
                        if not p.is_first:
                            act.wait_ge(t1_stored.sem, t1_stored.at(p, 0))
                        act.copy(t1[:, :, :], tokens_by_channels(2)).then_inc(t1_copied.sem, 1)

                    def take_xn_t():
                        act.wait_ge(xnt_ps[0].sem, xnt_ps[0].at(p, NH))
                        if b:
                            act.wait_ge(v_ps.sem, v_ps.at(b, 1))
                        act.copy(xn_t[0:C, 0, :], banks(2, 2)[0:C, :]).then_inc(xnt_copied[0].sem, 1)

                    def take_b():
                        act.wait_ge(bc_ps.sem, bc_ps.at(c, NH))
                        act.copy(b_rep[:, :], banks(0, 2)).then_inc(b_copied.sem, 1)

                    def take_c():
                        act.wait_ge(bc_ps.sem, bc_ps.at(c, 2 * NH))
                        act.copy(c_rep[:, :], banks(0, 2)).then_inc(c_copied.sem, 1)

                    def high(n):
                        ready, src = ((dt_ready, dt), (u_ready, u))[n]
                        act.wait_ge(ready.sem, ready.at(c, 1))
                        act.copy(part[3 * n], src).then_inc(high_parts.sem, 1)

                    def mid(n):
                        act.wait_ge(rests.sem, rests.at(c, n + 1))
                        act.copy(part[3 * n + 1], rest[:, n, :]).then_inc(mid_parts.sem, 1)

                    def high_qk():
                        act.wait_ge(qk_ps.sem, qk_ps.at(p, NH))
                        act.copy(qk_part[0], banks(2, 2)).then_inc(qk_high.sem, 1)

                    def mid_qk():
                        act.wait_ge(qk_rest.sem, qk_rest.at(p, 1))
                        act.copy(qk_part[1], rest_qk).then_inc(qk_mid.sem, 1)

                    for batch, work in ((c, silu_argument), (c, gate_tanh), (c, softplus_start), (p, group_norm),
                                        (c, softplus_end), (c, take_b), (c, lambda: high(0)), (c, take_c),
                                        (p, take_t1), (p, take_xn_t), (c, lambda: high(1)), (c, lambda: mid(0)),
                                        (p, high_qk), (c, lambda: mid(1)), (p, mid_qk)):
                        if batch:
                            work()

                    places = ring_places(c, b, f)

                    def bank_of(user):
                        return banks(RING[places[user] % len(RING)])

                    def decay_unit(k2):
                        k, h = k2 // 2, k2 % 2
                        act.wait_ge(dt_rep.sem, dt_rep.at(c, k2 + 1))
                        if k >= 2:
                            act.wait_ge(scanned.sem, scanned.at(c, k - 1))
                        j = chunk(k)[2]
                        act.activation(decay[:, k % 2, halves(h)], bank_of(("dt", k2)), ACT.Exp,
                                       scale=a_scale[:, j:j + 1])\
                           .then_inc(decayed.sem, 1)

                    def take_turn(turn):
                        kind, n = turn
                        from_bank = bank_of(turn)[0:C, :]
                        if kind == "attn_t":
                            act.wait_ge(attn_t_ps.sem, attn_t_ps.at(f, n + 1))
                            act.copy(attn_t[:, halves(n)], from_bank).then_inc(attn_t_copied.sem, 1)
                        elif kind == "proj":
                            square(1, f)
                        elif kind == "xn_t":
                            act.wait_ge(xnt_ps[1].sem, xnt_ps[1].at(f, n + 1))
                            act.copy(xn_t[0:C, 1, halves(n)], from_bank).then_inc(xnt_copied[1].sem, 1)
                        elif kind == "router":
                            act.wait_ge(gate_centred.sem, gate_centred.at(f, 1))
                            act.activation(gate_e[:, 1, :, :], gate_e[:, 0, :, :], ACT.Exp)\
                               .then_inc(gate_exped.sem, 1)
                        elif kind == "out_t":
                            act.wait_ge(x_out_ps.sem, x_out_ps.at(f, n + 1))
                            act.copy(x_out[:, halves(n)], from_bank).then_inc(x_out_copied.sem, 1)

                    def copy_sums(n):
                        act.wait_ge(values_added.sem, values_added.at(b, LAST_STEP[n] + 1))
                        if n >= 2:
                            act.wait_ge(heads_t_ps.sem, heads_t_ps.at(b, n - 1))
                        act.copy(acc_sb[:, n % 2, :], banks(ACC)).then_inc(acc_copied.sem, 1)

                    def softmax_step(s, heads):
                        n, quad, half, j = KEY_STEPS[s]
                        w = BANK - max(0, j * P - half * BANK)
                        for hq in heads:
                            e = QUAD * s + hq
                            act.wait_ge(weights_ps.sem, weights_ps.at(b, e + 1))
                            if hq == 0 and s >= 2:
                                act.wait_ge(values_added.sem, values_added.at(b, s - 1))
                            act.activation(probs[:, e % (2 * QUAD), 0:w], bank_of(("scores", e))[:, 0:w],
                                           ACT.Exp, scale=SCALE).then_inc(exped.sem, 1)

                    if c:
                        act.wait_ge(low_parts.sem, low_parts.at(c, 2))
                    for s, units, turns in ROUNDS:
                        if b and s is not None:
                            softmax_step(s, range(QUAD - 1))
                        if c and units:
                            decay_unit(units[0])
                        if b and s is not None:
                            softmax_step(s, (QUAD - 1,))
                            if s - 1 in LAST_STEP:
                                copy_sums(LAST_STEP.index(s - 1))
                        if c:
                            for k2 in units[1:]:
                                decay_unit(k2)
                        if f:
                            for turn in turns:
                                take_turn(turn)
                    if b:
                        copy_sums(len(GROUPS) - 1)
                pipeline(act, program)

            @block.vector
            def _(dve):
                def program(_, c, p, b, f):
                    def gate_scan():
                        dve.wait_ge(folded.sem, folded.at(p, NH * JG))
                        dve.scalar_tensor_tensor(y_skip, xc[:, :], d_skip[:, :], banks(2, 2), ALU.mult, ALU.add)\
                           .then_inc(skipped.sem, 1)

                    def take_values():
                        if not b.is_first:
                            dve.wait_ge(values_added.sem, values_added.at(b, 0))
                        dve.wait_ge(v_ps.sem, v_ps.at(b, 1))
                        dve.tensor_copy(v_aug[:, :, :, 0:DH], banks(0).rearrange("p (i h d) -> p i h d", h=H, d=DH))\
                           .then_inc(v_copied.sem, 1)

                    def channel_statistics():
                        dve.wait_ge(out_ps.sem, out_ps.at(p, NH))
                        for h in range(NH):
                            dve.bn_stats(gn_stats[:, h, :], ps[0:C, 2 + h, :]).then_inc(gn_chain.sem, 1)
                        dve.wait_ge(gn_chain.sem, gn_chain.at(p, 2))
                        hold(dve, "dve")
                        dve.bn_aggr(gn_mv[:, :], gn_stats[:, :, :]).then_inc(gn_chain.sem, 1)
                        dve.wait_ge(gn_chain.sem, gn_chain.at(p, 3))
                        dve.scalar_tensor_tensor(gn_mv[:, 1:2], gn_mv[:, 0:1], gn_mv[:, 0:1], gn_mv[:, 1:2],
                                                 ALU.mult, ALU.add).then_inc(gn_chain.sem, 1)

                    mean, mean_sq = gn_group[:, 0:1], gn_group[:, 1:2]

                    def group_variance():
                        dve.wait_ge(gn_ps.sem, gn_ps.at(p, 1))
                        dve.tensor_copy(gn_group[:, :], ps[C:2 * C, 2, 0:2]).then_inc(gn_chain.sem, 1)
                        dve.wait_ge(gn_chain.sem, gn_chain.at(p, 5))
                        dve.scalar_tensor_tensor(gn_v[:, 3:4], mean, mean, mean_sq, ALU.mult, ALU.subtract)\
                           .then_inc(gn_chain.sem, 1)
                        dve.wait_ge(gn_chain.sem, gn_chain.at(p, 6))
                        dve.tensor_scalar(gn_v[:, 0:1], gn_v[:, 3:4], -1.0, GN_EPS, ALU.mult, ALU.add)\
                           .then_inc(gn_chain.sem, 1)

                    def group_scale():
                        dve.wait_ge(gn_rstd.sem, gn_rstd.at(p, 1))
                        dve.tensor_tensor(gn_v[:, 2:3], gn_v[:, 1:2], gn_gamma_half[:, :], ALU.mult)\
                           .then_inc(gn_chain.sem, 1)
                        dve.wait_ge(gn_chain.sem, gn_chain.at(p, 8))
                        dve.scalar_tensor_tensor(gn_v[:, 3:4], mean, gn_v[:, 2:3], gn_beta_half[:, :],
                                                 ALU.mult, ALU.subtract).then_inc(gn_chain.sem, 1)
                        dve.wait_ge(gn_chain.sem, gn_chain.at(p, 9))
                        dve.tensor_scalar(gn_v[:, 4:5], gn_v[:, 3:4], -1.0, None, ALU.mult)\
                           .then_inc(gn_bias.sem, 1)

                    def gate_group_norm():
                        dve.wait_ge(gn_parts.sem, gn_parts.at(p, 2))
                        dve.scalar_tensor_tensor(x1, gn_t, 1.0, gn_h, ALU.add, ALU.mult).then_inc(gn_gated.sem, 1)

                    def convolved():
                        dve.wait_ge(silu_parts.sem, silu_parts.at(c, 2))
                        if p:
                            dve.wait_ge(skipped.sem, skipped.at(p, 1))
                        dve.scalar_tensor_tensor(xc[:, :], silu_t, 1.0, silu_h, ALU.add, ALU.mult)\
                           .then_inc(xc_ready.sem, 1)

                    def centre(n, batch, src):
                        dve.tensor_reduce(ln_s[:, n, 0, :], src, AX.X, ALU.add).then_inc(ln_chain[n].sem, 1)
                        dve.wait_ge(ln_chain[n].sem, ln_chain[n].at(batch, 1))
                        dve.tensor_scalar(ln_s[:, n, 1, :], ln_s[:, n, 0, :], 1.0 / C, None, ALU.mult)\
                           .then_inc(ln_chain[n].sem, 1)
                        dve.wait_ge(ln_chain[n].sem, ln_chain[n].at(batch, 2))
                        dve.tensor_tensor(xcen[:, n, :, :], src,
                                          ln_s[:, n, 1, :].unsqueeze(2).to_broadcast([P, TB, C]), ALU.subtract)\
                           .then_inc(centred[n].sem, 1)

                    def variance(n, batch):
                        dve.wait_ge(squared[n].sem, squared[n].at(batch, 1))
                        dve.tensor_reduce(ln_s[:, n, 2, :], xn[:, n, :, :], AX.X, ALU.add)\
                           .then_inc(ln_chain[n].sem, 1)
                        dve.wait_ge(ln_chain[n].sem, ln_chain[n].at(batch, 3))
                        dve.tensor_scalar(ln_s[:, n, 3, :], ln_s[:, n, 2, :], 1.0 / C, LN_EPS, ALU.mult, ALU.add)\
                           .then_inc(ln_var[n].sem, 1)

                    def centre_first():
                        dve.wait_ge(t1_ps.sem, t1_ps.at(p, 1))
                        centre(0, p, tokens_by_channels(2))

                    def qk_less_high():
                        dve.wait_ge(qk_high.sem, qk_high.at(p, 1))
                        dve.tensor_tensor(rest_qk, banks(2, 2), qk_part[0], ALU.subtract).then_inc(qk_rest.sem, 1)

                    def gated():
                        dve.wait_ge(z_tanh_done.sem, z_tanh_done.at(c, 1))
                        if p:
                            dve.wait_ge(y_ready.sem, y_ready.at(p, 1))
                        dve.scalar_tensor_tensor(z_gate[:, :], z_tanh, 1.0, banks(0, 2), ALU.add, ALU.mult)\
                           .then_inc(z_ready.sem, 1)

                    def row_maxima(s):
                        i, h0, nh = SCORE_STEPS[s]
                        dve.wait_ge(scores_ps.sem, scores_ps.at(b, s + 1))
                        scores = banks(4 + 2 * (s % 2), 2).rearrange("p (h k) -> p h k", h=nh)
                        dve.tensor_reduce(row_max[:, i, h0:h0 + nh], scores[:, :, 0:P * (i + 1)], AX.X, ALU.max,
                                          negate=True).then_inc(row_maxed.sem, 1)

                    beside = (
                        (0, b, take_values), (0, p, gate_scan), (3, c, convolved), (8, c, gated),
                        (8, p, channel_statistics), (11, p, group_variance), (14, p, group_scale),
                        (20, p, gate_group_norm), (26, p, centre_first), (27, p, lambda: variance(0, p)),
                        (39, p, qk_less_high))
                    for s in range(NSCORE):
                        for at, batch, work in beside:
                            if at == s and batch:
                                work()
                        if b:
                            row_maxima(s)
                    if b:
                        dve.wait_ge(row_maxed.sem, row_maxed.at(b, NSCORE))
                        dve.tensor_copy(max_parts[:, :, 0, :], row_max[:, :, :]).then_inc(max_chain.sem, 1)
                        dve.wait_ge(max_chain.sem, max_chain.at(b, 1))
                        dve.tensor_tensor(max_rest[:, :, :], row_max[:, :, :], max_parts[:, :, 0, :], ALU.subtract)\
                           .then_inc(max_chain.sem, 1)
                        dve.wait_ge(max_chain.sem, max_chain.at(b, 2))
                        dve.tensor_copy(max_parts[:, :, 1, :], max_rest[:, :, :]).then_inc(max_chain.sem, 1)
                        dve.wait_ge(max_chain.sem, max_chain.at(b, 3))
                        dve.tensor_tensor(max_parts[:, :, 2, :], max_rest[:, :, :], max_parts[:, :, 1, :],
                                          ALU.subtract).then_inc(max_parts_ready.sem, 1)

                    places = ring_places(c, b, f)

                    def bank_of(user):
                        return banks(RING[places[user] % len(RING)])

                    def take_max_t():
                        dve.wait_ge(max_t_ps.sem, max_t_ps.at(b, 1))
                        dve.tensor_copy(max_t[:, :], banks(ACC).bitcast(BF16)[0:3 * H, :])\
                           .then_inc(max_t_copied.sem, 1)

                    def scan(k):
                        dve.wait_ge(decayed.sem, decayed.at(c, 2 * k + 2))
                        dve.wait_ge(driven.sem, driven.at(c, 2 * k + 2))
                        if k >= 2:
                            dve.wait_ge(read_out.sem, read_out.at(c, k - 1))
                        dve.tensor_tensor_scan(state[:, k % 2, :], decay[:, k % 2, :], drive[:, k % 3, :], 0.0,
                                               ALU.mult, ALU.add).then_inc(scanned.sem, 1)

                    def drive_unit(k2):
                        k, h = k2 // 2, k2 % 2
                        dve.wait_ge(u_rep.sem, u_rep.at(c, k2 + 1))
                        if k >= 3:
                            dve.wait_ge(scanned.sem, scanned.at(c, k - 2))
                        dve.tensor_tensor(drive[:, k % 3, halves(h)], bank_of(("u", k2)), b_rep[:, halves(h)],
                                          ALU.mult)\
                           .then_inc(driven.sem, 1)
                        if h == 0 and k > 0:
                            scan(k - 1)

                    def divide_heads(n):
                        quad, half = GROUPS[n]
                        dve.wait_ge(heads_t_ps.sem, heads_t_ps.at(b, n + 1))
                        if f and n == 0:
                            dve.wait_ge(attn_t_ps.sem, attn_t_ps.at(f, NH))
                        heads = bank_of(("heads", n)).rearrange("p (i h d) -> p i h d", i=QB, d=GW)
                        blocks, hs = slice(half * QB, (half + 1) * QB), slice(quad * QUAD, (quad + 1) * QUAD)
                        dve.reciprocal(den[:, blocks, hs], heads[:, :, :, DH]).then_inc(den_ready.sem, 1)
                        dve.wait_ge(den_ready.sem, den_ready.at(b, n + 1))
                        out_heads = attn[:, blocks, :].rearrange("p i (h d) -> p i h d", d=DH)[:, :, hs, :]
                        dve.tensor_tensor(out_heads, heads[:, :, :, 0:DH],
                                          den[:, blocks, hs].unsqueeze(3).to_broadcast([P, QB, QUAD, DH]),
                                          ALU.mult).then_inc(attn_ready.sem, 1)

                    (shifted, ex, is_1, count_1, first, left, is_2, count_2, both, gate) = (
                        gate_e[:, k, :, :] for k in range(10))
                    top, top_1, top_2, inverse = (gate_m[:, k, :] for k in range(4))
                    step = [0]

                    def then(ins):
                        step[0] += 1
                        ins.then_inc(gate_chain.sem, 1)
                        dve.wait_ge(gate_chain.sem, gate_chain.at(f, step[0]))

                    def flat(t):
                        return t.rearrange("p i e -> p (i e)")

                    def per_expert(t):
                        return t.unsqueeze(2).to_broadcast([P, TB, E])

                    def gates():
                        dve.wait_ge(gate_exped.sem, gate_exped.at(f, 1))
                        then(dve.tensor_reduce(top_1, ex, AX.X, ALU.max))
                        then(dve.tensor_tensor(is_1, ex, per_expert(top_1), ALU.is_ge))
                        then(dve.tensor_tensor_scan(flat(count_1), flat(expert_start[:, :, :]), flat(is_1), 0.0,
                                                    ALU.mult, ALU.add))
                        then(dve.scalar_tensor_tensor(first, count_1, 1.0, is_1, ALU.is_equal, ALU.mult))
                        then(dve.scalar_tensor_tensor(left, first, -2.0, ex, ALU.mult, ALU.add))
                        then(dve.tensor_reduce(top_2, left, AX.X, ALU.max))
                        then(dve.tensor_tensor(is_2, left, per_expert(top_2), ALU.is_ge))
                        then(dve.tensor_tensor_scan(flat(count_2), flat(expert_start[:, :, :]), flat(is_2), 0.0,
                                                    ALU.mult, ALU.add))
                        then(dve.scalar_tensor_tensor(both, count_2, 1.0, is_2, ALU.is_equal, ALU.mult))
                        then(dve.tensor_tensor(both, both, first, ALU.add))
                        then(dve.tensor_tensor(top, top_1, top_2, ALU.add))
                        then(dve.reciprocal(inverse, top))
                        then(dve.tensor_tensor(both, both, ex, ALU.mult))
                        then(dve.tensor_tensor(gate, both, per_expert(inverse), ALU.mult))

                    def take_turn(turn):
                        kind, n = turn
                        if kind == "proj":
                            dve.wait_ge(proj_ps.sem, proj_ps.at(f, 1))
                            dve.wait_ge(t1_back_in.sem, t1_back_in.at(f, 16))
                            attended = bank_of(turn).rearrange("p (i c) -> p i c", c=C)
                            dve.tensor_tensor(t2[:, :, :], t1_back[:, :, :], attended, ALU.add)\
                               .then_inc(t2_ready.sem, 1)
                            dve.wait_ge(t2_ready.sem, t2_ready.at(f, 1))
                            centre(1, f, t2[:, :, :])
                        elif kind == "router":
                            dve.wait_ge(router_ps.sem, router_ps.at(f, 1))
                            logits = bank_of(turn)[:, 0:TB * E].rearrange("p (i e) -> p i e", e=E)
                            then(dve.tensor_reduce(top, logits, AX.X, ALU.max))
                            dve.tensor_tensor(shifted, logits, per_expert(top), ALU.subtract)\
                               .then_inc(gate_centred.sem, 1)
                        elif kind == "expert":
                            dve.wait_ge(expert_ps.sem, expert_ps.at(f, n + 1))
                            if n >= 2:
                                dve.wait_ge(combined.sem, combined.at(f, n - 1))
                            else:
                                dve.wait_ge(out_stored.sem, out_stored.at(f, 0))
                            dve.tensor_tensor(moe[:, n % 2, :, :], bank_of(turn).rearrange("p (e c) -> p e c", c=C),
                                              gate[:, n, :].unsqueeze(2).to_broadcast([P, E, C]), ALU.mult)\
                               .then_inc(weighted.sem, 1)
                            dve.wait_ge(weighted.sem, weighted.at(f, n + 1))
                            dve.tensor_reduce(moe_out[:, n, :], moe[:, n % 2, :, :].rearrange("p e c -> p c e"),
                                              AX.X, ALU.add).then_inc(combined.sem, 1)
                            if n == TB - 1:
                                dve.wait_ge(combined.sem, combined.at(f, TB))
                                dve.tensor_tensor(moe_out[:, :, :], moe_out[:, :, :], t2[:, :, :], ALU.add)\
                                   .then_inc(x2_ready.sem, 1)

                    def scale_second():
                        dve.wait_ge(ln_rstd[1].sem, ln_rstd[1].at(f, 1))
                        scale(dve, 1, f)

                    between = ((VARIANCE_AT, lambda: variance(1, f)), (SCALE_AT, scale_second), (GATES_AT, gates))
                    if c:
                        dve.wait_ge(b_copied.sem, b_copied.at(c, 1))
                    for n, (s, units, turns) in enumerate(ROUNDS):
                        if c:
                            for k2 in units:
                                drive_unit(k2)
                        if b and n == 0:
                            take_max_t()
                        if f:
                            for turn in turns:
                                take_turn(turn)
                            for at, work in between:
                                if at == n:
                                    work()
                        if b and s is not None and s - LAG in LAST_STEP:
                            divide_heads(LAST_STEP.index(s - LAG))
                    if c:
                        scan(NJ - 1)
                    if b:
                        divide_heads(len(GROUPS) - 1)
                pipeline(dve, program)

            @block.tensor
            def _(pe):
                def program(_, c, p, b, f):
                    def project(weights, src, bank, h, rows=P):
                        return pe.matmul(ps[0:rows, bank + h, :], weights, src[:, halves(h)], start=True, stop=True)

                    def to_channels(src, blocks, dst):
                        for n, i in enumerate(blocks):
                            last = pe.transpose(dst[0:C, tokens(n)], src[:, i, :], ident[:, :])
                        return last

                    def by_tokens(src, weights, dst, width):
                        for i in range(TB):
                            last = pe.matmul(dst[:, i * width:(i + 1) * width], src[:, tokens(i)], weights,
                                             start=True, stop=True)
                        return last

                    def fold_round(batch, q, h):
                        pe.wait_ge(read_out.sem, read_out.at(batch, NG * (q + 1)))
                        for g in range(NG):
                            k = NG * q + g
                            last = pe.matmul(ps[GW * g:GW * (g + 1), 2 + h, :], fold[:, q, :],
                                             read[:, k % (2 * NG), halves(h)], start=(q == 0), stop=(q == JG - 1))
                        last.then_inc(folded.sem, 1)

                    def last_folds(n):
                        fold_round(p, JG - 2 + n // NH, n % NH)

                    def value_projection(_):
                        by_tokens(xn_t[:, 0, :], w_v[:, :], banks(0), C).then_inc(v_ps.sem, 1)

                    def out_projection(h):
                        pe.wait_ge(y_ready.sem, y_ready.at(p, 1))
                        project(w_out[:, :], y, 2, h, C).then_inc(out_ps.sem, 1)

                    def group_mean_product(_):
                        pe.wait_ge(gn_chain.sem, gn_chain.at(p, 4))
                        hold(pe, "pe")
                        pe.matmul(ps[C:2 * C, 2, 0:2], group_mean[:, :, :].rearrange("p g c -> p (g c)"), gn_mv[:, :],
                                  start=True, stop=True).then_inc(gn_ps.sem, 1)

                    def x1_to_tokens(_):
                        pe.wait_ge(x1_ready.sem, x1_ready.at(p, 1))
                        hold(pe, "pe")
                        for i in range(TB):
                            last = pe.transpose(banks(2)[:, i * C:(i + 1) * C], x1[:, tokens(i)], ident[0:C, 0:C])
                        last.then_inc(t1_ps.sem, 1)

                    def xn_to_channels(h):
                        pe.wait_ge(t1_copied.sem, t1_copied.at(p, 1))
                        pe.wait_ge(xn_ready[0].sem, xn_ready[0].at(p, 1))
                        hold(pe, "pe")
                        to_channels(xn[:, 0, :, :], range(h * QB, (h + 1) * QB), banks(2 + h))\
                            .then_inc(xnt_ps[0].sem, 1)

                    def qk_projection(h):
                        pe.wait_ge(xnt_copied[0].sem, xnt_copied[0].at(p, 1))
                        project(w_qk[:, :], xn_t[:, 0, :], 2, h).then_inc(qk_ps.sem, 1)

                    def convolution(h):
                        pe.wait_ge(x_in.sem, x_in.at(c, 32))
                        if b:
                            pe.wait_ge(v_copied.sem, v_copied.at(b, 1))
                        project(w_conv[:, :], xs, 0, h).then_inc(conv_ps.sem, 1)

                    def gate_projection(h):
                        pe.wait_ge(silu_parts.sem, silu_parts.at(c, 2))
                        project(w_z[:, :], xs, 0, h).then_inc(z_ps.sem, 1)

                    def dt_before_bias(h):
                        pe.wait_ge(xc_ready.sem, xc_ready.at(c, 1))
                        pe.wait_ge(z_ready.sem, z_ready.at(c, 1))
                        project(w_dt_full[:, :], xc, 0, h).then_inc(dt_ps.sem, 1)

                    def b_product(h):
                        pe.wait_ge(relued.sem, relued.at(c, 1))
                        project(w_bc[:, 0, :, :].rearrange("p n e -> p (n e)"), xc, 0, h).then_inc(bc_ps.sem, 1)

                    def c_product(h):
                        pe.wait_ge(b_copied.sem, b_copied.at(c, 1))
                        project(w_bc[:, 1, :, :].rearrange("p n e -> p (n e)"), xc, 0, h).then_inc(bc_ps.sem, 1)

                    def score_step(s):
                        i, h0, nh = SCORE_STEPS[s]
                        if s >= 2:
                            pe.wait_ge(row_maxed.sem, row_maxed.at(b, s - 1))
                        for hh in range(nh):
                            for h in range(i // QB + 1):
                                bank = 4 + 2 * (s % 2) + hh + h
                                diagonal = h == i // QB
                                w = P * (i % QB + 1) if diagonal else BANK
                                last = pe.matmul(ps[:, bank, 0:w], q_stack[0:9 * DH, h0 + hh, tokens(i)],
                                                 k_stack[0:9 * DH, h0 + hh, h * BANK:h * BANK + w],
                                                 start=True, stop=not diagonal)
                                if diagonal:
                                    last = pe.matmul(ps[:, bank, w - P:w], ident_bf[:, :], mask_q[:, :],
                                                     start=False, stop=True)
                        last.then_inc(scores_ps.sem, 1)

                    beside = (
                        ((0, 0, 1, 2), p, last_folds), ((1,), b, value_projection), ((2, 2), c, convolution),
                        ((3, 5), c, gate_projection), ((6, 7), p, out_projection), ((10, 10), c, dt_before_bias),
                        ((11,), p, group_mean_product), ((16, 18), c, b_product), ((20, 21), c, c_product),
                        ((24,), p, x1_to_tokens), ((32, 33), p, xn_to_channels), ((35, 36), p, qk_projection))
                    for s in range(NSCORE):
                        for steps, batch, work in beside:
                            for n, at in enumerate(steps):
                                if at == s and batch:
                                    work(n)
                        if b:
                            if s % (NSCORE // 2) == 0:
                                quad = s // (NSCORE // 2)
                                pe.wait_ge(stacks_in[quad].sem, stacks_in[quad].at(b, 16 * 6))
                                if s == 0 and not b.is_first:
                                    pe.wait_ge(acc_copied.sem, acc_copied.at(b, 0))
                            score_step(s)
                    def turn_maxima():
                        pe.wait_ge(max_parts_ready.sem, max_parts_ready.at(b, 1))
                        for i in range(TB):
                            last = pe.transpose(banks(ACC).bitcast(BF16)[0:3 * H, tokens(i)],
                                                max_parts[:, i, :, :].rearrange("p r h -> p (r h)"), ident_bf[:, :])
                        last.then_inc(max_t_ps.sem, 1)

                    def replicate(k2, bank, rows):
                        g, q, _ = chunk(k2 // 2)
                        return pe.matmul(bank, pick[:, q, :, :].rearrange("p n e -> p (n e)"),
                                         rows[:, g, halves(k2 % 2)], start=True, stop=True)

                    places = ring_places(c, b, f)
                    users = list(places)

                    def free_bank(user):
                        place = places[user]
                        bank = RING[place % len(RING)]
                        if place >= len(RING):
                            read_by, batch, count = bank_read(users[place - len(RING)], c, b, f)
                            pe.wait_ge(read_by.sem, read_by.at(batch, count))
                        elif b and bank > ACC:
                            pe.wait_ge(row_maxed.sem, row_maxed.at(b, NSCORE))
                        return banks(bank)

                    def unit(k2):
                        if k2 == 0:
                            pe.wait_ge(dt_rows_in.sem, dt_rows_in.at(c, 16 * 3 * NG))
                            pe.wait_ge(c_copied.sem, c_copied.at(c, 1))
                        replicate(k2, free_bank(("dt", k2)), dt_rows).then_inc(dt_rep.sem, 1)
                        if k2 == 0:
                            pe.wait_ge(u_rows_in.sem, u_rows_in.at(c, 16 * 3 * NG))
                        replicate(k2, free_bank(("u", k2)), u_rows).then_inc(u_rep.sem, 1)

                    def take_turn(turn):
                        kind, n = turn
                        half_blocks = range(n * QB, (n + 1) * QB)
                        bank = free_bank(turn)
                        if turn == users[0]:
                            if b:
                                pe.wait_ge(v_copied.sem, v_copied.at(b, 1))
                            else:
                                pe.wait_ge(x_out_copied.sem, x_out_copied.at(f, 0))
                        if kind == "attn_t":
                            pe.wait_ge(attn_ready.sem, attn_ready.at(f, len(GROUPS)))
                            hold(pe, "pe")
                            to_channels(attn, half_blocks, bank).then_inc(attn_t_ps.sem, 1)
                        elif kind == "proj":
                            pe.wait_ge(attn_t_copied.sem, attn_t_copied.at(f, NH))
                            by_tokens(attn_t, w_o[:, :], bank, C).then_inc(proj_ps.sem, 1)
                        elif kind == "xn_t":
                            pe.wait_ge(xn_ready[1].sem, xn_ready[1].at(f, 1))
                            hold(pe, "pe")
                            to_channels(xn[:, 1, :, :], half_blocks, bank).then_inc(xnt_ps[1].sem, 1)
                        elif kind == "router":
                            pe.wait_ge(xnt_copied[1].sem, xnt_copied[1].at(f, NH))
                            by_tokens(xn_t[:, 1, :], w_router[:, :], bank, E).then_inc(router_ps.sem, 1)
                        elif kind == "expert":
                            pe.matmul(bank, xn_t[:, 1, tokens(n)],
                                      w_expert[:, :, :].rearrange("p e c -> p (e c)"), start=True, stop=True)\
                              .then_inc(expert_ps.sem, 1)
                        else:
                            pe.wait_ge(x2_ready.sem, x2_ready.at(f, 1))
                            hold(pe, "pe")
                            to_channels(moe_out, half_blocks, bank).then_inc(x_out_ps.sem, 1)

                    def weigh(s, heads):
                        n, quad, half, j = KEY_STEPS[s]
                        lo = max(half * BANK, j * P)
                        w = (half + 1) * BANK - lo
                        diagonal = lo == j * P
                        for hq in heads:
                            head, bank = quad * QUAD + hq, free_bank(("scores", QUAD * s + hq))
                            last = pe.matmul(bank[:, 0:w], k_stack[0:KQ, head, tokens(j)],
                                             q_stack[0:KQ, head, lo:lo + w], start=True, stop=not diagonal)
                            if diagonal:
                                last = pe.matmul(bank[:, 0:P], ident_bf[:, :], mask_k[:, :],
                                                 start=False, stop=True)
                            last.then_inc(weights_ps.sem, 1)

                    def add_values(s):
                        n, quad, half, j = KEY_STEPS[s]
                        lo = max(0, j * P - half * BANK)
                        pe.wait_ge(exped.sem, exped.at(b, QUAD * (s + 1)))
                        if n > 0 and j == 0:
                            pe.wait_ge(acc_copied.sem, acc_copied.at(b, n))
                        for hq in range(QUAD):
                            last = pe.matmul(ps[GW * hq:GW * (hq + 1), ACC, lo:BANK],
                                             v_aug[:, j, quad * QUAD + hq, :],
                                             probs[:, (QUAD * s + hq) % (2 * QUAD), 0:BANK - lo],
                                             start=(j == 0), stop=(j == QB * (half + 1) - 1))
                        last.then_inc(values_added.sem, 1)

                    def heads_to_tokens(n):
                        pe.wait_ge(acc_copied.sem, acc_copied.at(b, n + 1))
                        bank = free_bank(("heads", n))
                        for i in range(QB):
                            last = pe.transpose(bank[:, tokens(i)], acc_sb[:, n % 2, tokens(i)],
                                                ident[:, :])
                        last.then_inc(heads_t_ps.sem, 1)

                    for n, (s, units, turns) in enumerate(ROUNDS):
                        at_step = b and s is not None
                        if at_step:
                            if s == 0:
                                pe.wait_ge(v_copied.sem, v_copied.at(b, 1))
                                pe.wait_ge(max_in.sem, max_in.at(b, 16))
                            weigh(s, range(QUAD - 1))
                        if c and units:
                            unit(units[0])
                        if b and n == 0:
                            turn_maxima()
                        if at_step:
                            if s > 0:
                                add_values(s - 1)
                            weigh(s, (QUAD - 1,))
                            if s - LAG in LAST_STEP:
                                heads_to_tokens(LAST_STEP.index(s - LAG))
                        if c:
                            for q, h, at in FOLDS:
                                if at == n:
                                    if q == 0 and h == 0 and p:
                                        pe.wait_ge(qk_rest.sem, qk_rest.at(p, 1))
                                    fold_round(c, q, h)
                            for k2 in units[1:]:
                                unit(k2)
                        if f:
                            for turn in turns:
                                take_turn(turn)
                    if b:
                        add_values(NKEY - 1)
                        heads_to_tokens(len(GROUPS) - 1)
                    last_read = {}
                    for user in users[-len(RING):]:
                        read_by, batch, count = bank_read(user, c, b, f)
                        last_read[read_by] = (batch, count)
                    for read_by, (batch, count) in last_read.items():
                        pe.wait_ge(read_by.sem, read_by.at(batch, count))
                pipeline(pe, program)


_INS = ["x", "L0_conv_W_in", "L0_conv_conv_w", "L0_conv_conv_b", "L0_conv_W_x", "L0_conv_W_dt", "L0_conv_b_dt",
        "L0_conv_A_log", "L0_conv_D", "L0_conv_W_out", "L0_conv_gn_gamma", "L0_conv_gn_beta", "L1_attn_w_attn",
        "L1_attn_w_proj", "L1_ffn_router_w", "L1_ffn_router_b", "L1_ffn_expert_w", "L1_ffn_expert_b"]


def kernel(**inputs):
    import numpy as np
    import concourse.bacc as bacc
    from concourse.bass_utils import run_bass_kernel_spmd

    nc = bacc.Bacc("TRN2", target_bir_lowering=False, num_devices=1)
    arrays, args = {}, []
    for name in _INS:
        a = np.ascontiguousarray(inputs[name])
        arrays[f"in_{name}"] = a
        args.append(nc.dram_tensor(f"in_{name}", a.shape, mybir.dt.from_np(a.dtype), kind="ExternalInput").ap())
    out = nc.dram_tensor("out", inputs["x"].shape, F32, kind="ExternalOutput").ap()
    mamba_attention_moe(nc, *args, out)
    r = run_bass_kernel_spmd(nc, [arrays], core_ids=[0])
    return r.results[0]["out"]
```
